# Optimizing a Trainium2 kernel written in Bass

```python
import numpy as np
import jax
import jax.numpy as jnp

def _softmax(x, axis=-1):
    return jax.nn.softmax(x, axis=axis)

def _gelu(x):
    return jax.nn.gelu(x, approximate=True)

def _silu(x):
    return jax.nn.silu(x)

def _sigmoid(x):
    return jax.nn.sigmoid(x)

def _layernorm(x, axis=-1, eps=1e-05):
    m = jnp.mean(x, axis=axis, keepdims=True)
    v = jnp.var(x, axis=axis, keepdims=True)
    return (x - m) / jnp.sqrt(v + eps)

def _scatter_add(tgt, idx, src, axis=0):
    return tgt.at[idx].add(src)

def _segment_sum(src, seg, n):
    return jax.ops.segment_sum(src, seg, n)
kernel_name = 'mk_pixart_seq_d4_seqx_r8_aa2c5a'

def setup_inputs(seed: int=0):
    np.random.seed(seed)
    _w = jnp.asarray

    def _rec_inputs():
        import jax
        import jax.numpy as jnp
        _rk = jax.random.key(seed)
        x = 7.22e-05 + 1 * jax.random.normal(jax.random.fold_in(_rk, 1), (4, 512, 128), jnp.float32)
        _lenS = 512 - jax.random.randint(jax.random.fold_in(_rk, 7), (4,), 0, max(1, 512 // 4) + 1, jnp.int32)
        _lenS2 = 77 - jax.random.randint(jax.random.fold_in(_rk, 8), (4,), 0, max(1, 77 // 4) + 1, jnp.int32)
        cond_1024 = 0.000887014 + 1.03683 * jax.random.normal(jax.random.fold_in(_rk, 11), (4, 128), jnp.float32)
        _ctx_1024P = jax.random.normal(jax.random.fold_in(_rk, 12), (4, 16, 128), jnp.float32)
        _ctx_1024c = jax.random.dirichlet(jax.random.fold_in(_rk, 512), 0.3 * jnp.ones((16,), jnp.float32), (4, 77))
        _ctx_1024t = jnp.einsum('bsk,bkd->bsd', _ctx_1024c, _ctx_1024P)
        _ctx_1024t = _ctx_1024t * jax.lax.rsqrt(jnp.mean(jnp.square(_ctx_1024t)) + 1e-12) * 0.953939
        ctx_1024 = 0.00086875 + 0.999764 * (_ctx_1024t + 0.3 * jax.random.normal(jax.random.fold_in(_rk, 612), (4, 77, 128), jnp.float32))
        _validS = jnp.arange(512)[None, :] < _lenS[:, None]
        _validS2 = jnp.arange(77)[None, :] < _lenS2[:, None]
        _causal = jnp.tril(jnp.ones((512, 512), dtype=bool))
        mask_BxS2_bf1 = jnp.ones((4, 77), dtype=bool)
        mask_SxS_bk0 = jnp.logical_not(jnp.broadcast_to(_validS[0:1, :], (512, 512)))
        mask_BxS2_ik0 = jnp.where(jnp.broadcast_to(_validS2[:, :], (4, 77)), 0, 1).astype(jnp.int32)
        return (x, cond_1024, ctx_1024, mask_BxS2_bf1, mask_SxS_bk0, mask_BxS2_ik0)
    x, cond_1024, ctx_1024, mask_BxS2_bf1, mask_SxS_bk0, mask_BxS2_ik0 = _rec_inputs()

    def _L0_xcond_setup():
        import jax, jax.numpy as jnp
        import numpy as np
        C = 128
        H = 16
        D = C // H
        WIN = 64
        SHIFT = 32
        TOPK = 16
        HID = 512
        EPS = 1e-06

        def _ln(x):
            x32 = x.astype(jnp.float32)
            m = x32.mean(-1, keepdims=True)
            v = jnp.mean((x32 - m) ** 2, axis=-1, keepdims=True)
            return ((x32 - m) * jax.lax.rsqrt(v + EPS)).astype(x.dtype)

        def _self_attn(h, w_qkv, b_qkv, w_so, b_so):
            B, L, _ = h.shape
            qkv = h @ w_qkv + b_qkv
            qkv = jnp.roll(qkv, -SHIFT, axis=1)
            nw = L // WIN
            qkv = qkv.reshape(B, nw, WIN, 3, H, D)
            q, k, v = (qkv[:, :, :, 0], qkv[:, :, :, 1], qkv[:, :, :, 2])
            scores = jnp.einsum('bnqhd,bnkhd->bnhqk', q, k) / jnp.sqrt(jnp.float32(D)).astype(h.dtype)
            attn = jax.nn.softmax(scores, axis=-1)
            o = jnp.einsum('bnhqk,bnkhd->bnqhd', attn, v).reshape(B, L, C)
            o = jnp.roll(o, SHIFT, axis=1)
            return o @ w_so + b_so

        def _topk_cross_attn(h, ctx, w_q, b_q, w_kv, b_kv, w_co, b_co):
            B, L, _ = h.shape
            Lc = ctx.shape[1]
            q = (h @ w_q + b_q).reshape(B, L, H, D)
            kv = (ctx @ w_kv + b_kv).reshape(B, Lc, 2, H, D)
            k, v = (kv[:, :, 0], kv[:, :, 1])
            scores = jnp.einsum('bqhd,bkhd->bhqk', q, k) / jnp.sqrt(jnp.float32(D)).astype(h.dtype)
            top_s, top_i = jax.lax.top_k(scores, TOPK)
            attn = jax.nn.softmax(top_s, axis=-1)
            v_bh = jnp.transpose(v, (0, 2, 1, 3))
            vg = jnp.take_along_axis(v_bh[:, :, None, :, :], top_i[..., None], axis=3)
            o = jnp.einsum('bhqk,bhqkd->bqhd', attn, vg).reshape(B, L, C)
            return o @ w_co + b_co

        def _swiglu(h, w_m1, b_m1, w_m2, b_m2):
            u = h @ w_m1 + b_m1
            a, b = (u[..., :HID], u[..., HID:])
            return jax.nn.silu(a) * b @ w_m2 + b_m2
        key = jax.random.key(seed)
        ks = jax.random.split(key, 24)
        s = 0.02
        inp = {'x': jax.random.normal(ks[0], (2, 512, C), jnp.float32), 'mod': jax.random.normal(ks[1], (2, C), jnp.float32), 'context': jax.random.normal(ks[2], (2, 128, C), jnp.float32), 'w_ada': jax.random.normal(ks[3], (C, 9 * C), jnp.float32) * s, 'b_ada': jnp.zeros((9 * C,), jnp.float32), 'w_qkv': jax.random.normal(ks[4], (C, 3 * C), jnp.float32) * s, 'b_qkv': jnp.zeros((3 * C,), jnp.float32), 'w_so': jax.random.normal(ks[5], (C, C), jnp.float32) * s, 'b_so': jnp.zeros((C,), jnp.float32), 'w_q': jax.random.normal(ks[6], (C, C), jnp.float32) * s, 'b_q': jnp.zeros((C,), jnp.float32), 'w_kv': jax.random.normal(ks[7], (C, 2 * C), jnp.float32) * s, 'b_kv': jnp.zeros((2 * C,), jnp.float32), 'w_co': jax.random.normal(ks[8], (C, C), jnp.float32) * s, 'b_co': jnp.zeros((C,), jnp.float32), 'w_m1': jax.random.normal(ks[9], (C, 2 * HID), jnp.float32) * s, 'b_m1': jnp.zeros((2 * HID,), jnp.float32), 'w_m2': jax.random.normal(ks[10], (HID, C), jnp.float32) * s, 'b_m2': jnp.zeros((C,), jnp.float32)}
        return inp
    _L0_xcond_all = _L0_xcond_setup()
    _L0_xcond_in = {k: v for k, v in _L0_xcond_all.items() if k in ('w_ada', 'b_ada', 'w_qkv', 'b_qkv', 'w_so', 'b_so', 'w_q', 'b_q', 'w_kv', 'b_kv', 'w_co', 'b_co', 'w_m1', 'b_m1', 'w_m2', 'b_m2')}
    del _L0_xcond_all

    def _L1_xcond_setup():
        import jax, jax.numpy as jnp
        import numpy as np
        B, N, D, H, LC = (2, 128, 128, 16, 77)
        HD = D // H
        BLOCK = 16
        ROPE_BASE = 10000.0
        EPS = 1e-05

        def _block_diff_mask(n, block_size):
            idx = np.arange(2 * n)
            q = idx[:, None]
            kv = idx[None, :]
            fq = q >= n
            fkv = kv >= n
            bq = np.where(fq, (q - n) // block_size, q // block_size)
            bkv = np.where(fkv, (kv - n) // block_size, kv // block_size)
            block_diagonal = (bq == bkv) & (fq == fkv)
            offset_block_causal = (bq > bkv) & fkv & ~fq
            block_causal = (bq >= bkv) & fq & fkv
            return jnp.asarray(block_diagonal | offset_block_causal | block_causal)

        def _rope_tables(n):
            inv_freq = 1.0 / ROPE_BASE ** (np.arange(0, HD, 2, dtype=np.float32) / HD)
            freqs = np.outer(np.arange(n, dtype=np.float32), inv_freq)
            emb = np.concatenate([freqs, freqs], axis=-1)
            cos = jnp.asarray(np.cos(emb), jnp.float32)[None, :, None, :]
            sin = jnp.asarray(np.sin(emb), jnp.float32)[None, :, None, :]
            return (cos, sin)

        def _ln(x, w):
            xf = x.astype(jnp.float32)
            mu = jnp.mean(xf, axis=-1, keepdims=True)
            var = jnp.mean(jnp.square(xf - mu), axis=-1, keepdims=True)
            y = (xf - mu) * jax.lax.rsqrt(var + EPS)
            return y * w[None, None, :]

        def _apply_rope(t, cos, sin):
            t1, t2 = jnp.split(t, 2, axis=-1)
            rot = jnp.concatenate([-t2, t1], axis=-1)
            return t * cos + rot * sin

        def _attn(q, k, v, mask):
            scale = 1.0 / np.sqrt(HD)
            s = jnp.einsum('bqhd,bkhd->bhqk', q, k) * scale
            s = jnp.where(mask, s, jnp.finfo(s.dtype).min)
            a = jax.nn.softmax(s, axis=-1)
            return jnp.einsum('bhqk,bkhd->bqhd', a, v)
        key = jax.random.key(seed)
        ks = jax.random.split(key, 16)
        w = lambda k, shp: jax.random.normal(k, shp, jnp.float32) * 0.02
        inp = {'x': jax.random.normal(ks[0], (B, 2 * N, D), jnp.float32), 'cond_global': jax.random.normal(ks[1], (B, D), jnp.float32), 'cond_tokens': jax.random.normal(ks[2], (B, LC, D), jnp.float32), 'adaLN_W': w(ks[3], (D, 9 * D)), 'adaLN_b': w(ks[4], (9 * D,)), 'norm1_w': jnp.ones((D,), jnp.float32), 'qkv_W': w(ks[5], (D, 3 * D)), 'attn_out_W': w(ks[6], (D, D)), 'normc_w': jnp.ones((D,), jnp.float32), 'cq_W': w(ks[7], (D, D)), 'ck_W': w(ks[8], (D, D)), 'cv_W': w(ks[9], (D, D)), 'co_W': w(ks[10], (D, D)), 'norm2_w': jnp.ones((D,), jnp.float32), 'mlp_W1': w(ks[11], (D, 4 * D)), 'mlp_b1': w(ks[12], (4 * D,)), 'mlp_W2': w(ks[13], (4 * D, D)), 'mlp_b2': w(ks[14], (D,)), 'cond_kv_mask': jnp.ones((B, LC), bool), 'attn_mask': _block_diff_mask(N, BLOCK)}
        return inp
    _L1_xcond_all = _L1_xcond_setup()
    _L1_xcond_in = {k: v for k, v in _L1_xcond_all.items() if k in ('adaLN_W', 'adaLN_b', 'norm1_w', 'qkv_W', 'attn_out_W', 'normc_w', 'cq_W', 'ck_W', 'cv_W', 'co_W', 'norm2_w', 'mlp_W1', 'mlp_b1', 'mlp_W2', 'mlp_b2')}
    del _L1_xcond_all

    def _L2_xcond_setup():
        import jax, jax.numpy as jnp
        import numpy as np
        D = 128
        H = 16
        HD = D // H
        FF = 4 * D
        B, NQ, NK = (8, 128, 64)
        EPS = 1e-05

        def layernorm(x, g, b):
            m = jnp.mean(x, axis=-1, keepdims=True)
            v = jnp.mean(jnp.square(x - m), axis=-1, keepdims=True)
            return (x - m) * jax.lax.rsqrt(v + EPS) * g + b

        def mha(x, ctx, wq, bq, wk, bk, wv, bv, wo, bo, mask=None):
            Bq, Nq, _ = x.shape
            Nk = ctx.shape[1]
            q = (x @ wq + bq).reshape(Bq, Nq, H, HD)
            k = (ctx @ wk + bk).reshape(Bq, Nk, H, HD)
            v = (ctx @ wv + bv).reshape(Bq, Nk, H, HD)
            scores = jnp.einsum('bqhd,bkhd->bhqk', q, k) / np.sqrt(HD)
            if mask is not None:
                scores = jnp.where(mask[:, None, None, :].astype(bool), scores, -jnp.inf)
            attn = jax.nn.softmax(scores.astype(jnp.float32), axis=-1).astype(scores.dtype)
            out = jnp.einsum('bhqk,bkhd->bqhd', attn, v).reshape(Bq, Nq, D)
            return out @ wo + bo
        key = jax.random.key(seed)
        ks = jax.random.split(key, 40)
        rn = lambda k, shape, s=0.02: jax.random.normal(k, shape, jnp.float32) * s
        inp = {'x': jax.random.normal(ks[0], (B, NQ, D), jnp.float32), 't_emb': jax.random.normal(ks[1], (B, D), jnp.float32), 'context_emb': jax.random.normal(ks[2], (B, NK, D), jnp.float32), 'mask': jax.random.randint(ks[3], (B, NK), 0, 2, jnp.int32), 'ln1_g': jnp.ones((D,), jnp.float32), 'ln1_b': jnp.zeros((D,), jnp.float32), 'ln3_g': jnp.ones((D,), jnp.float32), 'ln3_b': jnp.zeros((D,), jnp.float32), 'ln2_g': jnp.ones((D,), jnp.float32), 'ln2_b': jnp.zeros((D,), jnp.float32), 'sa_wq': rn(ks[4], (D, D)), 'sa_bq': jnp.zeros((D,), jnp.float32), 'sa_wk': rn(ks[5], (D, D)), 'sa_bk': jnp.zeros((D,), jnp.float32), 'sa_wv': rn(ks[6], (D, D)), 'sa_bv': jnp.zeros((D,), jnp.float32), 'sa_wo': rn(ks[7], (D, D)), 'sa_bo': jnp.zeros((D,), jnp.float32), 'ca_wq': rn(ks[8], (D, D)), 'ca_bq': jnp.zeros((D,), jnp.float32), 'ca_wk': rn(ks[9], (D, D)), 'ca_bk': jnp.zeros((D,), jnp.float32), 'ca_wv': rn(ks[10], (D, D)), 'ca_bv': jnp.zeros((D,), jnp.float32), 'ca_wo': rn(ks[11], (D, D)), 'ca_bo': jnp.zeros((D,), jnp.float32), 'tp_w': rn(ks[12], (D, 3 * D)), 'tp_b': jnp.zeros((3 * D,), jnp.float32), 'w1': rn(ks[13], (D, FF)), 'b1': jnp.zeros((FF,), jnp.float32), 'w2': rn(ks[14], (FF, D)), 'b2': jnp.zeros((D,), jnp.float32)}
        return inp
    _L2_xcond_all = _L2_xcond_setup()
    _L2_xcond_in = {k: v for k, v in _L2_xcond_all.items() if k in ('ln1_g', 'ln1_b', 'ln3_g', 'ln3_b', 'ln2_g', 'ln2_b', 'sa_wq', 'sa_bq', 'sa_wk', 'sa_bk', 'sa_wv', 'sa_bv', 'sa_wo', 'sa_bo', 'ca_wq', 'ca_bq', 'ca_wk', 'ca_bk', 'ca_wv', 'ca_bv', 'ca_wo', 'ca_bo', 'tp_w', 'tp_b', 'w1', 'b1', 'w2', 'b2')}
    del _L2_xcond_all

    def _L3_xcond_setup():
        import jax, jax.numpy as jnp
        import numpy as np
        LN_EPS = 1e-06

        def _ln(x):
            mu = jnp.mean(x, axis=-1, keepdims=True)
            var = jnp.var(x, axis=-1, keepdims=True)
            return (x - mu) * jax.lax.rsqrt(var + LN_EPS)
        key = jax.random.key(seed)
        H, NH = (128, 16)
        B, N, S = (4, 128, 77)
        MLP = int(H * 4.0)
        ks = jax.random.split(key, 20)
        s = 1.0 / np.sqrt(H)
        return {'x': jax.random.normal(ks[0], (B, N, H), jnp.float32), 'c': jax.random.normal(ks[1], (B, H), jnp.float32), 'context': jax.random.normal(ks[2], (B, S, H), jnp.float32), 'W_mod': jax.random.normal(ks[3], (H, 6 * H), jnp.float32) * s, 'b_mod': jnp.zeros((6 * H,), jnp.float32), 'W_qkv': jax.random.normal(ks[4], (H, 3 * H), jnp.float32) * s, 'b_qkv': jnp.zeros((3 * H,), jnp.float32), 'W_proj': jax.random.normal(ks[5], (H, H), jnp.float32) * s, 'b_proj': jnp.zeros((H,), jnp.float32), 'W_qc': jax.random.normal(ks[6], (H, H), jnp.float32) * s, 'b_qc': jnp.zeros((H,), jnp.float32), 'W_kvc': jax.random.normal(ks[7], (H, 2 * H), jnp.float32) * s, 'b_kvc': jnp.zeros((2 * H,), jnp.float32), 'W_cproj': jax.random.normal(ks[8], (H, H), jnp.float32) * s, 'b_cproj': jnp.zeros((H,), jnp.float32), 'W_mlp1': jax.random.normal(ks[9], (H, MLP), jnp.float32) * s, 'b_mlp1': jnp.zeros((MLP,), jnp.float32), 'W_mlp2': jax.random.normal(ks[10], (MLP, H), jnp.float32) * (1.0 / np.sqrt(MLP)), 'b_mlp2': jnp.zeros((H,), jnp.float32)}
    _L3_xcond_all = _L3_xcond_setup()
    _L3_xcond_in = {k: v for k, v in _L3_xcond_all.items() if k in ('W_mod', 'b_mod', 'W_qkv', 'b_qkv', 'W_proj', 'b_proj', 'W_qc', 'b_qc', 'W_kvc', 'b_kvc', 'W_cproj', 'b_cproj', 'W_mlp1', 'b_mlp1', 'W_mlp2', 'b_mlp2')}
    del _L3_xcond_all
    return {'x': x, 'cond_1024': cond_1024, 'ctx_1024': ctx_1024, 'mask_BxS2_bf1': mask_BxS2_bf1, 'mask_SxS_bk0': mask_SxS_bk0, 'mask_BxS2_ik0': mask_BxS2_ik0, 'L0_xcond_w_ada': _L0_xcond_in['w_ada'], 'L0_xcond_b_ada': _L0_xcond_in['b_ada'], 'L0_xcond_w_qkv': _L0_xcond_in['w_qkv'], 'L0_xcond_b_qkv': _L0_xcond_in['b_qkv'], 'L0_xcond_w_so': _L0_xcond_in['w_so'], 'L0_xcond_b_so': _L0_xcond_in['b_so'], 'L0_xcond_w_q': _L0_xcond_in['w_q'], 'L0_xcond_b_q': _L0_xcond_in['b_q'], 'L0_xcond_w_kv': _L0_xcond_in['w_kv'], 'L0_xcond_b_kv': _L0_xcond_in['b_kv'], 'L0_xcond_w_co': _L0_xcond_in['w_co'], 'L0_xcond_b_co': _L0_xcond_in['b_co'], 'L0_xcond_w_m1': _L0_xcond_in['w_m1'], 'L0_xcond_b_m1': _L0_xcond_in['b_m1'], 'L0_xcond_w_m2': _L0_xcond_in['w_m2'], 'L0_xcond_b_m2': _L0_xcond_in['b_m2'], 'L1_xcond_adaLN_W': _L1_xcond_in['adaLN_W'], 'L1_xcond_adaLN_b': _L1_xcond_in['adaLN_b'], 'L1_xcond_norm1_w': _L1_xcond_in['norm1_w'], 'L1_xcond_qkv_W': _L1_xcond_in['qkv_W'], 'L1_xcond_attn_out_W': _L1_xcond_in['attn_out_W'], 'L1_xcond_normc_w': _L1_xcond_in['normc_w'], 'L1_xcond_cq_W': _L1_xcond_in['cq_W'], 'L1_xcond_ck_W': _L1_xcond_in['ck_W'], 'L1_xcond_cv_W': _L1_xcond_in['cv_W'], 'L1_xcond_co_W': _L1_xcond_in['co_W'], 'L1_xcond_norm2_w': _L1_xcond_in['norm2_w'], 'L1_xcond_mlp_W1': _L1_xcond_in['mlp_W1'], 'L1_xcond_mlp_b1': _L1_xcond_in['mlp_b1'], 'L1_xcond_mlp_W2': _L1_xcond_in['mlp_W2'], 'L1_xcond_mlp_b2': _L1_xcond_in['mlp_b2'], 'L2_xcond_ln1_g': _L2_xcond_in['ln1_g'], 'L2_xcond_ln1_b': _L2_xcond_in['ln1_b'], 'L2_xcond_ln3_g': _L2_xcond_in['ln3_g'], 'L2_xcond_ln3_b': _L2_xcond_in['ln3_b'], 'L2_xcond_ln2_g': _L2_xcond_in['ln2_g'], 'L2_xcond_ln2_b': _L2_xcond_in['ln2_b'], 'L2_xcond_sa_wq': _L2_xcond_in['sa_wq'], 'L2_xcond_sa_bq': _L2_xcond_in['sa_bq'], 'L2_xcond_sa_wk': _L2_xcond_in['sa_wk'], 'L2_xcond_sa_bk': _L2_xcond_in['sa_bk'], 'L2_xcond_sa_wv': _L2_xcond_in['sa_wv'], 'L2_xcond_sa_bv': _L2_xcond_in['sa_bv'], 'L2_xcond_sa_wo': _L2_xcond_in['sa_wo'], 'L2_xcond_sa_bo': _L2_xcond_in['sa_bo'], 'L2_xcond_ca_wq': _L2_xcond_in['ca_wq'], 'L2_xcond_ca_bq': _L2_xcond_in['ca_bq'], 'L2_xcond_ca_wk': _L2_xcond_in['ca_wk'], 'L2_xcond_ca_bk': _L2_xcond_in['ca_bk'], 'L2_xcond_ca_wv': _L2_xcond_in['ca_wv'], 'L2_xcond_ca_bv': _L2_xcond_in['ca_bv'], 'L2_xcond_ca_wo': _L2_xcond_in['ca_wo'], 'L2_xcond_ca_bo': _L2_xcond_in['ca_bo'], 'L2_xcond_tp_w': _L2_xcond_in['tp_w'], 'L2_xcond_tp_b': _L2_xcond_in['tp_b'], 'L2_xcond_w1': _L2_xcond_in['w1'], 'L2_xcond_b1': _L2_xcond_in['b1'], 'L2_xcond_w2': _L2_xcond_in['w2'], 'L2_xcond_b2': _L2_xcond_in['b2'], 'L3_xcond_W_mod': _L3_xcond_in['W_mod'], 'L3_xcond_b_mod': _L3_xcond_in['b_mod'], 'L3_xcond_W_qkv': _L3_xcond_in['W_qkv'], 'L3_xcond_b_qkv': _L3_xcond_in['b_qkv'], 'L3_xcond_W_proj': _L3_xcond_in['W_proj'], 'L3_xcond_b_proj': _L3_xcond_in['b_proj'], 'L3_xcond_W_qc': _L3_xcond_in['W_qc'], 'L3_xcond_b_qc': _L3_xcond_in['b_qc'], 'L3_xcond_W_kvc': _L3_xcond_in['W_kvc'], 'L3_xcond_b_kvc': _L3_xcond_in['b_kvc'], 'L3_xcond_W_cproj': _L3_xcond_in['W_cproj'], 'L3_xcond_b_cproj': _L3_xcond_in['b_cproj'], 'L3_xcond_W_mlp1': _L3_xcond_in['W_mlp1'], 'L3_xcond_b_mlp1': _L3_xcond_in['b_mlp1'], 'L3_xcond_W_mlp2': _L3_xcond_in['W_mlp2'], 'L3_xcond_b_mlp2': _L3_xcond_in['b_mlp2']}

def reference(x, cond_1024, ctx_1024, mask_BxS2_bf1, mask_SxS_bk0, mask_BxS2_ik0, L0_xcond_w_ada, L0_xcond_b_ada, L0_xcond_w_qkv, L0_xcond_b_qkv, L0_xcond_w_so, L0_xcond_b_so, L0_xcond_w_q, L0_xcond_b_q, L0_xcond_w_kv, L0_xcond_b_kv, L0_xcond_w_co, L0_xcond_b_co, L0_xcond_w_m1, L0_xcond_b_m1, L0_xcond_w_m2, L0_xcond_b_m2, L1_xcond_adaLN_W, L1_xcond_adaLN_b, L1_xcond_norm1_w, L1_xcond_qkv_W, L1_xcond_attn_out_W, L1_xcond_normc_w, L1_xcond_cq_W, L1_xcond_ck_W, L1_xcond_cv_W, L1_xcond_co_W, L1_xcond_norm2_w, L1_xcond_mlp_W1, L1_xcond_mlp_b1, L1_xcond_mlp_W2, L1_xcond_mlp_b2, L2_xcond_ln1_g, L2_xcond_ln1_b, L2_xcond_ln3_g, L2_xcond_ln3_b, L2_xcond_ln2_g, L2_xcond_ln2_b, L2_xcond_sa_wq, L2_xcond_sa_bq, L2_xcond_sa_wk, L2_xcond_sa_bk, L2_xcond_sa_wv, L2_xcond_sa_bv, L2_xcond_sa_wo, L2_xcond_sa_bo, L2_xcond_ca_wq, L2_xcond_ca_bq, L2_xcond_ca_wk, L2_xcond_ca_bk, L2_xcond_ca_wv, L2_xcond_ca_bv, L2_xcond_ca_wo, L2_xcond_ca_bo, L2_xcond_tp_w, L2_xcond_tp_b, L2_xcond_w1, L2_xcond_b1, L2_xcond_w2, L2_xcond_b2, L3_xcond_W_mod, L3_xcond_b_mod, L3_xcond_W_qkv, L3_xcond_b_qkv, L3_xcond_W_proj, L3_xcond_b_proj, L3_xcond_W_qc, L3_xcond_b_qc, L3_xcond_W_kvc, L3_xcond_b_kvc, L3_xcond_W_cproj, L3_xcond_b_cproj, L3_xcond_W_mlp1, L3_xcond_b_mlp1, L3_xcond_W_mlp2, L3_xcond_b_mlp2):
    import jax
    import jax.numpy as jnp

    def _L0_xcond_ref(x, mod, context, w_ada, b_ada, w_qkv, b_qkv, w_so, b_so, w_q, b_q, w_kv, b_kv, w_co, b_co, w_m1, b_m1, w_m2, b_m2):
        import jax, jax.numpy as jnp
        import numpy as np
        C = 128
        H = 16
        D = C // H
        WIN = 64
        SHIFT = 32
        TOPK = 16
        HID = 512
        EPS = 1e-06

        def _ln(x):
            x32 = x.astype(jnp.float32)
            m = x32.mean(-1, keepdims=True)
            v = jnp.mean((x32 - m) ** 2, axis=-1, keepdims=True)
            return ((x32 - m) * jax.lax.rsqrt(v + EPS)).astype(x.dtype)

        def _self_attn(h, w_qkv, b_qkv, w_so, b_so):
            B, L, _ = h.shape
            qkv = h @ w_qkv + b_qkv
            qkv = jnp.roll(qkv, -SHIFT, axis=1)
            nw = L // WIN
            qkv = qkv.reshape(B, nw, WIN, 3, H, D)
            q, k, v = (qkv[:, :, :, 0], qkv[:, :, :, 1], qkv[:, :, :, 2])
            scores = jnp.einsum('bnqhd,bnkhd->bnhqk', q, k) / jnp.sqrt(jnp.float32(D)).astype(h.dtype)
            attn = jax.nn.softmax(scores, axis=-1)
            o = jnp.einsum('bnhqk,bnkhd->bnqhd', attn, v).reshape(B, L, C)
            o = jnp.roll(o, SHIFT, axis=1)
            return o @ w_so + b_so

        def _topk_cross_attn(h, ctx, w_q, b_q, w_kv, b_kv, w_co, b_co):
            B, L, _ = h.shape
            Lc = ctx.shape[1]
            q = (h @ w_q + b_q).reshape(B, L, H, D)
            kv = (ctx @ w_kv + b_kv).reshape(B, Lc, 2, H, D)
            k, v = (kv[:, :, 0], kv[:, :, 1])
            scores = jnp.einsum('bqhd,bkhd->bhqk', q, k) / jnp.sqrt(jnp.float32(D)).astype(h.dtype)
            top_s, top_i = jax.lax.top_k(scores, TOPK)
            attn = jax.nn.softmax(top_s, axis=-1)
            v_bh = jnp.transpose(v, (0, 2, 1, 3))
            vg = jnp.take_along_axis(v_bh[:, :, None, :, :], top_i[..., None], axis=3)
            o = jnp.einsum('bhqk,bhqkd->bqhd', attn, vg).reshape(B, L, C)
            return o @ w_co + b_co

        def _swiglu(h, w_m1, b_m1, w_m2, b_m2):
            u = h @ w_m1 + b_m1
            a, b = (u[..., :HID], u[..., HID:])
            return jax.nn.silu(a) * b @ w_m2 + b_m2
        m = jax.nn.silu(mod) @ w_ada + b_ada
        sh_msa, sc_msa, g_msa, sh_mca, sc_mca, g_mca, sh_mlp, sc_mlp, g_mlp = [m[:, i * C:(i + 1) * C][:, None, :] for i in range(9)]
        h = _ln(x) * (1 + sc_msa) + sh_msa
        h = _self_attn(h, w_qkv, b_qkv, w_so, b_so)
        x = x + h * g_msa
        h = _ln(x) * (1 + sc_mca) + sh_mca
        h = _topk_cross_attn(h, context, w_q, b_q, w_kv, b_kv, w_co, b_co)
        x = x + h * g_mca
        h = _ln(x) * (1 + sc_mlp) + sh_mlp
        h = _swiglu(h, w_m1, b_m1, w_m2, b_m2)
        x = x + h * g_mlp
        return x

    def _L1_xcond_ref(x, cond_global, cond_tokens, adaLN_W, adaLN_b, norm1_w, qkv_W, attn_out_W, normc_w, cq_W, ck_W, cv_W, co_W, norm2_w, mlp_W1, mlp_b1, mlp_W2, mlp_b2, cond_kv_mask, attn_mask):
        import jax, jax.numpy as jnp
        import numpy as np
        B, N, D, H, LC = (2, 128, 128, 16, 77)
        HD = D // H
        BLOCK = 16
        ROPE_BASE = 10000.0
        EPS = 1e-05

        def _block_diff_mask(n, block_size):
            idx = np.arange(2 * n)
            q = idx[:, None]
            kv = idx[None, :]
            fq = q >= n
            fkv = kv >= n
            bq = np.where(fq, (q - n) // block_size, q // block_size)
            bkv = np.where(fkv, (kv - n) // block_size, kv // block_size)
            block_diagonal = (bq == bkv) & (fq == fkv)
            offset_block_causal = (bq > bkv) & fkv & ~fq
            block_causal = (bq >= bkv) & fq & fkv
            return jnp.asarray(block_diagonal | offset_block_causal | block_causal)

        def _rope_tables(n):
            inv_freq = 1.0 / ROPE_BASE ** (np.arange(0, HD, 2, dtype=np.float32) / HD)
            freqs = np.outer(np.arange(n, dtype=np.float32), inv_freq)
            emb = np.concatenate([freqs, freqs], axis=-1)
            cos = jnp.asarray(np.cos(emb), jnp.float32)[None, :, None, :]
            sin = jnp.asarray(np.sin(emb), jnp.float32)[None, :, None, :]
            return (cos, sin)

        def _ln(x, w):
            xf = x.astype(jnp.float32)
            mu = jnp.mean(xf, axis=-1, keepdims=True)
            var = jnp.mean(jnp.square(xf - mu), axis=-1, keepdims=True)
            y = (xf - mu) * jax.lax.rsqrt(var + EPS)
            return y * w[None, None, :]

        def _apply_rope(t, cos, sin):
            t1, t2 = jnp.split(t, 2, axis=-1)
            rot = jnp.concatenate([-t2, t1], axis=-1)
            return t * cos + rot * sin

        def _attn(q, k, v, mask):
            scale = 1.0 / np.sqrt(HD)
            s = jnp.einsum('bqhd,bkhd->bhqk', q, k) * scale
            s = jnp.where(mask, s, jnp.finfo(s.dtype).min)
            a = jax.nn.softmax(s, axis=-1)
            return jnp.einsum('bhqk,bkhd->bqhd', a, v)
        b, s, d = x.shape
        n = s // 2
        mod = (cond_global @ adaLN_W + adaLN_b)[:, None, :]
        sh_msa, sc_msa, g_msa, sh_x, sc_x, g_x, sh_mlp, sc_mlp, g_mlp = jnp.split(mod, 9, axis=-1)
        x_norm = _ln(x, norm1_w) * (1 + sc_msa) + sh_msa
        cos, sin = _rope_tables(n)

        def qkv(h):
            t = (h @ qkv_W).reshape(b, n, 3, H, HD)
            q, k, v = (t[:, :, 0], t[:, :, 1], t[:, :, 2])
            return (_apply_rope(q, cos, sin), _apply_rope(k, cos, sin), v)
        q1, k1, v1 = qkv(x_norm[:, :n])
        q2, k2, v2 = qkv(x_norm[:, n:])
        q = jnp.concatenate([q1, q2], axis=1)
        k = jnp.concatenate([k1, k2], axis=1)
        v = jnp.concatenate([v1, v2], axis=1)
        self_out = _attn(q, k, v, attn_mask[None, None]).reshape(b, s, d) @ attn_out_W
        x = x + g_msa * self_out
        xc = _ln(x, normc_w) * (1 + sc_x) + sh_x
        qc = (xc @ cq_W).reshape(b, s, H, HD)
        kc = (cond_tokens @ ck_W).reshape(b, LC, H, HD)
        vc = (cond_tokens @ cv_W).reshape(b, LC, H, HD)
        cross = _attn(qc, kc, vc, cond_kv_mask[:, None, None, :]).reshape(b, s, d) @ co_W
        x = x + g_x * cross
        xm = _ln(x, norm2_w) * (1 + sc_mlp) + sh_mlp
        h = jax.nn.gelu(xm @ mlp_W1 + mlp_b1, approximate=True)
        mlp_out = h @ mlp_W2 + mlp_b2
        return x + g_mlp * mlp_out

    def _L2_xcond_ref(x, t_emb, context_emb, mask, ln1_g, ln1_b, ln3_g, ln3_b, ln2_g, ln2_b, sa_wq, sa_bq, sa_wk, sa_bk, sa_wv, sa_bv, sa_wo, sa_bo, ca_wq, ca_bq, ca_wk, ca_bk, ca_wv, ca_bv, ca_wo, ca_bo, tp_w, tp_b, w1, b1, w2, b2):
        import jax, jax.numpy as jnp
        import numpy as np
        D = 128
        H = 16
        HD = D // H
        FF = 4 * D
        B, NQ, NK = (8, 128, 64)
        EPS = 1e-05

        def layernorm(x, g, b):
            m = jnp.mean(x, axis=-1, keepdims=True)
            v = jnp.mean(jnp.square(x - m), axis=-1, keepdims=True)
            return (x - m) * jax.lax.rsqrt(v + EPS) * g + b

        def mha(x, ctx, wq, bq, wk, bk, wv, bv, wo, bo, mask=None):
            Bq, Nq, _ = x.shape
            Nk = ctx.shape[1]
            q = (x @ wq + bq).reshape(Bq, Nq, H, HD)
            k = (ctx @ wk + bk).reshape(Bq, Nk, H, HD)
            v = (ctx @ wv + bv).reshape(Bq, Nk, H, HD)
            scores = jnp.einsum('bqhd,bkhd->bhqk', q, k) / np.sqrt(HD)
            if mask is not None:
                scores = jnp.where(mask[:, None, None, :].astype(bool), scores, -jnp.inf)
            attn = jax.nn.softmax(scores.astype(jnp.float32), axis=-1).astype(scores.dtype)
            out = jnp.einsum('bhqk,bkhd->bqhd', attn, v).reshape(Bq, Nq, D)
            return out @ wo + bo
        t_biases = jax.nn.silu(t_emb) @ tp_w + tp_b
        t_sa, t_ca, t_mlp = jnp.split(t_biases, 3, axis=-1)
        h = layernorm(x, ln1_g, ln1_b)
        h = mha(h, h, sa_wq, sa_bq, sa_wk, sa_bk, sa_wv, sa_bv, sa_wo, sa_bo)
        x = x + h + t_sa[:, None, :]
        h = layernorm(x, ln3_g, ln3_b)
        h = mha(h, context_emb, ca_wq, ca_bq, ca_wk, ca_bk, ca_wv, ca_bv, ca_wo, ca_bo, mask=mask)
        x = x + h + t_ca[:, None, :]
        h = layernorm(x, ln2_g, ln2_b)
        h = jax.nn.gelu(h @ w1 + b1, approximate=False) @ w2 + b2
        x = x + h + t_mlp[:, None, :]
        return x

    def _L3_xcond_ref(x, c, context, W_mod, b_mod, W_qkv, b_qkv, W_proj, b_proj, W_qc, b_qc, W_kvc, b_kvc, W_cproj, b_cproj, W_mlp1, b_mlp1, W_mlp2, b_mlp2):
        import jax, jax.numpy as jnp
        import numpy as np
        LN_EPS = 1e-06

        def _ln(x):
            mu = jnp.mean(x, axis=-1, keepdims=True)
            var = jnp.var(x, axis=-1, keepdims=True)
            return (x - mu) * jax.lax.rsqrt(var + LN_EPS)
        B, N, H = x.shape
        NH = 16
        hd = H // NH
        scale = hd ** (-0.5)
        c_proj = jax.nn.silu(c) @ W_mod + b_mod
        shift_a, scale_a, gate_a, shift_m, scale_m, gate_m = jnp.split(c_proj, 6, axis=-1)

        def modulate(t, shift, sc):
            return t * (1 + sc[:, None]) + shift[:, None]
        x_norm = modulate(_ln(x), shift_a, scale_a)
        qkv = x_norm @ W_qkv + b_qkv
        q, k, v = jnp.split(qkv, 3, axis=-1)
        q = q.reshape(B, N, NH, hd).transpose(0, 2, 1, 3)
        k = k.reshape(B, N, NH, hd).transpose(0, 2, 1, 3)
        v = v.reshape(B, N, NH, hd).transpose(0, 2, 1, 3)
        attn_w = jax.nn.softmax(jnp.einsum('bhqd,bhkd->bhqk', q, k) * scale, axis=-1)
        attn_out = jnp.einsum('bhqk,bhkd->bhqd', attn_w, v)
        attn_out = attn_out.transpose(0, 2, 1, 3).reshape(B, N, H)
        attn_out = attn_out @ W_proj + b_proj
        x = x + gate_a[:, None] * attn_out
        S = context.shape[1]
        q_c = _ln(x) @ W_qc + b_qc
        kv_c = _ln(context) @ W_kvc + b_kvc
        k_c, v_c = jnp.split(kv_c, 2, axis=-1)
        q_c = q_c.reshape(B, N, NH, hd).transpose(0, 2, 1, 3)
        k_c = k_c.reshape(B, S, NH, hd).transpose(0, 2, 1, 3)
        v_c = v_c.reshape(B, S, NH, hd).transpose(0, 2, 1, 3)
        c_attn_w = jax.nn.softmax(jnp.einsum('bhqd,bhsd->bhqs', q_c, k_c) * scale, axis=-1)
        c_attn_out = jnp.einsum('bhqs,bhsd->bhqd', c_attn_w, v_c)
        c_attn_out = c_attn_out.transpose(0, 2, 1, 3).reshape(B, N, H)
        c_attn_out = c_attn_out @ W_cproj + b_cproj
        x = x + c_attn_out
        x_norm2 = modulate(_ln(x), shift_m, scale_m)
        h = jax.nn.gelu(x_norm2 @ W_mlp1 + b_mlp1)
        h = h @ W_mlp2 + b_mlp2
        x = x + gate_m[:, None] * h
        return x
    x = _L0_xcond_ref(x, cond_1024, ctx_1024, L0_xcond_w_ada, L0_xcond_b_ada, L0_xcond_w_qkv, L0_xcond_b_qkv, L0_xcond_w_so, L0_xcond_b_so, L0_xcond_w_q, L0_xcond_b_q, L0_xcond_w_kv, L0_xcond_b_kv, L0_xcond_w_co, L0_xcond_b_co, L0_xcond_w_m1, L0_xcond_b_m1, L0_xcond_w_m2, L0_xcond_b_m2)
    x = _L1_xcond_ref(x, cond_1024, ctx_1024, L1_xcond_adaLN_W, L1_xcond_adaLN_b, L1_xcond_norm1_w, L1_xcond_qkv_W, L1_xcond_attn_out_W, L1_xcond_normc_w, L1_xcond_cq_W, L1_xcond_ck_W, L1_xcond_cv_W, L1_xcond_co_W, L1_xcond_norm2_w, L1_xcond_mlp_W1, L1_xcond_mlp_b1, L1_xcond_mlp_W2, L1_xcond_mlp_b2, mask_BxS2_bf1, mask_SxS_bk0)
    x = _L2_xcond_ref(x, cond_1024, ctx_1024, mask_BxS2_ik0, L2_xcond_ln1_g, L2_xcond_ln1_b, L2_xcond_ln3_g, L2_xcond_ln3_b, L2_xcond_ln2_g, L2_xcond_ln2_b, L2_xcond_sa_wq, L2_xcond_sa_bq, L2_xcond_sa_wk, L2_xcond_sa_bk, L2_xcond_sa_wv, L2_xcond_sa_bv, L2_xcond_sa_wo, L2_xcond_sa_bo, L2_xcond_ca_wq, L2_xcond_ca_bq, L2_xcond_ca_wk, L2_xcond_ca_bk, L2_xcond_ca_wv, L2_xcond_ca_bv, L2_xcond_ca_wo, L2_xcond_ca_bo, L2_xcond_tp_w, L2_xcond_tp_b, L2_xcond_w1, L2_xcond_b1, L2_xcond_w2, L2_xcond_b2)
    x = _L3_xcond_ref(x, cond_1024, ctx_1024, L3_xcond_W_mod, L3_xcond_b_mod, L3_xcond_W_qkv, L3_xcond_b_qkv, L3_xcond_W_proj, L3_xcond_b_proj, L3_xcond_W_qc, L3_xcond_b_qc, L3_xcond_W_kvc, L3_xcond_b_kvc, L3_xcond_W_cproj, L3_xcond_b_cproj, L3_xcond_W_mlp1, L3_xcond_b_mlp1, L3_xcond_W_mlp2, L3_xcond_b_mlp2)
    return x

_drawn_inputs = setup_inputs


def setup_inputs(seed=0):
    import zlib

    import numpy as np

    out = dict(_drawn_inputs(seed))
    spreads = {'L0_xcond_b_ada': (0.0, 0.436),
     'L0_xcond_b_qkv': (0.0, 0.8),
     'L0_xcond_b_so': (0.0, 0.511),
     'L0_xcond_b_q': (0.0, 0.8),
     'L0_xcond_b_kv': (0.0, 0.8),
     'L0_xcond_b_co': (0.0, 0.467),
     'L0_xcond_b_m1': (0.0, 0.8),
     'L0_xcond_b_m2': (0.0, 0.447),
     'L1_xcond_norm1_w': (1.0, 0.6),
     'L1_xcond_normc_w': (1.0, 0.6),
     'L1_xcond_norm2_w': (1.0, 0.6),
     'L2_xcond_ln1_g': (1.0, 0.6),
     'L2_xcond_ln1_b': (0.0, 0.8),
     'L2_xcond_ln3_g': (1.0, 0.6),
     'L2_xcond_ln3_b': (0.0, 2.0),
     'L2_xcond_ln2_g': (1.0, 0.6),
     'L2_xcond_ln2_b': (0.0, 2.0),
     'L2_xcond_sa_bq': (0.0, 0.8),
     'L2_xcond_sa_bk': (0.0, 2.0),
     'L2_xcond_sa_bv': (0.0, 1.607),
     'L2_xcond_sa_bo': (0.0, 0.8),
     'L2_xcond_ca_bq': (0.0, 2.0),
     'L2_xcond_ca_bk': (0.0, 2.0),
     'L2_xcond_ca_bv': (0.0, 2.0),
     'L2_xcond_ca_bo': (0.0, 0.8),
     'L2_xcond_tp_b': (0.0, 0.532),
     'L2_xcond_b1': (0.0, 2.0),
     'L2_xcond_b2': (0.0, 0.8),
     'L3_xcond_b_mod': (0.0, 0.495),
     'L3_xcond_b_qkv': (0.0, 0.8),
     'L3_xcond_b_proj': (0.0, 0.8),
     'L3_xcond_b_qc': (0.0, 2.0),
     'L3_xcond_b_kvc': (0.0, 0.8),
     'L3_xcond_b_cproj': (0.0, 0.8),
     'L3_xcond_b_mlp1': (0.0, 2.0),
     'L3_xcond_b_mlp2': (0.0, 0.8)}
    factors = {'L0_xcond_w_qkv': 8.0,
     'L0_xcond_w_so': 8.0,
     'L0_xcond_w_q': 8.0,
     'L0_xcond_w_kv': 8.0,
     'L0_xcond_w_co': 8.0,
     'L0_xcond_w_m1': 8.0,
     'L0_xcond_w_m2': 8.0,
     'L1_xcond_adaLN_W': 4.102,
     'L1_xcond_adaLN_b': 8.0,
     'L1_xcond_qkv_W': 8.0,
     'L1_xcond_attn_out_W': 8.0,
     'L1_xcond_cq_W': 8.0,
     'L1_xcond_ck_W': 8.0,
     'L1_xcond_cv_W': 8.0,
     'L1_xcond_co_W': 8.0,
     'L1_xcond_mlp_W1': 5.304,
     'L1_xcond_mlp_b1': 8.0,
     'L1_xcond_mlp_W2': 5.155,
     'L1_xcond_mlp_b2': 32.571,
     'L2_xcond_sa_wq': 8.0,
     'L2_xcond_sa_wk': 8.0,
     'L2_xcond_sa_wv': 8.0,
     'L2_xcond_sa_wo': 2.781,
     'L2_xcond_ca_wq': 64.0,
     'L2_xcond_ca_wk': 64.0,
     'L2_xcond_ca_wv': 8.0,
     'L2_xcond_ca_wo': 6.078,
     'L2_xcond_w1': 6.862,
     'L2_xcond_w2': 4.793,
     'L3_xcond_W_qc': 3.234}
    for name, (base, spread) in spreads.items():
        noise = np.random.default_rng([zlib.crc32(name.encode()), seed]).standard_normal(out[name].shape)
        drawn = base * np.exp(spread * noise) if base else spread * noise
        out[name] = jnp.asarray(drawn.astype(out[name].dtype))
    for name, factor in factors.items():
        out[name] = (out[name] * factor).astype(out[name].dtype)
    return out
```

```python
from contextlib import ExitStack

import numpy as np
import concourse.bass as bass
import concourse.mybir as mybir

F32 = mybir.dt.float32
BF16 = mybir.dt.bfloat16
U8 = mybir.dt.uint8
I32 = mybir.dt.int32
ALU = mybir.AluOpType
ACT = mybir.ActivationFunctionType
AX = mybir.AxisListType

P = 128
B, L, C, H, HD = 4, 512, 128, 16, 8
T = L // P
NC = 77
WIN, SHIFT, TOPK = 64, 32, 16
HID = 512
NL = 4
J = H // 2
QUERY_PART = (0, 0, 0, 1, 1, 2)
KEY_PART = (0, 1, 2, 0, 1, 0)
ROWS = 8 * len(QUERY_PART)
ROW_MASK, ROW_MAX = ROWS, ROWS + 1
ROWS_FULL = ROWS + 4
QSCALE = float(1.0 / np.sqrt(np.float32(HD)))
MASKED = -1.0e30
TAKEN = -3.0e38
EPS = (1e-6, 1e-5, 1e-5, 1e-6)
FF_TILES = (8, 4, 4, 4)

CHUNKS = ([(l, kind, br) for l in (0, 1) for br in range(3) for kind in ("sh", "sc", "g")]
          + [(2, "t", br) for br in range(3)]
          + [(3, kind, br) for br in (0, 2) for kind in ("sh", "sc", "g")])


def weight_table():
    names = []
    for l in range(NL):
        names += [(f"q{l}", C), (f"k{l}", C), (f"v{l}", C), (f"o{l}", C)]
        if l == 1:
            names += [("qrot1", C), ("krot1", C)]
        names += [(f"cq{l}", C), (f"ck{l}", C), (f"cv{l}", C), (f"co{l}", C)]
        names += [(f"f1_{l}", FF_TILES[l] * P), (f"f2_{l}", HID)]
    at, off = {}, 0
    for n, w in names:
        at[n] = (off, w)
        off += w
    return at, off


def column_table():
    names = [("cond", B), ("adab", len(CHUNKS))]
    for l in (0, 2, 3):
        names += [(f"{n}{l}", 1) for n in ("bq", "bcq")]
    for l in (0, 2, 3):
        names += [(f"{n}{l}", 1) for n in ("bk", "bv", "bo", "bck", "bcv", "bco")]
    for l in range(NL):
        names += [(f"b1_{l}", FF_TILES[l]), (f"b2_{l}", 1)]
    names += [("w1", 3), ("w2", 3), ("lb2", 3)]
    at, off = {}, 0
    for n, w in names:
        at[n] = (off, w)
        off += w
    return at, off


def build(nc, x, wpack, ada_w, cols, ctx_t, ctx_tok, mask_self, mask1, mask2, ident_in, rope, const_rows, out):
    const_rows = const_rows.bitcast(BF16)
    WT, NW = weight_table()
    CT, NCOL = column_table()
    ctx = ExitStack()
    with ctx:
        def sb(name, shape, dt=F32):
            return ctx.enter_context(nc.sbuf_tensor(name, shape, dt))

        def sem(name):
            return ctx.enter_context(nc.semaphore(name))

        W = sb("weights", [P, NW])
        COL = sb("columns", [P, NCOL])
        ident = sb("ident", [P, P])
        identb = sb("identb", [P, P], BF16)
        xr = sb("x_rolled", [P, B * T, C])
        xs = sb("x_state", [P, B * T, C])
        ctxT = sb("ctx_channels", [P, B * NC])
        ctxLT = sb("ctx_normed_channels", [P, B * NC])
        ctxK = sb("ctx_tokens", [NC, B, C])
        scond = sb("silu_cond", [P, B])
        mod = sb("mod", [P, len(CHUNKS), B])
        cb = sb("out_bias", [P, 6])
        VEC = sb("vectors", [P, NL * B * 12])
        bqs = sb("q_bias_scaled", [P, 6])
        kc32 = sb("ctx_keys", [P, B * NC])
        kcp = sb("ctx_key_parts", [P, 3, B * NC], BF16)
        KC = sb("ctx_keys_stacked", [P, NL, J, B * NC], BF16)
        VC = sb("ctx_values", [NC, NL, B, C])
        mword = sb("ctx_mask_raw1", [P, B * NC // 4], I32)
        mrow8 = mword[:, :].bitcast(U8)
        mrow32 = sb("ctx_mask_raw2", [P, B * NC], I32)
        mkf = sb("ctx_mask", [P, B * NC])
        mkany = sb("ctx_any", [P, B])
        poison = sb("ctx_none", [P, B])
        mkb = sb("ctx_mask_bias", [8, 2, B * NC], BF16)
        ms32 = sb("self_mask_raw", [P, T, L // 4], I32)
        ms8 = ms32[:, :, :].bitcast(U8)
        MB = sb("self_bias", [P, T, L], BF16)
        MBT = sb("self_bias_t", [P, T, L], BF16)
        rany = sb("row_any", [P, T])
        diag = sb("row_any_diag", [P, T, P])
        ones = sb("ones", [P, P])
        ROPE = sb("rope", [P, 2, L])
        ROPEQ = sb("rope_q", [P, 2, L])
        cst = sb("ctx_stats", [NC, B, 6])
        cmv = sb("ctx_mv", [NC, B, 2])
        cve = sb("ctx_ve", [NC, 2 * B])
        V4 = sb("vec4", [P, 4])
        st = sb("stats", [P, T, 6])
        mv = sb("mv", [P, T, 2])
        ve = sb("ve", [P, T])
        rstd = sb("rstd", [P, T])
        mhalf = sb("minus_half", [P, T])
        XN = sb("x_normed", [P, T, C])
        hT = sb("h_channels", [P, L])
        qk = sb("qk", [P, 2, L])
        ra = sb("rope_a", [P, L])
        rb = sb("rope_b", [P, L])
        qkp = sb("qk_parts", [P, 2, 3, L], BF16)
        QS = sb("q_stacked", [P, J, L], BF16)
        KS = sb("k_stacked", [P, J, L], BF16)
        KX = sb("ctx_k_stacked", [P, J, NC], BF16)
        VA = sb("values", [P, T, H * 32])
        VX = sb("ctx_values_now", [NC, H * 32])
        mneg = sb("minus_max", [P, T, H])
        m3 = sb("max_parts", [P, T, 2, 3, J], BF16)
        mT = sb("max_rows", [48, L], BF16)
        PT = sb("probs", [P, 4, 2 * L])
        ADA = PT[:, :, :].rearrange("p a n -> p (a n)")
        U = sb("out_rows", [P, 2, L])
        rec = sb("recip", [P, T * H])
        ON = sb("out_normed", [P, T, C])
        OT = sb("out_channels", [P, L])
        YT = sb("y_channels", [P, L])
        HB = sb("hidden", [P, 4, L])
        SX = sb("topk_scores", [P, 2, 8, NC])
        W1 = sb("topk_w1", [P, 8, NC])
        W2 = sb("topk_w2", [P, 2, 8, NC])
        HBF = HB[:, :, :].rearrange("p a n -> p (a n)")
        E = HBF[:, 0:16 * NC].rearrange("p (a h n) -> p a h n", a=2, h=8)
        PW = HBF[:, 16 * NC:24 * NC].rearrange("p (h n) -> p h n", h=8)
        v8 = sb("top8", [P, 2, 8, 8])
        nm8 = sb("topk_minus_max", [P, 2, 8])

        PS = ctx.enter_context(nc.psum_tensor("PS", [P, 8, 512], F32))
        M0, M1 = 6, 7
        M0B = PS[:, M0, :].bitcast(BF16)
        M1B = PS[:, M1, :].bitcast(BF16)

        names = """loaded x_loaded const_rows_in base_consts prep_act prep_pe prep_dve prep_kparts prep_stacked
            prep_mask_rows unrolled stats_done aggr_done ve_ready rstd_ready xn_ready xnT_ready hT_ready
            qk_ready v_ready qk_evac rope_step q_ready k_ready q_part k_part va_ready q_stacked k_stacked kvx_ready
            sA_ready sA_used m_step mT_ps mT_ready m_stacked sB_ready p_ready pv_used u_ready
            T_ready rec_ready on_ready onT_ready oT_ready y_ps y_ready yb_ready x_done
            silu_ready ctx_rstd_ready stats_ctx ff_ready gate_ready hid_ready sx_ready top_step w2_ready negm_ready e_ready pick_ready pw_ready pT_ready
            stored waits_held""".split()
        S = {n: sem(n) for n in names}

        def w(name, a=0, n=None):
            o, width = WT[name]
            return W[:, o + a:o + (width if n is None else a + n)]

        def col(name, a=0):
            o, _ = CT[name]
            return COL[:, o + a:o + a + 1]

        def attn(l, b, c):
            return 8 * l + c + 2 * b

        def branch(l, b, br):
            return 12 * l + (8 + b if br == 2 else 2 * b + br)

        def selfs(l, b):
            return 4 * l + b

        def counted(n):
            def f(l, b, c):
                return 4 * sum(sum(n[m]) for m in range(l)) + (n[l][0] if c else 0) + b * sum(n[l])
            return f

        units_a = counted([(4, 8)] + [(32, 8)] * 3)
        units_b = counted([(4, 8)] + [(32, 8)] * 3)
        reduced = counted([(4, 0)] + [(32, 8)] * 3)
        scored = counted([(4, 0)] + [(32, 8)] * 3)
        maxes = counted([(1, 0)] + [(1, 1)] * 3)

        def held(eng, semaphore, value):
            eng.wait_ge(semaphore, value)
            eng.sem_inc(S["waits_held"], 1)

        block = ctx.enter_context(nc.Block())

        @block.sync
        def _(sp):
            for dst, src in ((COL[:, :], cols), (ident[:, :], ident_in), (ctxT[:, :], ctx_t),
                             (W[:, :], wpack), (ADA[:, 0:len(CHUNKS) * C], ada_w),
                             (ctxK[:, :, :], ctx_tok), (ms32[:, :, :], mask_self.rearrange("(t p) k -> p t k", p=P)),
                             (mword[:, :], mask1.rearrange("(a n) -> a n", a=1).broadcast_to([P, B * NC // 4])),
                             (mrow32[:, :], mask2.rearrange("(a n) -> a n", a=1).broadcast_to([P, B * NC])),
                             (ROPE[:, :, :], rope)):
                sp.dma_start(dst, src).then_inc(S["loaded"], 16)
            for b in range(B):
                sp.dma_start(xr[:, T * b:T * b + T, :],
                             x[b].rearrange("(t p) c -> p t c", p=P)).then_inc(S["x_loaded"], 16)
            for i in range(2):
                r = 64 * i + ROW_MASK
                sp.dma_start(KS[r:r + 4, :, :], const_rows.rearrange("r (j n) -> r j n", j=J)).then_inc(
                    S["const_rows_in"], 16)
                for l in range(NL):
                    sp.dma_start(KC[r:r + 4, l, :, :],
                                 const_rows[:, 0:J * B * NC].rearrange("r (j n) -> r j n", j=J)).then_inc(
                        S["const_rows_in"], 16)
            for l in range(NL):
                for r, part in enumerate(KEY_PART):
                    sp.wait_ge(S["prep_kparts"], 4 * l + (1, 3, 4)[part])
                    for i in range(2):
                        sp.dma_start(KC[64 * i + 8 * r:64 * i + 8 * r + 8, l, :, :],
                                     kcp[64 * i:64 * i + 64, part, :]).then_inc(S["prep_stacked"], 16)
            sp.wait_ge(S["const_rows_in"], 16 * 2 * (1 + NL))
            sp.wait_ge(S["prep_mask_rows"], 2)
            for i in range(2):
                r = 64 * i + ROW_MASK
                for n in range(2):
                    sp.dma_start(KC[r:r + 1, 1 + n, :, :], mkb[:, n, :]).then_inc(S["prep_stacked"], 16)

            def stack(dst, which, map_, ready, base, done):
                for part in range(3):
                    sp.wait_ge(ready, base + (1, 3, 4)[part])
                    for r in range(len(map_)):
                        if map_[r] == part:
                            for i in range(2):
                                sp.dma_start(dst[64 * i + 8 * r:64 * i + 8 * r + 8, :, :],
                                             qkp[64 * i:64 * i + 64, which, part, :]).then_inc(done, 16)

            for l in range(NL):
                with sp.Fori(0, B) as b:
                    for c in range(2):
                        a = attn(l, b, c)
                        if c == 0:
                            stack(KS, 1, KEY_PART, S["k_part"], 4 * selfs(l, b), S["k_stacked"])
                        stack(QS, 0, QUERY_PART, S["q_part"], 4 * a, S["q_stacked"])
                        if l == 0 and c == 1:
                            continue
                        sp.wait_ge(S["mT_ready"], maxes(l, b, c) + 1)
                        for i in range(2):
                            sp.dma_start(QS[64 * i + ROW_MAX:64 * i + ROW_MAX + 3, :, :],
                                         mT[24 * i:24 * i + 24, :]).then_inc(S["m_stacked"], 16)
                if l == 0:
                    sp.wait_ge(S["x_done"], 12)
                    q = P - SHIFT
                    sp.dma_start(xs[SHIFT:P, :, :], xr[0:q, :, :]).then_inc(S["unrolled"], 16)
                    for b in range(B):
                        sp.dma_start(xs[0:SHIFT, T * b + 1:T * b + T, :],
                                     xr[q:P, T * b:T * b + T - 1, :]).then_inc(S["unrolled"], 16)
                        sp.dma_start(xs[0:SHIFT, T * b:T * b + 1, :],
                                     xr[q:P, T * b + T - 1:T * b + T, :]).then_inc(S["unrolled"], 16)
            for b in range(B):
                sp.wait_ge(S["x_done"], branch(NL - 1, b, 2) + 1)
                sp.dma_start(out[b].rearrange("(t p) c -> p t c", p=P), xs[:, T * b:T * b + T, :]).then_inc(
                    S["stored"], 16)
            sp.wait_ge(S["stored"], 16 * B)

        @block.gpsimd
        def _(pool):
            g = nc.gpsimd
            g.memset(mhalf[:, :], -0.5).then_inc(S["base_consts"], 1)
            g.memset(QS[:, :, :], 1.0).then_inc(S["base_consts"], 1)
            g.memset(VX[:, :], 0.0).then_inc(S["base_consts"], 1)
            g.memset(VA[:, :, :], 0.0).then_inc(S["base_consts"], 1)
            g.memset(ones[:, :], 1.0).then_inc(S["base_consts"], 1)
            pool.wait_ge(S["base_consts"], 4)
            for s in range(2):
                VAv = VA[:, :, 256 * s:256 * s + 256].rearrange("p t (h e) -> p t h e", e=32)
                g.memset(VAv[:, :, :, 16 * s + 8:16 * s + 16], 1.0).then_inc(S["base_consts"], 1)
                VXv = VX[:, 256 * s:256 * s + 256].rearrange("p (h e) -> p h e", e=32)
                g.memset(VXv[:, :, 16 * s + 8:16 * s + 16], 1.0).then_inc(S["base_consts"], 1)
            pool.wait_ge(S["prep_dve"], 1)
            pool.wait_ge(S["base_consts"], 1)
            g.tensor_tensor(cve[:, B:2 * B], cve[:, 0:B], mhalf[0:NC, :], ALU.pow).then_inc(S["ctx_rstd_ready"], 1)

            def inverse_deviation(k):
                pool.wait_ge(S["ve_ready"], k + 1)
                g.tensor_tensor(rstd[:, :], ve[:, :], mhalf[:, :], ALU.pow).then_inc(S["rstd_ready"], 1)

            for l in range(NL):
                with pool.Fori(0, B) as b:
                    n = selfs(l, b)
                    inverse_deviation(branch(l, b, 0))
                    held(pool, S["k_ready"], n + 1)
                    k32, kp = qk[:, 1, :], qkp[:, 1, :, :]
                    g.tensor_copy(kp[:, 0, :], k32).then_inc(S["k_part"], 1)
                    pool.wait_ge(S["k_part"], 4 * n + 1)
                    g.tensor_tensor(k32, k32, kp[:, 0, :], ALU.subtract).then_inc(S["k_part"], 1)
                    held(pool, S["k_part"], 4 * n + 2)
                    g.tensor_copy(kp[:, 1, :], k32).then_inc(S["k_part"], 1)
                    pool.wait_ge(S["k_part"], 4 * n + 3)
                    g.tensor_tensor(kp[:, 2, :], k32, kp[:, 1, :], ALU.subtract).then_inc(S["k_part"], 1)
                    inverse_deviation(branch(l, b, 1))
                    if l == 0:
                        pool.wait_ge(S["prep_stacked"], 16 * (12 * NL + 4))
                        pool.wait_ge(S["prep_dve"], PREP_VC)
                        pool.wait_ge(S["base_consts"], 9)
                    pool.wait_ge(S["rstd_ready"], branch(l, b, 1) + 1)
                    for i in range(2):
                        r = slice(64 * i, 64 * i + ROWS_FULL)
                        if i:
                            held(pool, S["kvx_ready"], 4 * n + i)
                        g.tensor_copy(KX[r, :, :], KC[r, l, :, bass.ds(NC * b, NC)]).then_inc(S["kvx_ready"], 1)
                    for s in range(2):
                        held(pool, S["kvx_ready"], 4 * n + 2 + s)
                        src = VC[:, l, bass.ds(b, 1), 64 * s:64 * s + 64].rearrange("p a (h d) -> p (a h) d", d=HD)
                        dst = VX[:, 256 * s:256 * s + 256].rearrange("p (h e) -> p h e", e=32)
                        g.tensor_copy(dst[:, :, 16 * s:16 * s + 8], src).then_inc(S["kvx_ready"], 1)
                    if l == 0:
                        for u in range(8):
                            held(pool, S["w2_ready"], 8 * b + u + 1)
                            g.tensor_scalar(PW[:, :, :], W2[:, u % 2, :, :], TAKEN / 2, None, ALU.is_le).then_inc(
                                S["pick_ready"], 1)
                            pool.wait_ge(S["pick_ready"], 8 * b + u + 1)
                            pool.wait_ge(S["e_ready"], 8 * b + u + 1)
                            g.tensor_tensor(PW[:, :, :], PW[:, :, :], E[:, u % 2, :, :], ALU.mult).then_inc(
                                S["pw_ready"], 1)
                            held(pool, S["pT_ready"], 8 * b + u + 1)
                with pool.Fori(0, B) as b:
                    inverse_deviation(branch(l, b, 2))

        @block.scalar
        def _(act):
            a_ = nc.scalar
            act.wait_ge(S["loaded"], 16 * 10)
            a_.activation(scond[:, :], COL[:, CT["cond"][0]:CT["cond"][0] + B], ACT.Silu).then_inc(S["silu_ready"], 1)
            act.wait_ge(S["prep_pe"], PE_CTXT)
            a_.activation(ctxLT[:, :], PS[:, M1, 0:B * NC], ACT.Identity).then_inc(S["prep_act"], 1)
            for l in range(NL):
                act.wait_ge(S["prep_pe"], PE_K[l])
                if l:
                    act.wait_ge(S["prep_kparts"], 4 * l)
                a_.activation(kc32[:, :], PS[:, l, 0:B * NC], ACT.Identity,
                              bias=(0.0 if l == 1 else col(f"bck{l}"))).then_inc(S["prep_act"], 1)

            def to_channels(k):
                act.wait_ge(S["xnT_ready"], k + 1)
                a_.activation(hT[:, :], PS[:, M0, :], ACT.Identity, bias=V4[:, 1:2], scale=V4[:, 0:1]).then_inc(
                    S["hT_ready"], 1)

            def gated(k):
                act.wait_ge(S["y_ps"], k + 1)
                a_.activation(YT[:, :], PS[:, M1, :], ACT.Identity, bias=V4[:, 3:4], scale=V4[:, 2:3]).then_inc(
                    S["y_ready"], 1)

            def exps(l, b, c):
                base = units_b(l, b, c)
                np_ = NC if c else P
                for u in range(8 if c else 32 if l else 4):
                    act.wait_ge(S["sB_ready"], scored(l, b, c) + u + 1)
                    if u >= 4:
                        act.wait_ge(S["pv_used"], base + u - 3)
                    bk = 2 * (u % 2)
                    a_.activation(PT[0:np_, u % 4, :].rearrange("p (a n) -> p a n", a=2), PS[0:np_, bk:bk + 2, :],
                                  ACT.Exp).then_inc(S["p_ready"], 1)

            def finish(l, b, c, k):
                a = attn(l, b, c)
                act.wait_ge(S["pv_used"], units_b(l, b, c) + (32 if l and not c else 8 if c else 4))
                if l == 0 and c == 0:
                    o = U[:, :, :].rearrange("p k (t w n) -> p k t w n", t=T, w=2)
                    for wd in range(2):
                        for k2 in range(2):
                            ins = a_.activation(o[:, k2, :, wd, :],
                                                PS[:, 4 + 2 * wd + k2, 0:256].rearrange("p (t n) -> p t n", t=T),
                                                ACT.Identity)
                else:
                    ins = a_.activation(U[:, :, :], PS[:, 4:6, :], ACT.Identity)
                ins.then_inc(S["u_ready"], 1)
                act.wait_ge(S["onT_ready"], a + 1)
                a_.activation(OT[:, :], PS[:, M0, :], ACT.Identity).then_inc(S["oT_ready"], 1)
                gated(k)

            for l in range(NL):
                with act.Fori(0, B) as b:
                    n = selfs(l, b)
                    to_channels(branch(l, b, 0))
                    if l != 1:
                        act.wait_ge(S["qk_ready"], 2 * n + 1)
                        a_.activation(qk[:, 0, :], PS[:, 0, :], ACT.Identity, bias=bqs[:, BQ[l]:BQ[l] + 1],
                                      scale=QSCALE).then_inc(S["q_ready"], 1)
                        a_.activation(qk[:, 1, :], PS[:, 1, :], ACT.Identity, bias=col(f"bk{l}")).then_inc(
                            S["k_ready"], 1)
                    exps(l, b, 0)
                    finish(l, b, 0, branch(l, b, 0))
                    to_channels(branch(l, b, 1))
                    act.wait_ge(S["qk_ready"], 2 * n + 2)
                    a_.activation(qk[:, 0, :], PS[:, 0, :], ACT.Identity,
                                  bias=(0.0 if l == 1 else bqs[:, BQ[l] + 1:BQ[l] + 2]),
                                  scale=QSCALE).then_inc(S["q_ready"], 1)
                    if l:
                        exps(l, b, 1)
                    else:
                        def scores_out(u):
                            act.wait_ge(S["sA_ready"], units_a(0, b, 1) + u + 1)
                            if u >= 2:
                                act.wait_ge(S["w2_ready"], 8 * b + u - 1)
                                act.wait_ge(S["e_ready"], 8 * b + u - 1)
                            a_.activation(SX[:, u % 2, :, :].rearrange("p (i j) n -> p i (j n)", i=2),
                                          PS[:, 2 * (u % 2):2 * (u % 2) + 2, 0:4 * NC], ACT.Identity).then_inc(
                                S["sx_ready"], 1)

                        def exp_top(u):
                            act.wait_ge(S["negm_ready"], 8 * b + u + 1)
                            if u >= 2:
                                act.wait_ge(S["pw_ready"], 8 * b + u - 1)
                            for h in range(8):
                                ins = a_.activation(E[:, u % 2, h, :], SX[:, u % 2, h, :], ACT.Exp,
                                                    bias=nm8[:, u % 2, h:h + 1])
                            ins.then_inc(S["e_ready"], 1)

                        def probs_out(u):
                            act.wait_ge(S["pT_ready"], 8 * b + u + 1)
                            if u >= 2:
                                act.wait_ge(S["pv_used"], units_b(0, b, 1) + u - 1)
                            a_.activation(PT[0:NC, u % 2, :].rearrange("p (a n) -> p a n", a=2),
                                          PS[0:NC, M0:M0 + 2, :], ACT.Identity).then_inc(S["p_ready"], 1)

                        for u in range(8):
                            scores_out(u)
                            exp_top(u)
                            if u:
                                probs_out(u - 1)
                        probs_out(7)
                    finish(l, b, 1, branch(l, b, 1))
                with act.Fori(0, B) as b:
                    n, k = selfs(l, b), branch(l, b, 2)
                    to_channels(k)
                    for m in range(4):
                        act.wait_ge(S["ff_ready"], 4 * n + m + 1)
                        if l == 0:
                            a_.activation(HB[:, m, :], PS[:, 2 * (m % 2), :], ACT.Silu,
                                          bias=col("b1_0", m)).then_inc(S["gate_ready"], 1)
                        else:
                            a_.activation(HB[:, m, :], PS[:, m, :], ACT.Gelu if l == 2 else ACT.Gelu_apprx_tanh,
                                          bias=col(f"b1_{l}", m)).then_inc(S["hid_ready"], 1)
                    gated(k)

        @block.tensor
        def _(pe):
            t_ = nc.tensor

            def mm(o, a, m, start=True, stop=True, **kw):
                return t_.matmul(o, a, m, start=start, stop=stop, **kw)

            pe.wait_ge(S["loaded"], 16 * 10)
            pe.wait_ge(S["silu_ready"], 1)
            for n, (l, kind, br) in enumerate(CHUNKS):
                cond = COL[:, CT["cond"][0]:CT["cond"][0] + B] if l == 1 else scond[:, :]
                mm(PS[:, M0, B * n:B * n + B], ADA[:, C * n:C * n + C], cond)
            n0 = B * len(CHUNKS)
            for n, l in enumerate((0, 2, 3)):
                mm(PS[:, M0, n0 + 2 * n:n0 + 2 * n + 1], w(f"o{l}"), col(f"bv{l}"))
                ins = mm(PS[:, M0, n0 + 2 * n + 1:n0 + 2 * n + 2], w(f"co{l}"), col(f"bcv{l}"))
            ins.then_inc(S["prep_pe"], 1)
            pe.wait_ge(S["prep_dve"], DVE_CTX)
            for b in range(B):
                ins = t_.transpose(PS[:, M1, NC * b:NC * b + NC], ctxK[:, b, :], ident[0:NC, 0:NC])
            ins.then_inc(S["prep_pe"], 1)
            for l in range(NL):
                if l == 3:
                    pe.wait_ge(S["prep_act"], 1)
                src = ctxLT if l == 3 else ctxT
                mm(PS[:, l, 0:B * NC], w(f"ck{l}"), src[:, :]).then_inc(S["prep_pe"], 1)
                if l >= 2:
                    pe.wait_ge(S["prep_dve"], DVE_VC[l - 2])
                for b in range(B):
                    ins = mm(PS[0:NC, 4 + l % 2, C * b:C * b + C], src[:, NC * b:NC * b + NC], w(f"cv{l}"))
                ins.then_inc(S["prep_pe"], 1)
            pe.wait_ge(S["prep_dve"], DVE_MASK)
            for kt in range(T):
                for t in range(T):
                    dst = (M0B, M1B)[kt // 2]
                    o = 512 * (kt % 2) + P * t
                    ins = t_.transpose(dst[:, o:o + P], MB[:, t, P * kt:P * kt + P], identb[:, :])
            ins.then_inc(S["prep_pe"], 1)
            for t in range(T):
                ins = mm(PS[:, 4, P * t:P * t + P], ones[:, :], diag[:, t, :])
            ins.then_inc(S["prep_pe"], 1)

            def turned_norm(k):
                for t in range(T):
                    pe.wait_ge(S["xn_ready"], 4 * k + t + 1)
                    ins = t_.transpose(PS[:, M0, P * t:P * t + P], XN[:, t, :], ident[:, :])
                ins.then_inc(S["xnT_ready"], 1)
                pe.wait_ge(S["hT_ready"], k + 1)

            def back_to_tokens(k):
                pe.wait_ge(S["y_ready"], k + 1)
                for t in range(T):
                    ins = t_.transpose(PS[:, M0, P * t:P * t + P], YT[:, P * t:P * t + P], ident[:, :])
                ins.then_inc(S["yb_ready"], 1)

            def output(l, b, c, k):
                a = attn(l, b, c)
                pe.wait_ge(S["u_ready"], a + 1)
                for t in range(T):
                    for k2 in range(2):
                        o = 256 * t + 128 * k2
                        ins = t_.transpose(PS[:, 4 + o // 512, o % 512:o % 512 + P], U[:, k2, P * t:P * t + P],
                                           ident[:, :])
                ins.then_inc(S["T_ready"], 1)
                pe.wait_ge(S["on_ready"], a + 1)
                for t in range(T):
                    ins = t_.transpose(PS[:, M0, P * t:P * t + P], ON[:, t, :], ident[:, :])
                ins.then_inc(S["onT_ready"], 1)
                pe.wait_ge(S["oT_ready"], a + 1)
                mm(PS[:, M1, :], w(f"{'c' if c else ''}o{l}"), OT[:, :]).then_inc(S["y_ps"], 1)
                back_to_tokens(k)

            def heads(pair, i):
                return slice(64 * i, 64 * i + ROWS), slice(64 * i, 64 * i + ROWS_FULL)

            def max_rows(l, b, c):
                n = maxes(l, b, c)
                held(pe, S["m_step"], 4 * n + 4)
                for t in range(T):
                    ins = t_.transpose(M0B[0:48, P * t:P * t + P],
                                       m3[:, t, :, :, :].rearrange("p i r j -> p (i r j)"), identb[:, :])
                ins.then_inc(S["mT_ps"], 1)
                held(pe, S["m_stacked"], 32 * (n + 1))

            def values_in(l, b, c, hd, lhs_rows, kt, moving, o, start, stop):
                g, bank = hd % 4, (hd // 4) % 2
                va = VX[0:NC, 32 * hd:32 * hd + 32] if c else VA[lhs_rows, kt, 32 * hd:32 * hd + 32]
                return mm(o[32 * g:32 * g + 32], va, moving, start=start, stop=stop, skip_group_check=True)

            for l in range(NL):
                with pe.Fori(0, B) as b:
                    n = selfs(l, b)
                    a, k = attn(l, b, 0), branch(l, b, 0)
                    turned_norm(k)
                    mm(PS[:, 0, :], w(f"q{l}"), hT[:, :])
                    ins = mm(PS[:, 1, :], w(f"k{l}"), hT[:, :])
                    if l == 1:
                        mm(PS[:, 2, :], w("qrot1"), hT[:, :])
                        ins = mm(PS[:, 3, :], w("krot1"), hT[:, :])
                    ins.then_inc(S["qk_ready"], 1)
                    for t in range(T):
                        ins = mm(PS[:, M1, P * t:P * t + P], hT[:, P * t:P * t + P], w(f"v{l}"))
                    ins.then_inc(S["v_ready"], 1)
                    ua, ub = units_a(l, b, 0), units_b(l, b, 0)
                    pe.wait_ge(S["k_stacked"], 192 * (n + 1))
                    held(pe, S["q_stacked"], 192 * (a + 1))
                    if l == 0:
                        pe.wait_ge(S["const_rows_in"], 16 * 2 * (1 + NL))
                        for t in range(T):
                            if t >= 2:
                                held(pe, S["sA_used"], reduced(l, b, 0) + t - 1)
                            for i in range(2):
                                r = slice(64 * i, 64 * i + ROWS)
                                for j in range(J):
                                    for wd in range(2):
                                        q0 = P * t + WIN * wd
                                        ins = mm(PS[64 * wd:64 * wd + 64, 2 * (t % 2) + i, WIN * j:WIN * j + WIN],
                                                 QS[r, j, q0:q0 + WIN], KS[r, j, q0:q0 + WIN])
                            ins.then_inc(S["sA_ready"], 1)
                    else:
                        for u in range(32):
                            t, j = divmod(u, J)
                            if u >= 2:
                                pe.wait_ge(S["sA_used"], reduced(l, b, 0) + u - 1)
                            for i in range(2):
                                r = slice(64 * i, 64 * i + ROWS)
                                ins = mm(PS[:, 2 * (u % 2) + i, :], QS[r, j, P * t:P * t + P], KS[r, j, :],
                                         stop=l != 1)
                            if l == 1:
                                for i in range(2):
                                    ins = mm(PS[:, 2 * (u % 2) + i, :], identb[:, :], MB[:, t, :], start=False)
                            ins.then_inc(S["sA_ready"], 1)
                    max_rows(l, b, 0)
                    held(pe, S["va_ready"], 2 * n + 2)
                    if l == 0:
                        def win_scores(t):
                            if t >= 2:
                                held(pe, S["p_ready"], ub + t - 1)
                            for i in range(2):
                                r = slice(64 * i, 64 * i + ROWS_FULL)
                                for j in range(J):
                                    for wd in range(2):
                                        q0 = P * t + WIN * wd
                                        ins = mm(PS[64 * wd:64 * wd + 64, 2 * (t % 2) + i, WIN * j:WIN * j + WIN],
                                                 KS[r, j, q0:q0 + WIN], QS[r, j, q0:q0 + WIN])
                            ins.then_inc(S["sB_ready"], 1)

                        def win_values(t):
                            held(pe, S["p_ready"], ub + t + 1)
                            for wd in range(2):
                                r = slice(64 * wd, 64 * wd + 64)
                                for hd in range(H):
                                    i, j = hd % 2, hd // 2
                                    o = PS[:, 4 + 2 * wd + (hd // 4) % 2, WIN * t:WIN * t + WIN]
                                    ins = values_in(l, b, 0, hd, r, t,
                                                    PT[r, t, 512 * i + WIN * j:512 * i + WIN * j + WIN], o,
                                                    t == 0 and hd < 8, t == T - 1 and hd >= 8)
                            ins.then_inc(S["pv_used"], 1)

                        for t in range(T):
                            win_scores(t)
                            if t:
                                win_values(t - 1)
                        win_values(T - 1)
                    else:
                        def scores(u):
                            q, kt, half = u // 8, u % 8 // 2, u % 2
                            j = 2 * q + half
                            if u >= 2:
                                pe.wait_ge(S["p_ready"], ub + u - 1)
                            for i in range(2):
                                r = slice(64 * i, 64 * i + ROWS_FULL)
                                ins = mm(PS[:, 2 * (u % 2) + i, :], KS[r, j, P * kt:P * kt + P], QS[r, j, :],
                                         stop=l != 1)
                            if l == 1:
                                for i in range(2):
                                    ins = mm(PS[:, 2 * (u % 2) + i, :], identb[:, :], MBT[:, kt, :], start=False)
                            ins.then_inc(S["sB_ready"], 1)

                        def values(u):
                            q, kt = u // 8, u % 8 // 2
                            pe.wait_ge(S["p_ready"], ub + u + 2)
                            for g in range(4):
                                ins = values_in(l, b, 0, 4 * q + g, slice(0, P), kt,
                                                PT[:, (u + g // 2) % 4, 512 * (g % 2):512 * (g % 2) + 512],
                                                PS[:, 4 + q % 2, :], q < 2 and kt == 0, q >= 2 and kt == 3)
                            ins.then_inc(S["pv_used"], 2)

                        for u in range(0, 32, 2):
                            scores(u)
                            scores(u + 1)
                            if u:
                                values(u - 2)
                        values(30)
                    output(l, b, 0, k)
                    a, k = attn(l, b, 1), branch(l, b, 1)
                    turned_norm(k)
                    mm(PS[:, 0, :], w(f"cq{l}"), hT[:, :]).then_inc(S["qk_ready"], 1)
                    ua, ub = units_a(l, b, 1), units_b(l, b, 1)
                    pe.wait_ge(S["kvx_ready"], 4 * n + 4)
                    held(pe, S["q_stacked"], 192 * (a + 1))

                    def ctx_scores(u):
                        t, part = divmod(u, 2)
                        if u >= 2:
                            pe.wait_ge(S["sA_used" if l else "sx_ready"], (reduced(l, b, 1) if l else 8 * b) + u - 1)
                        rows = ROWS + 1 if l in (1, 2) else ROWS
                        for i in range(2):
                            r = slice(64 * i, 64 * i + rows)
                            for jj in range(4):
                                j = 4 * part + jj
                                ins = mm(PS[:, 2 * (u % 2) + i, NC * jj:NC * jj + NC], QS[r, j, P * t:P * t + P],
                                         KX[r, j, :])
                        ins.then_inc(S["sA_ready"], 1)

                    if l:
                        for u in range(8):
                            ctx_scores(u)
                        max_rows(l, b, 1)

                        def scores_x(j):
                            if j >= 2:
                                pe.wait_ge(S["p_ready"], ub + j - 1)
                            for i in range(2):
                                r = slice(64 * i, 64 * i + ROWS_FULL)
                                ins = mm(PS[0:NC, 2 * (j % 2) + i, :], KX[r, j, :], QS[r, j, :])
                            ins.then_inc(S["sB_ready"], 1)

                        def values_x(j):
                            pe.wait_ge(S["p_ready"], ub + j + 2)
                            for g in range(4):
                                hd = 2 * j + g
                                ins = values_in(l, b, 1, hd, None, 0,
                                                PT[0:NC, (j + g // 2) % 4, 512 * (g % 2):512 * (g % 2) + 512],
                                                PS[:, 4 + (hd // 4) % 2, :], hd < 8, hd >= 8)
                            ins.then_inc(S["pv_used"], 2)

                        for j in range(0, J, 2):
                            scores_x(j)
                            scores_x(j + 1)
                            if j:
                                values_x(j - 2)
                        values_x(J - 2)
                    else:
                        def turn_probs(u):
                            pe.wait_ge(S["pw_ready"], 8 * b + u + 1)
                            if u:
                                pe.wait_ge(S["p_ready"], ub + u)
                            for h in range(8):
                                ins = t_.transpose(PS[0:NC, M0 + h // 4, P * (h % 4):P * (h % 4) + P],
                                                   PW[:, h, :], ident[:, :])
                            ins.then_inc(S["pT_ready"], 1)

                        def values_t(u):
                            t, part = divmod(u, 2)
                            pe.wait_ge(S["p_ready"], ub + u + 1)
                            for hh in range(8):
                                hd = 8 * part + hh
                                i, jj = hh % 2, hh // 2
                                ins = values_in(l, b, 1, hd, None, 0,
                                                PT[0:NC, u % 2, 512 * i + P * jj:512 * i + P * jj + P],
                                                PS[:, 4 + (hd // 4) % 2, P * t:P * t + P],
                                                u == 0, u == 7)
                            ins.then_inc(S["pv_used"], 1)

                        ctx_scores(0)
                        for u in range(8):
                            if u < 7:
                                ctx_scores(u + 1)
                            turn_probs(u)
                            if u:
                                values_t(u - 1)
                        values_t(7)
                    output(l, b, 1, k)
                with pe.Fori(0, B) as b:
                    n, k = selfs(l, b), branch(l, b, 2)
                    turned_norm(k)
                    for m in range(4):
                        if l == 0:
                            if m >= 2:
                                pe.wait_ge(S["hid_ready"], 4 * n + m - 1)
                            mm(PS[:, 2 * (m % 2), :], w("f1_0", P * m, P), hT[:, :])
                            mm(PS[:, 2 * (m % 2) + 1, :], w("f1_0", P * (4 + m), P), hT[:, :]).then_inc(
                                S["ff_ready"], 1)
                        else:
                            mm(PS[:, m, :], w(f"f1_{l}", P * m, P), hT[:, :]).then_inc(S["ff_ready"], 1)
                    for m in range(4):
                        pe.wait_ge(S["hid_ready"], 4 * n + m + 1)
                        ins = mm(PS[:, M1, :], w(f"f2_{l}", C * m, C), HB[:, m, :], start=m == 0, stop=m == 3)
                    ins.then_inc(S["y_ps"], 1)
                    back_to_tokens(k)

        @block.vector
        def _(dve):
            v = nc.vector
            done = [0]

            def step(ins):
                done[0] += 1
                ins.then_inc(S["prep_dve"], 1)
                return done[0]

            def after(n):
                dve.wait_ge(S["prep_dve"], n)

            dve.wait_ge(S["loaded"], 16 * 10)
            stats = S["stats_ctx"]
            for b in range(B):
                v.bn_stats(cst[:, b, :], ctxK[:, b, :]).then_inc(stats, 1)
            for b in range(B):
                dve.wait_ge(stats, b + 1)
                v.bn_aggr(cmv[:, b, :], cst[:, b, :]).then_inc(stats, 1)
            dve.wait_ge(stats, 2 * B)
            assert step(v.tensor_scalar(cve[:, 0:B], cmv[:, :, 1], EPS[3], None, ALU.add)) == 1
            o, _ = CT["bq0"]
            step(v.tensor_scalar(bqs[:, :], COL[:, o:o + 6], QSCALE, None, ALU.mult))
            step(v.tensor_copy(identb[:, :], ident[:, :]))
            dve.wait_ge(S["ctx_rstd_ready"], 1)
            for b in range(B):
                step(v.tensor_scalar(ctxK[:, b, :], ctxK[:, b, :], cmv[:, b, 0:1], cve[:, B + b:B + b + 1],
                                     ALU.subtract, ALU.mult))
            assert done[0] == DVE_CTX
            step(v.tensor_copy(mkf[:, :], mrow8))
            after(done[0])
            m_any = step(v.tensor_reduce(mkany[:, :], mkf[:, :].rearrange("p (b n) -> p b n", b=B), AX.X, ALU.max))
            after(m_any)
            n = step(v.tensor_scalar(mkf[:, :], mkf[:, :], -MASKED, MASKED, ALU.mult, ALU.add))
            after(n)
            n = step(v.tensor_tensor(mkb[:, 0, :].rearrange("p (b n) -> p b n", b=B),
                                     mkf[0:8, :].rearrange("p (b n) -> p b n", b=B),
                                     mkany[0:8, :].unsqueeze(2).broadcast_to([8, B, NC]), ALU.mult))
            after(n)
            n = step(v.tensor_copy(mkf[:, :], mrow32[:, :]))
            after(n)
            n = step(v.tensor_scalar(mkf[:, :], mkf[:, :], 0.0, None, ALU.is_equal))
            after(n)
            n = step(v.tensor_reduce(poison[:, :], mkf[:, :].rearrange("p (b n) -> p b n", b=B), AX.X, ALU.min))
            v.tensor_scalar(mkb[:, 1, :], mkf[0:8, :], MASKED, None, ALU.mult).then_inc(S["prep_mask_rows"], 2)
            after(n)
            n = step(v.tensor_scalar(poison[:, :], poison[:, :], -1.0, 1.0, ALU.mult, ALU.add))
            after(n)
            n = step(v.reciprocal(poison[:, :], poison[:, :]))
            after(n)
            step(v.tensor_scalar(poison[:, :], poison[:, :], 0.0, None, ALU.mult))
            dve.wait_ge(S["prep_pe"], 1)
            o, _ = CT["adab"]
            nch = len(CHUNKS)
            n = step(v.tensor_tensor(mod[:, :, :], PS[:, M0, 0:B * nch].rearrange("p (n b) -> p n b", b=B),
                                     COL[:, o:o + nch].unsqueeze(2).broadcast_to([P, nch, B]), ALU.add))
            for i, l in enumerate((0, 2, 3)):
                for c in range(2):
                    q = PS[:, M0, B * nch + 2 * i + c:B * nch + 2 * i + c + 1]
                    n = step(v.tensor_scalar(cb[:, 2 * i + c:2 * i + c + 1], q,
                                             col(f"{'bco' if c else 'bo'}{l}"), None, ALU.add))
            after(n)
            where = {ch: i for i, ch in enumerate(CHUNKS)}

            def m(l, kind, br):
                return mod[:, where[(l, kind, br)], :]

            VV = VEC[:, :].rearrange("p (l b r f) -> p l b r f", l=NL, b=B, r=3)
            for l in range(NL):
                for br in range(3):
                    scale, shift, gate, gbias = (VV[:, l, :, br, f] for f in range(4))
                    has = (l, "sc", br) in where
                    if has:
                        step(v.tensor_scalar(scale, m(l, "sc", br), 1.0, col("w1", br) if l == 1 else 1.0,
                                             ALU.add, ALU.mult))
                        step(v.tensor_copy(shift, m(l, "sh", br)))
                        step(v.tensor_copy(gate, m(l, "g", br)))
                    else:
                        step(v.memset(gate, 1.0))
                        if l == 2:
                            step(v.tensor_copy(scale, col("w2", br).broadcast_to([P, B])))
                            step(v.tensor_copy(shift, col("lb2", br).broadcast_to([P, B])))
                        else:
                            step(v.memset(scale, 1.0))
                            step(v.memset(shift, 0.0))
                    bias = (col(f"b2_{l}") if br == 2 else
                            None if l == 1 else cb[:, 2 * (0, None, 1, 2)[l] + br:2 * (0, None, 1, 2)[l] + br + 1])
                    if bias is None:
                        step(v.memset(gbias, 0.0))
                    elif l == 2:
                        n = step(v.tensor_scalar(gbias, m(2, "t", br), bias, None, ALU.add))
                        if br == 1:
                            after(n)
                            step(v.tensor_tensor(gbias, gbias, poison[:, :], ALU.add))
                    elif has:
                        step(v.tensor_scalar(gbias, m(l, "g", br), bias, None, ALU.mult))
                    else:
                        step(v.tensor_copy(gbias, bias.broadcast_to([P, B])))
            kstep = S["prep_kparts"]
            for l in range(NL):
                dve.wait_ge(S["prep_act"], 2 + l)
                if l:
                    dve.wait_ge(S["prep_stacked"], 16 * 12 * l)
                if l == 1:
                    k3 = kc32[:, :].rearrange("p (b n) -> p b n", b=B)
                    after(step(v.tensor_tensor(k3, k3, mkany[:, :].unsqueeze(2).broadcast_to([P, B, NC]), ALU.mult)))
                v.tensor_copy(kcp[:, 0, :], kc32[:, :]).then_inc(kstep, 1)
                dve.wait_ge(kstep, 4 * l + 1)
                v.tensor_tensor(kc32[:, :], kc32[:, :], kcp[:, 0, :], ALU.subtract).then_inc(kstep, 1)
                dve.wait_ge(kstep, 4 * l + 2)
                v.tensor_copy(kcp[:, 1, :], kc32[:, :]).then_inc(kstep, 1)
                dve.wait_ge(kstep, 4 * l + 3)
                v.tensor_tensor(kcp[:, 2, :], kc32[:, :], kcp[:, 1, :], ALU.subtract).then_inc(kstep, 1)
                dve.wait_ge(S["prep_pe"], PE_V[l])
                n = step(v.tensor_copy(VC[:, l, :, :], PS[0:NC, 4 + l % 2, :].rearrange("p (b n) -> p b n", b=B)))
                if l < 2:
                    assert n == DVE_VC[l], (l, n)
            assert n == PREP_VC, n
            n = step(v.tensor_copy(MB[:, :, :], ms8))
            after(n)
            n = step(v.tensor_reduce(rany[:, :], MB[:, :, :], AX.X, ALU.max))
            after(n)
            n = step(v.tensor_scalar(MB[:, :, :], MB[:, :, :], -MASKED, MASKED, ALU.mult, ALU.add))
            after(n)
            for t in range(T):
                step(v.tensor_scalar(MB[:, t, :], MB[:, t, :], rany[:, t:t + 1], None, ALU.mult))
                n = step(v.tensor_scalar(diag[:, t, :], ident[:, :], rany[:, t:t + 1], None, ALU.mult))
            assert n == DVE_MASK, n
            dve.wait_ge(S["prep_pe"], PE_V[3] + 2)
            for k2, src in enumerate((M0B, M1B)):
                step(v.tensor_copy(MBT[:, 2 * k2:2 * k2 + 2, :], src.rearrange("p (a n) -> p a n", a=2)))
            for f in range(2):
                n = step(v.scalar_tensor_tensor(ROPEQ[:, f, :], PS[:, 4, :], QSCALE, ROPE[:, f, :], ALU.mult, ALU.mult))
            after(n)
            dve.wait_ge(S["x_loaded"], 16 * B)
            dve.wait_ge(S["base_consts"], 9)

            def norm(l, b, br):
                k = branch(l, b, br)
                X = xr if l == 0 else xs
                v.tensor_copy(V4[:, :], VEC[:, bass.ds(12 * b + 48 * l + 4 * br, 4)]).then_inc(S["stats_done"], 1)
                for t in range(T):
                    v.bn_stats(st[:, t, :], X[:, bass.ds(T * b + t, 1), :].rearrange("p a c -> p (a c)")).then_inc(
                        S["stats_done"], 1)
                for t in range(T):
                    held(dve, S["stats_done"], 5 * k + t + 2)
                    v.bn_aggr(mv[:, t, :], st[:, t, :]).then_inc(S["aggr_done"], 1)
                dve.wait_ge(S["aggr_done"], 4 * k + 4)
                v.tensor_scalar(ve[:, :], mv[:, :, 1], EPS[l], None, ALU.add).then_inc(S["ve_ready"], 1)
                dve.wait_ge(S["rstd_ready"], k + 1)
                for t in range(T):
                    v.tensor_scalar(XN[:, t, :], X[:, bass.ds(T * b + t, 1), :].rearrange("p a c -> p (a c)"),
                                    mv[:, t, 0:1], rstd[:, t:t + 1], ALU.subtract, ALU.mult).then_inc(
                        S["xn_ready"], 1)

            def residual(l, b, br):
                k = branch(l, b, br)
                X = xr if l == 0 else xs
                xb = X[:, bass.ds(T * b, T), :]
                dve.wait_ge(S["yb_ready"], k + 1)
                v.tensor_tensor(xb, PS[:, M0, :].rearrange("p (t c) -> p t c", t=T), xb, ALU.add).then_inc(
                    S["x_done"], 1)
                dve.wait_ge(S["x_done"], k + 1)

            def query_parts(a):
                q32, qp, part = qk[:, 0, :], qkp[:, 0, :, :], S["q_part"]
                dve.wait_ge(S["q_ready"], a + 1)
                v.tensor_copy(qp[:, 0, :], q32).then_inc(part, 1)
                dve.wait_ge(part, 4 * a + 1)
                v.tensor_tensor(q32, q32, qp[:, 0, :], ALU.subtract).then_inc(part, 1)
                dve.wait_ge(part, 4 * a + 2)
                v.tensor_copy(qp[:, 1, :], q32).then_inc(part, 1)
                dve.wait_ge(part, 4 * a + 3)
                v.tensor_tensor(qp[:, 2, :], q32, qp[:, 1, :], ALU.subtract).then_inc(part, 1)

            def max_parts(l, b, c):
                n = maxes(l, b, c)
                step_ = S["m_step"]
                src = mneg[:, :, :].rearrange("p t (j i) -> p t i j", i=2)
                dve.wait_ge(S["sA_used"], reduced(l, b, c) + (4 if l == 0 else 8 if c else 32))
                v.tensor_copy(m3[:, :, :, 0, :], src).then_inc(step_, 1)
                dve.wait_ge(step_, 4 * n + 1)
                v.tensor_tensor(src, src, m3[:, :, :, 0, :], ALU.subtract).then_inc(step_, 1)
                dve.wait_ge(step_, 4 * n + 2)
                v.tensor_copy(m3[:, :, :, 1, :], src).then_inc(step_, 1)
                dve.wait_ge(step_, 4 * n + 3)
                v.tensor_tensor(m3[:, :, :, 2, :], src, m3[:, :, :, 1, :], ALU.subtract).then_inc(step_, 1)
                dve.wait_ge(S["mT_ps"], n + 1)
                v.tensor_copy(mT[:, :], M0B[0:48, 0:L]).then_inc(S["mT_ready"], 1)

            def normalise(a):
                dve.wait_ge(S["T_ready"], a + 1)
                rows = PS[:, 4:6, :].rearrange("p k (h e) -> p (k h) e", e=16)
                v.reciprocal(rec[:, :].unsqueeze(2), rows[:, :, 8:9]).then_inc(S["rec_ready"], 1)
                dve.wait_ge(S["rec_ready"], a + 1)
                v.tensor_tensor(ON[:, :, :].rearrange("p t (h d) -> p (t h) d", d=HD), rows[:, :, 0:8],
                                rec[:, :].unsqueeze(2).broadcast_to([P, T * H, HD]), ALU.mult).then_inc(
                    S["on_ready"], 1)

            for l in range(NL):
                if l == 1:
                    dve.wait_ge(S["unrolled"], 16 * (1 + 2 * B))
                with dve.Fori(0, B) as b:
                    n = selfs(l, b)
                    norm(l, b, 0)
                    if l == 1:
                        dve.wait_ge(S["qk_ready"], 2 * n + 1)
                        for which, tab in ((0, ROPEQ), (1, ROPE)):
                            o = 4 * b + 2 * which
                            v.tensor_tensor(ra[:, :], PS[:, which, :], tab[:, 0, :], ALU.mult).then_inc(
                                S["rope_step"], 1)
                            v.tensor_tensor(rb[:, :], PS[:, 2 + which, :], tab[:, 1, :], ALU.mult).then_inc(
                                S["rope_step"], 1)
                            dve.wait_ge(S["rope_step"], o + 2)
                            v.tensor_tensor(qk[:, which, :], ra[:, :], rb[:, :], ALU.add).then_inc(
                                S["q_ready" if which == 0 else "k_ready"], 1)
                            dve.wait_ge(S["q_ready" if which == 0 else "k_ready"],
                                        attn(1, b, 0) + 1 if which == 0 else n + 1)
                    query_parts(attn(l, b, 0))
                    dve.wait_ge(S["v_ready"], n + 1)
                    for s in range(2):
                        src = PS[:, M1, :].rearrange("p (t n) -> p t n", t=T)[:, :, 64 * s:64 * s + 64]
                        dst = VA[:, :, 256 * s:256 * s + 256].rearrange("p t (h e) -> p t h e", e=32)
                        v.tensor_copy(dst[:, :, :, 16 * s:16 * s + 8],
                                      src.rearrange("p t (h d) -> p t h d", d=8)).then_inc(S["va_ready"], 1)
                    ua = units_a(l, b, 0)
                    if l == 0:
                        for t in range(T):
                            dve.wait_ge(S["sA_ready"], ua + t + 1)
                            bk = 2 * (t % 2)
                            v.tensor_reduce(mneg[:, t, :].rearrange("p (j i) -> p i j", i=2),
                                            PS[:, bk:bk + 2, :].rearrange("p i (j n) -> p i j n", n=WIN), AX.X,
                                            ALU.max, negate=True).then_inc(S["sA_used"], 1)
                    else:
                        for u in range(32):
                            t, j = divmod(u, J)
                            dve.wait_ge(S["sA_ready"], ua + u + 1)
                            bk = 2 * (u % 2)
                            v.tensor_reduce(mneg[:, t, 2 * j:2 * j + 2], PS[:, bk:bk + 2, :], AX.X, ALU.max,
                                            negate=True).then_inc(S["sA_used"], 1)
                    max_parts(l, b, 0)
                    normalise(attn(l, b, 0))
                    residual(l, b, 0)
                    norm(l, b, 1)
                    query_parts(attn(l, b, 1))
                    ua = units_a(l, b, 1)
                    if l:
                        for u in range(8):
                            t, part = divmod(u, 2)
                            dve.wait_ge(S["sA_ready"], ua + u + 1)
                            bk = 2 * (u % 2)
                            v.tensor_reduce(mneg[:, t, 8 * part:8 * part + 8].rearrange("p (j i) -> p i j", i=2),
                                            PS[:, bk:bk + 2, 0:4 * NC].rearrange("p i (j n) -> p i j n", n=NC),
                                            AX.X, ALU.max, negate=True).then_inc(S["sA_used"], 1)
                        max_parts(l, b, 1)
                    else:
                        top = S["top_step"]
                        for u in range(8):
                            o = 31 * (8 * b + u)
                            sl = u % 2
                            held(dve, S["sx_ready"], 8 * b + u + 1)
                            for h in range(8):
                                v.max(v8[:, 0, h, :], SX[:, sl, h, :]).then_inc(top, 1)
                            dve.wait_ge(top, o + 8)
                            if u >= 2:
                                dve.wait_ge(S["e_ready"], 8 * b + u - 1)
                            v.tensor_scalar(nm8[:, sl, :], v8[:, 0, :, 0], -1.0, None, ALU.mult).then_inc(
                                S["negm_ready"], 1)
                            for h in range(8):
                                v.match_replace(W1[:, h, :], v8[:, 0, h, :], SX[:, sl, h, :], TAKEN).then_inc(top, 1)
                            for h in range(8):
                                held(dve, top, o + 9 + h)
                                v.max(v8[:, 1, h, :], W1[:, h, :]).then_inc(top, 1)
                            if u >= 2:
                                dve.wait_ge(S["pick_ready"], 8 * b + u - 1)
                            for h in range(8):
                                held(dve, top, o + 17 + h)
                                v.match_replace(W2[:, sl, h, :], v8[:, 1, h, :], W1[:, h, :], TAKEN).then_inc(
                                    S["w2_ready"] if h == 7 else top, 1)
                            held(dve, S["w2_ready"], 8 * b + u + 1)
                    normalise(attn(l, b, 1))
                    residual(l, b, 1)
                with dve.Fori(0, B) as b:
                    n = selfs(l, b)
                    norm(l, b, 2)
                    if l == 0:
                        for q in range(4):
                            dve.wait_ge(S["gate_ready"], 4 * n + q + 1)
                            v.scalar_tensor_tensor(HB[:, q, :], PS[:, 2 * (q % 2) + 1, :], col("b1_0", 4 + q),
                                                   HB[:, q, :], ALU.add, ALU.mult).then_inc(S["hid_ready"], 1)
                    residual(l, b, 2)


PE_CTXT = 2
PE_K = [3, 5, 7, 9]
PE_V = [4, 6, 8, 10]
DVE_CTX = 7
DVE_VC = [74, 76]
PREP_VC = 78
DVE_MASK = 89
BQ = {0: 0, 2: 2, 3: 4}


def qk_order():
    return np.array([8 * (2 * j + i) + d for i in range(2) for d in range(HD) for j in range(J)])


def out_order():
    return np.array([8 * (8 * s + hh) + d for hh in range(8) for s in range(2) for d in range(HD)])


def pack(inputs):
    g = {k: np.asarray(v) for k, v in inputs.items()}
    qo, oo = qk_order(), out_order()
    rot = np.array([c // HD * HD + (c % HD + HD // 2) % HD for c in range(C)])
    W, V = {}, {}
    L0, L1, L2, L3 = ("L%d_xcond_" % l for l in range(4))
    for l, (pre, wqkv) in enumerate(((L0, "w_qkv"), (L1, "qkv_W"), (None, None), (L3, "W_qkv"))):
        if pre:
            q = g[pre + wqkv]
            W[f"q{l}"], W[f"k{l}"], W[f"v{l}"] = q[:, :C][:, qo], q[:, C:2 * C][:, qo], q[:, 2 * C:]
            if l == 1:
                W["qrot1"], W["krot1"] = q[:, :C][:, rot][:, qo], q[:, C:2 * C][:, rot][:, qo]
    W["q2"], W["k2"], W["v2"] = g[L2 + "sa_wq"][:, qo], g[L2 + "sa_wk"][:, qo], g[L2 + "sa_wv"]
    for l, n in enumerate((L0 + "w_so", L1 + "attn_out_W", L2 + "sa_wo", L3 + "W_proj")):
        W[f"o{l}"] = g[n][oo]
    for l, n in enumerate((L0 + "w_co", L1 + "co_W", L2 + "ca_wo", L3 + "W_cproj")):
        W[f"co{l}"] = g[n][oo]
    for l, n in enumerate((L0 + "w_q", L1 + "cq_W", L2 + "ca_wq", L3 + "W_qc")):
        W[f"cq{l}"] = g[n][:, qo]
    W["ck0"], W["cv0"] = g[L0 + "w_kv"][:, :C][:, qo], g[L0 + "w_kv"][:, C:]
    W["ck1"], W["cv1"] = g[L1 + "ck_W"][:, qo], g[L1 + "cv_W"]
    W["ck2"], W["cv2"] = g[L2 + "ca_wk"][:, qo], g[L2 + "ca_wv"]
    W["ck3"], W["cv3"] = g[L3 + "W_kvc"][:, :C][:, qo], g[L3 + "W_kvc"][:, C:]
    ff = ((L0 + "w_m1", L0 + "w_m2"), (L1 + "mlp_W1", L1 + "mlp_W2"), (L2 + "w1", L2 + "w2"),
          (L3 + "W_mlp1", L3 + "W_mlp2"))
    for l, (a, b) in enumerate(ff):
        W[f"f1_{l}"] = g[a]
        W[f"f2_{l}"] = g[b].reshape(4, P, C).transpose(1, 0, 2).reshape(P, 4 * C)
    ada = {0: (L0 + "w_ada", L0 + "b_ada"), 1: (L1 + "adaLN_W", L1 + "adaLN_b"), 2: (L2 + "tp_w", L2 + "tp_b"),
           3: (L3 + "W_mod", L3 + "b_mod")}
    place = {"sh": 0, "sc": 1, "g": 2}
    aw, ab = [], []
    for l, kind, br in CHUNKS:
        n = br if l == 2 else 3 * (br // 2 if l == 3 else br) + place[kind]
        aw.append(g[ada[l][0]][:, n * C:(n + 1) * C])
        ab.append(g[ada[l][1]][n * C:(n + 1) * C])
    V["cond"] = g["cond_1024"].T
    V["adab"] = np.stack(ab, 1)
    for l, n in ((0, L0 + "b_qkv"), (3, L3 + "b_qkv")):
        V[f"bq{l}"], V[f"bk{l}"], V[f"bv{l}"] = g[n][:C][qo], g[n][C:2 * C][qo], g[n][2 * C:][oo]
    V["bq2"], V["bk2"], V["bv2"] = g[L2 + "sa_bq"][qo], g[L2 + "sa_bk"][qo], g[L2 + "sa_bv"][oo]
    V["bo0"], V["bo2"], V["bo3"] = g[L0 + "b_so"], g[L2 + "sa_bo"], g[L3 + "b_proj"]
    V["bcq0"], V["bcq2"], V["bcq3"] = g[L0 + "b_q"][qo], g[L2 + "ca_bq"][qo], g[L3 + "b_qc"][qo]
    V["bck0"], V["bcv0"] = g[L0 + "b_kv"][:C][qo], g[L0 + "b_kv"][C:][oo]
    V["bck2"], V["bcv2"] = g[L2 + "ca_bk"][qo], g[L2 + "ca_bv"][oo]
    V["bck3"], V["bcv3"] = g[L3 + "b_kvc"][:C][qo], g[L3 + "b_kvc"][C:][oo]
    V["bco0"], V["bco2"], V["bco3"] = g[L0 + "b_co"], g[L2 + "ca_bo"], g[L3 + "b_cproj"]
    for l, (a, b) in enumerate(((L0 + "b_m1", L0 + "b_m2"), (L1 + "mlp_b1", L1 + "mlp_b2"), (L2 + "b1", L2 + "b2"),
                                (L3 + "b_mlp1", L3 + "b_mlp2"))):
        V[f"b1_{l}"], V[f"b2_{l}"] = g[a].reshape(-1, P).T, g[b]
    V["w1"] = np.stack([g[L1 + "norm1_w"], g[L1 + "normc_w"], g[L1 + "norm2_w"]], 1)
    V["w2"] = np.stack([g[L2 + "ln1_g"], g[L2 + "ln3_g"], g[L2 + "ln2_g"]], 1)
    V["lb2"] = np.stack([g[L2 + "ln1_b"], g[L2 + "ln3_b"], g[L2 + "ln2_b"]], 1)
    out = {}
    for name, table, parts in (("wpack", weight_table(), W), ("cols", column_table(), V)):
        at, width = table
        out[name] = np.zeros((P, width), np.float32)
        for n, (o, k) in at.items():
            out[name][:, o:o + k] = parts[n].reshape(P, k)
    out["ada_w"] = np.concatenate(aw, 1)
    out["x"] = np.roll(g["x"], -SHIFT, axis=1)
    out["ctx_t"] = g["ctx_1024"].transpose(2, 0, 1).reshape(C, B * NC)
    out["ctx_tok"] = g["ctx_1024"].transpose(1, 0, 2)
    out["mask_self"] = g["mask_SxS_bk0"].view(np.int32)
    out["mask1"] = g["mask_BxS2_bf1"].reshape(B * NC).view(np.int32)
    out["mask2"] = g["mask_BxS2_ik0"].reshape(B * NC)
    out["ident_in"] = np.eye(P, dtype=np.float32)
    half = L // 2
    inv = 1.0 / 10000.0 ** (np.arange(0, HD, 2, dtype=np.float32) / HD)
    freqs = np.outer(np.arange(half, dtype=np.float32), inv)
    emb = np.concatenate([freqs, freqs], axis=-1)
    cos, sin = np.cos(emb).astype(np.float32), np.sin(emb).astype(np.float32)
    d = qo % HD
    sign = np.where(d < HD // 2, -1.0, 1.0).astype(np.float32)[:, None]
    out["rope"] = np.stack([np.tile(cos.T[d], (1, 2)), sign * np.tile(sin.T[d], (1, 2))], 1)
    rows = np.full((4, J * L), 0x3F80, np.uint16)
    rows[0] = 0
    out["const_rows"] = rows
    return {k: np.ascontiguousarray(v) for k, v in out.items()}


_INS = ["x", "wpack", "ada_w", "cols", "ctx_t", "ctx_tok", "mask_self", "mask1", "mask2", "ident_in", "rope", "const_rows"]


def kernel(**inputs):
    import concourse.bacc as bacc
    from concourse.bass_utils import run_bass_kernel_spmd

    nc = bacc.Bacc("TRN2", target_bir_lowering=False, num_devices=1)
    laid = pack(inputs)
    arrays, args = {}, []
    for name in _INS:
        a = laid[name]
        arrays[f"in_{name}"] = a
        args.append(nc.dram_tensor(f"in_{name}", a.shape, mybir.dt.from_np(a.dtype), kind="ExternalInput").ap())
    args.append(nc.dram_tensor("out_x", (B, L, C), F32, kind="ExternalOutput").ap())
    build(nc, *args)
    r = run_bass_kernel_spmd(nc, [arrays], core_ids=[0])
    return r.results[0]["out_x"]
```

```python
from contextlib import ExitStack

import numpy as np
import concourse.bass as bass
import concourse.mybir as mybir

F32 = mybir.dt.float32
BF16 = mybir.dt.bfloat16
U8 = mybir.dt.uint8
I32 = mybir.dt.int32
ALU = mybir.AluOpType
ACT = mybir.ActivationFunctionType
AX = mybir.AxisListType

P = 128
B, L, C, H, HD = 4, 512, 128, 16, 8
T = L // P
NC = 77
WIN, SHIFT, TOPK = 64, 32, 16
HID = 512
NL = 4
J = H // 2
QUERY_PART = (0, 0, 0, 1, 1, 2)
KEY_PART = (0, 1, 2, 0, 1, 0)
ROWS = 8 * len(QUERY_PART)
ROW_MASK, ROW_MAX = ROWS, ROWS + 1
ROWS_FULL = ROWS + 4
QSCALE = float(1.0 / np.sqrt(np.float32(HD)))
MASKED = -1.0e30
TAKEN = -3.0e38
EPS = (1e-6, 1e-5, 1e-5, 1e-6)
FF_TILES = (8, 4, 4, 4)

CHUNKS = ([(l, kind, br) for l in (0, 1) for br in range(3) for kind in ("sh", "sc", "g")]
          + [(2, "t", br) for br in range(3)]
          + [(3, kind, br) for br in (0, 2) for kind in ("sh", "sc", "g")])


def weight_table():
    names = []
    for l in range(NL):
        names += [(f"q{l}", C), (f"k{l}", C), (f"v{l}", C), (f"o{l}", C)]
        if l == 1:
            names += [("qrot1", C), ("krot1", C)]
        names += [(f"cq{l}", C), (f"ck{l}", C), (f"cv{l}", C), (f"co{l}", C)]
        names += [(f"f1_{l}", FF_TILES[l] * P), (f"f2_{l}", HID)]
    at, off = {}, 0
    for n, w in names:
        at[n] = (off, w)
        off += w
    return at, off


def column_table():
    names = [("cond", B), ("adab", len(CHUNKS))]
    for l in (0, 2, 3):
        names += [(f"{n}{l}", 1) for n in ("bq", "bcq")]
    for l in (0, 2, 3):
        names += [(f"{n}{l}", 1) for n in ("bk", "bv", "bo", "bck", "bcv", "bco")]
    for l in range(NL):
        names += [(f"b1_{l}", FF_TILES[l]), (f"b2_{l}", 1)]
    names += [("w1", 3), ("w2", 3), ("lb2", 3)]
    at, off = {}, 0
    for n, w in names:
        at[n] = (off, w)
        off += w
    return at, off


def build(nc, x, wpack, ada_w, cols, ctx_t, ctx_tok, mask_self, mask1, mask2, ident_in, rope, const_rows, out):
    const_rows = const_rows.bitcast(BF16)
    WT, NW = weight_table()
    CT, NCOL = column_table()
    ctx = ExitStack()
    with ctx:
        def sb(name, shape, dt=F32):
            return ctx.enter_context(nc.sbuf_tensor(name, shape, dt))

        def sem(name):
            return ctx.enter_context(nc.semaphore(name))

        W = sb("weights", [P, NW])
        COL = sb("columns", [P, NCOL])
        ident = sb("ident", [P, P])
        identb = sb("identb", [P, P], BF16)
        xs = sb("x_state", [P, B * T, C])
        room = sb("room", [P, 9216])
        taken = [0]

        def early(n, dt=F32):
            width = n if dt != BF16 else (n + 1) // 2
            a = room[:, taken[0]:taken[0] + width]
            taken[0] += width
            assert taken[0] <= 9216
            return a if dt == F32 else a.bitcast(dt)

        xr = early(B * T * C).rearrange("p (t c) -> p t c", c=C)
        ctxT = early(B * NC)
        ctxLT = early(B * NC)
        ctxK = early(B * C)[0:NC].rearrange("p (b c) -> p b c", c=C)
        kc32 = early(B * NC)
        kcp = early(3 * B * NC, BF16).rearrange("p (r n) -> p r n", r=3)
        mword = early(B * NC // 4, I32)
        mrow8 = mword.bitcast(U8)
        mrow32 = early(B * NC, I32)
        mkf = early(B * NC)
        ms32 = early(T * L // 4, I32).rearrange("p (t n) -> p t n", t=T)
        ms8 = ms32.bitcast(U8)
        diag = early(T * P).rearrange("p (t n) -> p t n", t=T)
        ones = early(P)
        SX = early(16 * NC).rearrange("p (a h n) -> p a h n", a=2, h=8)
        W1 = early(8 * NC).rearrange("p (h n) -> p h n", h=8)
        W2 = early(16 * NC).rearrange("p (a h n) -> p a h n", a=2, h=8)
        KX = early(J * NC, BF16).rearrange("p (j n) -> p j n", j=J)
        taken[0] = 0
        QS2 = early(J * L, BF16).rearrange("p (j n) -> p j n", j=J)
        KS2 = early(J * L, BF16).rearrange("p (j n) -> p j n", j=J)
        QX = early(J * L, BF16).rearrange("p (j n) -> p j n", j=J)
        VA2 = early(T * H * 32).rearrange("p (t n) -> p t n", t=T)
        qxp = early(3 * L, BF16).rearrange("p (r n) -> p r n", r=3)
        mTx = early(L, BF16)[0:48]
        scond = sb("silu_cond", [P, B])
        mod = sb("mod", [P, len(CHUNKS), B])
        cb = sb("out_bias", [P, 6])
        VEC = sb("vectors", [P, NL * B * 12])
        bqs = sb("q_bias_scaled", [P, 6])
        KC = sb("ctx_keys_stacked", [P, NL, J, B * NC], BF16)
        VC = sb("ctx_values", [NC, NL, B, C])
        mkany = sb("ctx_any", [P, B])
        poison = sb("ctx_none", [P, B])
        mkb = sb("ctx_mask_bias", [8, 2, B * NC], BF16)
        MB = sb("self_bias", [P, T, L], BF16)
        MBT = sb("self_bias_t", [P, T, L], BF16)
        rany = sb("row_any", [P, T])
        ROPE = sb("rope", [P, 2, L])
        ROPEQ = sb("rope_q", [P, 2, L])
        cst = sb("ctx_stats", [NC, B, 6])
        cmv = sb("ctx_mv", [NC, B, 2])
        cve = sb("ctx_ve", [NC, 2 * B])
        V4 = sb("vec4", [P, 4])
        st = sb("stats", [P, T, 6])
        mv = sb("mv", [P, T, 2])
        ve = sb("ve", [P, T])
        rstd = sb("rstd", [P, T])
        mhalf = sb("minus_half", [P, T])
        XN = sb("x_normed", [P, T, C])
        hT = sb("h_channels", [P, L])
        qk = sb("qk", [P, 2, L])
        qkp = sb("qk_parts", [P, 2, 3, L], BF16)
        QS = sb("q_stacked", [P, J, L], BF16)
        KS = sb("k_stacked", [P, J, L], BF16)
        VA = sb("values", [P, T, H * 32])
        VX = sb("ctx_values_now", [NC, H * 32])
        mneg = sb("minus_max", [P, T, H])
        m3 = sb("max_parts", [P, T, 2, 3, J], BF16)
        mT = sb("max_rows", [48, L], BF16)
        PT = sb("probs", [P, 4, 2 * L])
        ADA = PT[:, :, :].rearrange("p a n -> p (a n)")
        U = sb("out_rows", [P, 2, L])
        rec = sb("recip", [P, T * H])
        ON = sb("out_normed", [P, T, C])
        OT = sb("out_channels", [P, L])
        YT = sb("y_channels", [P, L])
        HB = sb("hidden", [P, 4, L])
        HBF = HB[:, :, :].rearrange("p a n -> p (a n)")
        E = HBF[:, 0:16 * NC].rearrange("p (a h n) -> p a h n", a=2, h=8)
        PW = HBF[:, 16 * NC:24 * NC].rearrange("p (h n) -> p h n", h=8)
        v8 = sb("top8", [P, 2, 8, 8])
        nm8 = sb("topk_minus_max", [P, 2, 8])

        QSs, KSs, VAs = (QS, QS2), (KS, KS2), (VA, VA2)
        RA, RB = HB[:, 0, :], HB[:, 1, :]
        PX = HB
        GP = PT[:, :, :].rearrange("p a (g n) -> p (a g) n", g=2)
        XN1, XN2 = XN, ON
        QX32 = XN1[:, :, :].rearrange("p t c -> p (t c)")
        H1, H2, HF = hT, OT, YT
        U2 = sb("cross_out_rows", [P, 2, L])
        mnegx = sb("cross_minus_max", [P, T, H])
        m3x = sb("cross_max_parts", [P, T, 2, 3, J], BF16)
        st2, mv2, ve2, rstd2 = (sb("stats2", [P, T, 6]), sb("mv2", [P, T, 2]), sb("ve2", [P, T]), sb("rstd2", [P, T]))
        rec2 = sb("recip2", [P, T * H])

        PS = ctx.enter_context(nc.psum_tensor("PS", [P, 8, 512], F32))
        M0, M1 = 6, 7
        M0B = PS[:, M0, :].bitcast(BF16)
        M1B = PS[:, M1, :].bitcast(BF16)

        names = """loaded x_loaded const_rows_in base_consts prep_act prep_pe prep_dve prep_kparts prep_stacked
            prep_mask_rows unrolled stats_done aggr_done ve_ready rstd_ready xn_ready xnT_ready hT_ready
            qk_ready v_ready qk_evac rope_step q_ready k_ready q_part k_part va_ready q_stacked k_stacked kvx_ready
            sA_ready sA_used m_step mT_ps mT_ready m_stacked sB_ready p_ready pv_used u_ready
            T_ready rec_ready on_ready onT_ready oT_ready y_ps y_ready yb_ready x_done
            silu_ready ctx_rstd_ready stats_ctx ff_ready gate_ready hid_ready sx_ready top_step w2_ready negm_ready e_ready pick_ready pw_ready pT_ready
            stored waits_held
            late_consts late_rows b_ready b_exp b_pv b_u a_ready a_used a_m a_mTps a_mT a_rows f_qkps f_rope f_q f_k f_qpart f_kpart
            k_in k_in0 q_in q_in0 v_ps v_in x_in0
            c1_T c1_rec c1_on c1_onT c1_oT c1_yps c1_y c1_yb c1_x c1_st c1_ag c1_ve c1_rs c1_xn c1_xnT c1_h
            x_qps x_q x_part x_in xa_ready xa_used xa_m xa_mTps xa_mT xa_rows
            xb_kv xb_ready xb_exp xb_pv xb_u
            c2_T c2_rec c2_on c2_onT c2_oT c2_yps c2_y c2_yb c2_x c2_st c2_ag c2_ve c2_rs c2_xn c2_xnT c2_h
            ff_ps ff_hid""".split()
        S = {n: sem(n) for n in names}

        def w(name, a=0, n=None):
            o, width = WT[name]
            return W[:, o + a:o + (width if n is None else a + n)]

        def col(name, a=0):
            o, _ = CT[name]
            return COL[:, o + a:o + a + 1]

        def attn(l, b, c):
            return 8 * l + c + 2 * b

        def branch(l, b, br):
            return 12 * l + (8 + b if br == 2 else 2 * b + br)

        def selfs(l, b):
            return 4 * l + b

        def counted(n):
            def f(l, b, c):
                return 4 * sum(sum(n[m]) for m in range(l)) + (n[l][0] if c else 0) + b * sum(n[l])
            return f

        units_a = counted([(4, 8)] + [(32, 8)] * 3)
        units_b = counted([(4, 8)] + [(32, 8)] * 3)
        reduced = counted([(4, 0)] + [(32, 8)] * 3)
        scored = counted([(4, 0)] + [(32, 8)] * 3)
        maxes = counted([(1, 0)] + [(1, 1)] * 3)

        def held(eng, semaphore, value):
            eng.wait_ge(semaphore, value)
            eng.sem_inc(S["waits_held"], 1)

        N = (NL - 1) * B
        SLOTS = range(-2, N + 2)
        POINTS = 64
        QUADS = (0, 2, 1, 3)
        BANK_B, BANK_A, BANK_V, BANK_1, BANK_2 = (0, 1), (2, 3), 4, 5, (6, 7)

        LATE = 6

        def item(n):
            return (1 + n // B, n % B) if 0 <= n < N else (None, None)

        def maxima_at(p):
            return max(0, min(64, (p - A_FROM) * 64 // (A_TO - A_FROM)))

        def unit_a(a):
            return a // 32, a // 8 % 4, a % 8

        def vec(l, b, br, f):
            o = 12 * (B * l + b) + 4 * br + f
            return VEC[:, o:o + 1]

        def order2(which, n):
            if which == "ff":
                return n + min(n + 4, N)
            return n + max(0, n - 3)

        block = ctx.enter_context(nc.Block())

        @block.sync
        def _(sp):
            for dst, src in ((COL[:, :], cols), (ident[:, :], ident_in), (ctxT[:, :], ctx_t),
                             (W[:, :], wpack), (ADA[:, 0:len(CHUNKS) * C], ada_w),
                             (ctxK[:, :, :], ctx_tok), (ms32[:, :, :], mask_self.rearrange("(t p) k -> p t k", p=P)),
                             (mword[:, :], mask1.rearrange("(a n) -> a n", a=1).broadcast_to([P, B * NC // 4])),
                             (mrow32[:, :], mask2.rearrange("(a n) -> a n", a=1).broadcast_to([P, B * NC])),
                             (ROPE[:, :, :], rope)):
                sp.dma_start(dst, src).then_inc(S["loaded"], 16)
            for b in range(B):
                sp.dma_start(xr[:, T * b:T * b + T, :],
                             x[b].rearrange("(t p) c -> p t c", p=P)).then_inc(S["x_loaded"], 16)
            sp.wait_ge(S["base_consts"], 1)
            for i in range(2):
                r = 64 * i + ROW_MASK
                sp.dma_start(KS[r:r + 4, :, :], const_rows.rearrange("r (j n) -> r j n", j=J)).then_inc(
                    S["const_rows_in"], 16)
                for l in range(NL):
                    sp.dma_start(KC[r:r + 4, l, :, :],
                                 const_rows[:, 0:J * B * NC].rearrange("r (j n) -> r j n", j=J)).then_inc(
                        S["const_rows_in"], 16)
            for l in range(NL):
                for r, part in enumerate(KEY_PART):
                    sp.wait_ge(S["prep_kparts"], 4 * l + (1, 3, 4)[part])
                    for i in range(2):
                        sp.dma_start(KC[64 * i + 8 * r:64 * i + 8 * r + 8, l, :, :],
                                     kcp[64 * i:64 * i + 64, part, :]).then_inc(S["prep_stacked"], 16)
            sp.wait_ge(S["const_rows_in"], 16 * 2 * (1 + NL))
            sp.wait_ge(S["prep_mask_rows"], 2)
            for i in range(2):
                r = 64 * i + ROW_MASK
                for n in range(2):
                    sp.dma_start(KC[r:r + 1, 1 + n, :, :], mkb[:, n, :]).then_inc(S["prep_stacked"], 16)

            def stack(dst, which, map_, ready, base, done):
                for part in range(3):
                    sp.wait_ge(ready, base + (1, 3, 4)[part])
                    for r in range(len(map_)):
                        if map_[r] == part:
                            for i in range(2):
                                sp.dma_start(dst[64 * i + 8 * r:64 * i + 8 * r + 8, :, :],
                                             qkp[64 * i:64 * i + 64, which, part, :]).then_inc(done, 16)

            for l in (0,):
                with sp.Fori(0, B) as b:
                    for c in range(2):
                        a = attn(l, b, c)
                        if c == 0:
                            stack(KS, 1, KEY_PART, S["k_part"], 4 * selfs(l, b), S["k_stacked"])
                        stack(QS, 0, QUERY_PART, S["q_part"], 4 * a, S["q_stacked"])
                        if l == 0 and c == 1:
                            continue
                        sp.wait_ge(S["mT_ready"], maxes(l, b, c) + 1)
                        for i in range(2):
                            sp.dma_start(QS[64 * i + ROW_MAX:64 * i + ROW_MAX + 3, :, :],
                                         mT[24 * i:24 * i + 24, :]).then_inc(S["m_stacked"], 16)
                if l == 0:
                    sp.wait_ge(S["x_done"], 12)
                    q = P - SHIFT
                    sp.dma_start(xs[SHIFT:P, :, :], xr[0:q, :, :]).then_inc(S["unrolled"], 16)
                    for b in range(B):
                        sp.dma_start(xs[0:SHIFT, T * b + 1:T * b + T, :],
                                     xr[q:P, T * b:T * b + T - 1, :]).then_inc(S["unrolled"], 16)
                        sp.dma_start(xs[0:SHIFT, T * b:T * b + 1, :],
                                     xr[q:P, T * b + T - 1:T * b + T, :]).then_inc(S["unrolled"], 16)
            sp.wait_ge(S["late_consts"], 1)
            for i in range(2):
                r = 64 * i + ROW_MASK
                sp.dma_start(KS2[r:r + 4, :, :], const_rows.rearrange("r (j n) -> r j n", j=J)).then_inc(
                    S["late_rows"], 16)
            sp.wait_ge(S["late_rows"], 32)
            sp.wait_ge(S["late_consts"], LATE)

            def stack_parts(dst, src, map_, ready, n, done, i):
                for part in range(3):
                    if i == 0:
                        sp.wait_ge(ready, 4 * n + (1, 3, 4)[part])
                    for r in range(len(map_)):
                        if map_[r] == part:
                            sp.dma_start(dst[64 * i + 8 * r:64 * i + 8 * r + 8, :, :],
                                         src[64 * i:64 * i + 64, part, :]).then_inc(done[i], 16)

            def max_rows_in(dst, rows, ready, n, done):
                sp.wait_ge(ready, n + 1)
                for i in range(2):
                    sp.dma_start(dst[64 * i + ROW_MAX:64 * i + ROW_MAX + 3, :, :],
                                 rows[24 * i:24 * i + 24, :]).then_inc(done, 16)

            for s in SLOTS:
                if 0 <= s + 1 < N:
                    n = s + 1
                    if n >= 2:
                        sp.wait_ge(S["b_ready"], 64 * (n - 1))
                    for i in range(2):
                        stack_parts(QSs[n % 2], qkp[:, 0, :, :], QUERY_PART, S["f_qpart"], n, (S["q_in0"], S["q_in"]), i)
                        stack_parts(KSs[n % 2], qkp[:, 1, :, :], KEY_PART, S["f_kpart"], n, (S["k_in0"], S["k_in"]), i)
                if 0 <= s - 1 < N:
                    n = s - 1
                    if n:
                        sp.wait_ge(S["xb_ready"], 16 * n)
                    for i in range(2):
                        stack_parts(QX, qxp, QUERY_PART, S["x_part"], n, (S["x_in0"], S["x_in"]), i)
                    max_rows_in(QX, mTx, S["xa_mT"], n, S["xa_rows"])
                if 0 <= s + 1 < N:
                    max_rows_in(QSs[(s + 1) % 2], mT, S["a_mT"], s + 1, S["a_rows"])
                if B * (NL - 2) <= s - 2 < N:
                    b = s - 2 - B * (NL - 2)
                    sp.wait_ge(S["c2_x"], 2 * (s - 1))
                    sp.dma_start(out[b].rearrange("(t p) c -> p t c", p=P), xs[:, T * b:T * b + T, :]).then_inc(
                        S["stored"], 16)
            sp.wait_ge(S["stored"], 16 * B)

        @block.gpsimd
        def _(pool):
            g = nc.gpsimd
            g.memset(KS[:, :, :], 0.0).then_inc(S["base_consts"], 1)
            g.memset(mhalf[:, :], -0.5).then_inc(S["base_consts"], 1)
            g.memset(QS[:, :, :], 1.0).then_inc(S["base_consts"], 1)
            g.memset(VX[:, :], 0.0).then_inc(S["base_consts"], 1)
            g.memset(VA[:, :, :], 0.0).then_inc(S["base_consts"], 1)
            g.memset(ones[:, :], 1.0).then_inc(S["base_consts"], 1)
            pool.wait_ge(S["base_consts"], 5)
            for s in range(2):
                VAv = VA[:, :, 256 * s:256 * s + 256].rearrange("p t (h e) -> p t h e", e=32)
                g.memset(VAv[:, :, :, 16 * s + 8:16 * s + 16], 1.0).then_inc(S["base_consts"], 1)
                VXv = VX[:, 256 * s:256 * s + 256].rearrange("p (h e) -> p h e", e=32)
                g.memset(VXv[:, :, 16 * s + 8:16 * s + 16], 1.0).then_inc(S["base_consts"], 1)
            pool.wait_ge(S["prep_dve"], 1)
            pool.wait_ge(S["base_consts"], 2)
            g.tensor_tensor(cve[:, B:2 * B], cve[:, 0:B], mhalf[0:NC, :], ALU.pow).then_inc(S["ctx_rstd_ready"], 1)

            def inverse_deviation(k):
                pool.wait_ge(S["ve_ready"], k + 1)
                g.tensor_tensor(rstd[:, :], ve[:, :], mhalf[:, :], ALU.pow).then_inc(S["rstd_ready"], 1)

            for l in (0,):
                with pool.Fori(0, B) as b:
                    n = selfs(l, b)
                    inverse_deviation(branch(l, b, 0))
                    held(pool, S["k_ready"], n + 1)
                    k32, kp = qk[:, 1, :], qkp[:, 1, :, :]
                    g.tensor_copy(kp[:, 0, :], k32).then_inc(S["k_part"], 1)
                    pool.wait_ge(S["k_part"], 4 * n + 1)
                    g.tensor_tensor(k32, k32, kp[:, 0, :], ALU.subtract).then_inc(S["k_part"], 1)
                    held(pool, S["k_part"], 4 * n + 2)
                    g.tensor_copy(kp[:, 1, :], k32).then_inc(S["k_part"], 1)
                    pool.wait_ge(S["k_part"], 4 * n + 3)
                    g.tensor_tensor(kp[:, 2, :], k32, kp[:, 1, :], ALU.subtract).then_inc(S["k_part"], 1)
                    inverse_deviation(branch(l, b, 1))
                    if l == 0:
                        pool.wait_ge(S["prep_stacked"], 16 * (12 * NL + 4))
                        pool.wait_ge(S["prep_dve"], PREP_VC)
                        pool.wait_ge(S["base_consts"], 10)
                    pool.wait_ge(S["rstd_ready"], branch(l, b, 1) + 1)
                    for i in range(2):
                        r = slice(64 * i, 64 * i + ROWS_FULL)
                        if i:
                            held(pool, S["kvx_ready"], 4 * n + i)
                        g.tensor_copy(KX[r, :, :], KC[r, l, :, bass.ds(NC * b, NC)]).then_inc(S["kvx_ready"], 1)
                    for s in range(2):
                        held(pool, S["kvx_ready"], 4 * n + 2 + s)
                        src = VC[:, l, bass.ds(b, 1), 64 * s:64 * s + 64].rearrange("p a (h d) -> p (a h) d", d=HD)
                        dst = VX[:, 256 * s:256 * s + 256].rearrange("p (h e) -> p h e", e=32)
                        g.tensor_copy(dst[:, :, 16 * s:16 * s + 8], src).then_inc(S["kvx_ready"], 1)
                    if l == 0:
                        for u in range(8):
                            held(pool, S["w2_ready"], 8 * b + u + 1)
                            g.tensor_scalar(PW[:, :, :], W2[:, u % 2, :, :], TAKEN / 2, None, ALU.is_le).then_inc(
                                S["pick_ready"], 1)
                            pool.wait_ge(S["pick_ready"], 8 * b + u + 1)
                            pool.wait_ge(S["e_ready"], 8 * b + u + 1)
                            g.tensor_tensor(PW[:, :, :], PW[:, :, :], E[:, u % 2, :, :], ALU.mult).then_inc(
                                S["pw_ready"], 1)
                            held(pool, S["pT_ready"], 8 * b + u + 1)
                with pool.Fori(0, B) as b:
                    inverse_deviation(branch(l, b, 2))

            pool.wait_ge(S["unrolled"], 16 * (1 + 2 * B))
            g.memset(KS2, 0.0).then_inc(S["late_consts"], 1)
            g.memset(QS2, 1.0).then_inc(S["late_consts"], 1)
            g.memset(QX, 1.0).then_inc(S["late_consts"], 1)
            g.memset(VA2, 0.0).then_inc(S["late_consts"], 1)
            pool.wait_ge(S["late_consts"], 4)
            for s in range(2):
                VAv = VA2[:, :, 256 * s:256 * s + 256].rearrange("p t (h e) -> p t h e", e=32)
                g.memset(VAv[:, :, :, 16 * s + 8:16 * s + 16], 1.0).then_inc(S["late_consts"], 1)

            def deviation(ready, done, ve_, rstd_, k):
                pool.wait_ge(ready, k + 1)
                g.tensor_tensor(rstd_[:, :], ve_[:, :], mhalf[:, :], ALU.pow).then_inc(done, 1)

            for s in SLOTS:
                n = s - 2
                l, b = item(n)
                if l:
                    if n:
                        pool.wait_ge(S["xb_pv"], 4 * n)
                    for s2 in range(2):
                        src = VC[:, l, b, 64 * s2:64 * s2 + 64].rearrange("p (h d) -> p h d", d=HD)
                        dst = VX[:, 256 * s2:256 * s2 + 256].rearrange("p (h e) -> p h e", e=32)
                        if s2:
                            pool.wait_ge(S["xb_kv"], 2 * n + 1)
                        g.tensor_copy(dst[:, :, 16 * s2:16 * s2 + 8], src).then_inc(S["xb_kv"], 1)
                    pool.wait_ge(S["xb_kv"], 2 * n + 2)
                if item(s - 1)[0]:
                    deviation(S["c1_ve"], S["c1_rs"], ve, rstd, s - 1)
                if l:
                    deviation(S["c2_ve"], S["c2_rs"], ve2, rstd2, order2("ff", n))
                n = s + 2
                if item(n)[0]:
                    deviation(S["c2_ve"], S["c2_rs"], ve2, rstd2, order2("front", n))
                    pool.wait_ge(S["f_k"], n + 1)
                    if n:
                        pool.wait_ge(S["k_in"], 96 * n)
                    k32, kp = qk[:, 1, :], qkp[:, 1, :, :]
                    g.tensor_copy(kp[:, 0, :], k32).then_inc(S["f_kpart"], 1)
                    pool.wait_ge(S["f_kpart"], 4 * n + 1)
                    g.tensor_tensor(k32, k32, kp[:, 0, :], ALU.subtract).then_inc(S["f_kpart"], 1)
                    pool.wait_ge(S["f_kpart"], 4 * n + 2)
                    g.tensor_copy(kp[:, 1, :], k32).then_inc(S["f_kpart"], 1)
                    pool.wait_ge(S["f_kpart"], 4 * n + 3)
                    g.tensor_tensor(kp[:, 2, :], k32, kp[:, 1, :], ALU.subtract).then_inc(S["f_kpart"], 1)

        @block.scalar
        def _(act):
            a_ = nc.scalar
            act.wait_ge(S["loaded"], 16 * 10)
            a_.activation(scond[:, :], COL[:, CT["cond"][0]:CT["cond"][0] + B], ACT.Silu).then_inc(S["silu_ready"], 1)
            act.wait_ge(S["prep_pe"], PE_CTXT)
            a_.activation(ctxLT[:, :], PS[:, M1, 0:B * NC], ACT.Identity).then_inc(S["prep_act"], 1)
            for l in range(NL):
                act.wait_ge(S["prep_pe"], PE_K[l])
                if l:
                    act.wait_ge(S["prep_kparts"], 4 * l)
                a_.activation(kc32[:, :], PS[:, l, 0:B * NC], ACT.Identity,
                              bias=(0.0 if l == 1 else col(f"bck{l}"))).then_inc(S["prep_act"], 1)

            def to_channels(k):
                act.wait_ge(S["xnT_ready"], k + 1)
                a_.activation(hT[:, :], PS[:, M0, :], ACT.Identity, bias=V4[:, 1:2], scale=V4[:, 0:1]).then_inc(
                    S["hT_ready"], 1)

            def gated(k):
                act.wait_ge(S["y_ps"], k + 1)
                a_.activation(YT[:, :], PS[:, M1, :], ACT.Identity, bias=V4[:, 3:4], scale=V4[:, 2:3]).then_inc(
                    S["y_ready"], 1)

            def exps(l, b, c):
                base = units_b(l, b, c)
                np_ = NC if c else P
                for u in range(8 if c else 32 if l else 4):
                    act.wait_ge(S["sB_ready"], scored(l, b, c) + u + 1)
                    if u >= 4:
                        act.wait_ge(S["pv_used"], base + u - 3)
                    bk = 2 * (u % 2)
                    a_.activation(PT[0:np_, u % 4, :].rearrange("p (a n) -> p a n", a=2), PS[0:np_, bk:bk + 2, :],
                                  ACT.Exp).then_inc(S["p_ready"], 1)

            def finish(l, b, c, k):
                a = attn(l, b, c)
                act.wait_ge(S["pv_used"], units_b(l, b, c) + (32 if l and not c else 8 if c else 4))
                if l == 0 and c == 0:
                    o = U[:, :, :].rearrange("p k (t w n) -> p k t w n", t=T, w=2)
                    for wd in range(2):
                        for k2 in range(2):
                            ins = a_.activation(o[:, k2, :, wd, :],
                                                PS[:, 4 + 2 * wd + k2, 0:256].rearrange("p (t n) -> p t n", t=T),
                                                ACT.Identity)
                else:
                    ins = a_.activation(U[:, :, :], PS[:, 4:6, :], ACT.Identity)
                ins.then_inc(S["u_ready"], 1)
                act.wait_ge(S["onT_ready"], a + 1)
                a_.activation(OT[:, :], PS[:, M0, :], ACT.Identity).then_inc(S["oT_ready"], 1)
                gated(k)

            for l in (0,):
                with act.Fori(0, B) as b:
                    n = selfs(l, b)
                    to_channels(branch(l, b, 0))
                    if l != 1:
                        act.wait_ge(S["qk_ready"], 2 * n + 1)
                        a_.activation(qk[:, 0, :], PS[:, 0, :], ACT.Identity, bias=bqs[:, BQ[l]:BQ[l] + 1],
                                      scale=QSCALE).then_inc(S["q_ready"], 1)
                        a_.activation(qk[:, 1, :], PS[:, 1, :], ACT.Identity, bias=col(f"bk{l}")).then_inc(
                            S["k_ready"], 1)
                    exps(l, b, 0)
                    finish(l, b, 0, branch(l, b, 0))
                    to_channels(branch(l, b, 1))
                    act.wait_ge(S["qk_ready"], 2 * n + 2)
                    a_.activation(qk[:, 0, :], PS[:, 0, :], ACT.Identity,
                                  bias=(0.0 if l == 1 else bqs[:, BQ[l] + 1:BQ[l] + 2]),
                                  scale=QSCALE).then_inc(S["q_ready"], 1)
                    if l:
                        exps(l, b, 1)
                    else:
                        def scores_out(u):
                            act.wait_ge(S["sA_ready"], units_a(0, b, 1) + u + 1)
                            if u >= 2:
                                act.wait_ge(S["w2_ready"], 8 * b + u - 1)
                                act.wait_ge(S["e_ready"], 8 * b + u - 1)
                            a_.activation(SX[:, u % 2, :, :].rearrange("p (i j) n -> p i (j n)", i=2),
                                          PS[:, 2 * (u % 2):2 * (u % 2) + 2, 0:4 * NC], ACT.Identity).then_inc(
                                S["sx_ready"], 1)

                        def exp_top(u):
                            act.wait_ge(S["negm_ready"], 8 * b + u + 1)
                            if u >= 2:
                                act.wait_ge(S["pw_ready"], 8 * b + u - 1)
                            for h in range(8):
                                ins = a_.activation(E[:, u % 2, h, :], SX[:, u % 2, h, :], ACT.Exp,
                                                    bias=nm8[:, u % 2, h:h + 1])
                            ins.then_inc(S["e_ready"], 1)

                        def probs_out(u):
                            act.wait_ge(S["pT_ready"], 8 * b + u + 1)
                            if u >= 2:
                                act.wait_ge(S["pv_used"], units_b(0, b, 1) + u - 1)
                            a_.activation(PT[0:NC, u % 2, :].rearrange("p (a n) -> p a n", a=2),
                                          PS[0:NC, M0:M0 + 2, :], ACT.Identity).then_inc(S["p_ready"], 1)

                        for u in range(8):
                            scores_out(u)
                            exp_top(u)
                            if u:
                                probs_out(u - 1)
                        probs_out(7)
                    finish(l, b, 1, branch(l, b, 1))
                with act.Fori(0, B) as b:
                    n, k = selfs(l, b), branch(l, b, 2)
                    to_channels(k)
                    for m in range(4):
                        act.wait_ge(S["ff_ready"], 4 * n + m + 1)
                        if l == 0:
                            a_.activation(HB[:, m, :], PS[:, 2 * (m % 2), :], ACT.Silu,
                                          bias=col("b1_0", m)).then_inc(S["gate_ready"], 1)
                        else:
                            a_.activation(HB[:, m, :], PS[:, m, :], ACT.Gelu if l == 2 else ACT.Gelu_apprx_tanh,
                                          bias=col(f"b1_{l}", m)).then_inc(S["hid_ready"], 1)
                    gated(k)

            def out_of(dst, src, done, bias=0.0, scale=1.0):
                a_.activation(dst, src, ACT.Identity, bias=bias, scale=scale).then_inc(done, 1)

            def rows_out(dst, bank, ready, n, done):
                act.wait_ge(ready, n + 1)
                out_of(dst[:, :], PS[:, bank, :].bitcast(BF16)[0:48, 0:L], done)

            def self_exp(n, p):
                u, grp = 64 * n + p, 16 * n + p // 4
                act.wait_ge(S["b_ready"], u + 1)
                if p % 4 == 0 and grp >= 2:
                    act.wait_ge(S["b_pv"], grp - 1)
                a_.activation(GP[:, 4 * (grp % 2) + p % 4, :], PS[:, BANK_B[p % 2], :], ACT.Exp).then_inc(
                    S["b_exp"], 1)

            def cross_exp(n, h):
                act.wait_ge(S["xb_ready"], 16 * n + h + 1)
                if h % 4 == 0 and 4 * n + h // 4 >= 1:
                    act.wait_ge(S["xb_pv"], 4 * n + h // 4)
                a_.activation(PX[0:NC, h % 4, :], PS[0:NC, BANK_2[0], :], ACT.Exp).then_inc(S["xb_exp"], 1)

            def gelus(l, n, half):
                act.wait_ge(S["ff_ps"], 4 * n + 2 * half + 2)
                for m in (2 * half, 2 * half + 1):
                    a_.activation(HB[:, m, :], PS[:, BANK_2[m % 2], :], ACT.Gelu if l == 2 else ACT.Gelu_apprx_tanh,
                                  bias=col(f"b1_{l}", m)).then_inc(S["ff_hid"], 1)

            for s in SLOTS:
                n1, n2, n3 = s - 1, s - 2, s + 2
                (l1, b1), (l2, b2), (l3, b3) = item(n1), item(n2), item(n3)
                for p in range(POINTS):
                    if item(s + 1)[0]:
                        if p == M_TURN + 1:
                            rows_out(mT, BANK_A[0], S["a_mTps"], s + 1, S["a_mT"])
                        if p == 27:
                            n = s + 1
                            act.wait_ge(S["v_ps"], n + 1)
                            if n == 1:
                                act.wait_ge(S["late_consts"], LATE)
                            for s2 in range(2):
                                src = PS[:, BANK_1, :].rearrange("p (t n) -> p t n", t=T)[:, :, 64 * s2:64 * s2 + 64]
                                dst = VAs[n % 2][:, :, 256 * s2:256 * s2 + 256].rearrange("p t (h e) -> p t h e",
                                                                                          e=32)
                                out_of(dst[:, :, :, 16 * s2:16 * s2 + 8], src.rearrange("p t (h d) -> p t h d", d=8),
                                       S["v_in"])
                    if l1 and p == XM_TURN + 1:
                        rows_out(mTx, BANK_1, S["xa_mTps"], n1, S["xa_mT"])
                    if item(s)[0]:
                        self_exp(s, p)
                        if p == U_HALF:
                            act.wait_ge(S["b_pv"], 16 * s + 8)
                            if s:
                                act.wait_ge(S["c1_T"], 2 * s)
                            out_of(U[:, 0, :], PS[:, BANK_V, :], S["b_u"])
                    if l1:
                        if p == 3:
                            act.wait_ge(S["b_pv"], 16 * n1 + 16)
                            out_of(U[:, 1, :], PS[:, BANK_V, :], S["b_u"])
                        if p == 11:
                            act.wait_ge(S["c1_onT"], n1 + 1)
                            out_of(H1[:, :], PS[:, BANK_1, :], S["c1_oT"])
                        if p == 13:
                            act.wait_ge(S["c1_yps"], n1 + 1)
                            out_of(XN1[:, :, :].rearrange("p t c -> p (t c)"), PS[:, BANK_1, :], S["c1_y"],
                                   vec(l1, b1, 0, 3), vec(l1, b1, 0, 2))
                        if p == 21:
                            act.wait_ge(S["c1_xnT"], n1 + 1)
                            out_of(H1[:, :], PS[:, BANK_1, :], S["c1_h"], vec(l1, b1, 1, 1), vec(l1, b1, 1, 0))
                        if p == 23:
                            act.wait_ge(S["x_qps"], n1 + 1)
                            i = BQ.get(l1, 0) + 1
                            out_of(QX32, PS[:, BANK_1, :], S["x_q"], 0.0 if l1 == 1 else bqs[:, i:i + 1], QSCALE)
                    if l2:
                        quad, k = divmod(p, 5)
                        if quad < 4 and k < 4:
                            cross_exp(n2, 4 * quad + k)
                        if p in (10, 20):
                            act.wait_ge(S["xb_pv"], 4 * n2 + (2 if p == 10 else 4))
                            out_of(U2[:, p // 20, :], PS[:, BANK_2[1], :], S["xb_u"])
                        if p == 25:
                            act.wait_ge(S["c2_onT"], n2 + 1)
                            out_of(H2[:, :], PS[:, BANK_2[0], :], S["c2_oT"])
                        if p == 27:
                            act.wait_ge(S["c2_yps"], 2 * n2 + 1)
                            out_of(XN2[:, :, :].rearrange("p t c -> p (t c)"), PS[:, BANK_2[1], :], S["c2_y"],
                                   vec(l2, b2, 1, 3), vec(l2, b2, 1, 2))
                        if p == 35:
                            act.wait_ge(S["c2_xnT"], order2("ff", n2) + 1)
                            out_of(H2[:, :], PS[:, BANK_2[0], :], S["c2_h"], vec(l2, b2, 2, 1), vec(l2, b2, 2, 0))
                        if p in (38, 41):
                            gelus(l2, n2, (p - 38) // 3)
                        if p == 44:
                            act.wait_ge(S["c2_yps"], 2 * n2 + 2)
                            out_of(XN2[:, :, :].rearrange("p t c -> p (t c)"), PS[:, BANK_2[1], :], S["c2_y"],
                                   vec(l2, b2, 2, 3), vec(l2, b2, 2, 2))
                    if l3:
                        if p == 53:
                            act.wait_ge(S["c2_xnT"], order2("front", n3) + 1)
                            out_of(HF[:, :], PS[:, BANK_2[0], :], S["c2_h"], vec(l3, b3, 0, 1), vec(l3, b3, 0, 0))
                        if p == 55 and l3 != 1:
                            act.wait_ge(S["f_qkps"], 2 * n3 + 2)
                            i = BQ[l3]
                            if n3:
                                act.wait_ge(S["k_in"], 96 * n3)
                            out_of(qk[:, 0, :], PS[:, BANK_2[0], :], S["f_q"], bqs[:, i:i + 1], QSCALE)
                            out_of(qk[:, 1, :], PS[:, BANK_2[1], :], S["f_k"], col(f"bk{l3}"))

        @block.tensor
        def _(pe):
            t_ = nc.tensor

            def mm(o, a, m, start=True, stop=True, **kw):
                return t_.matmul(o, a, m, start=start, stop=stop, **kw)

            pe.wait_ge(S["loaded"], 16 * 10)
            pe.wait_ge(S["silu_ready"], 1)
            for n, (l, kind, br) in enumerate(CHUNKS):
                cond = COL[:, CT["cond"][0]:CT["cond"][0] + B] if l == 1 else scond[:, :]
                mm(PS[:, M0, B * n:B * n + B], ADA[:, C * n:C * n + C], cond)
            n0 = B * len(CHUNKS)
            for n, l in enumerate((0, 2, 3)):
                mm(PS[:, M0, n0 + 2 * n:n0 + 2 * n + 1], w(f"o{l}"), col(f"bv{l}"))
                ins = mm(PS[:, M0, n0 + 2 * n + 1:n0 + 2 * n + 2], w(f"co{l}"), col(f"bcv{l}"))
            ins.then_inc(S["prep_pe"], 1)
            pe.wait_ge(S["prep_dve"], DVE_CTX)
            for b in range(B):
                ins = t_.transpose(PS[:, M1, NC * b:NC * b + NC], ctxK[:, b, :], ident[0:NC, 0:NC])
            ins.then_inc(S["prep_pe"], 1)
            for l in range(NL):
                if l == 3:
                    pe.wait_ge(S["prep_act"], 1)
                src = ctxLT if l == 3 else ctxT
                mm(PS[:, l, 0:B * NC], w(f"ck{l}"), src[:, :]).then_inc(S["prep_pe"], 1)
                if l >= 2:
                    pe.wait_ge(S["prep_dve"], DVE_VC[l - 2])
                for b in range(B):
                    ins = mm(PS[0:NC, 4 + l % 2, C * b:C * b + C], src[:, NC * b:NC * b + NC], w(f"cv{l}"))
                ins.then_inc(S["prep_pe"], 1)
            pe.wait_ge(S["prep_dve"], DVE_MASK)
            for kt in range(T):
                for t in range(T):
                    dst = (M0B, M1B)[kt // 2]
                    o = 512 * (kt % 2) + P * t
                    ins = t_.transpose(dst[:, o:o + P], MB[:, t, P * kt:P * kt + P], identb[:, :])
            ins.then_inc(S["prep_pe"], 1)
            for t in range(T):
                ins = mm(PS[:, 4, P * t:P * t + P], ones[:, :], diag[:, t, :])
            ins.then_inc(S["prep_pe"], 1)

            def turned_norm(k):
                for t in range(T):
                    pe.wait_ge(S["xn_ready"], 4 * k + t + 1)
                    ins = t_.transpose(PS[:, M0, P * t:P * t + P], XN[:, t, :], ident[:, :])
                ins.then_inc(S["xnT_ready"], 1)
                pe.wait_ge(S["hT_ready"], k + 1)

            def back_to_tokens(k):
                pe.wait_ge(S["y_ready"], k + 1)
                for t in range(T):
                    ins = t_.transpose(PS[:, M0, P * t:P * t + P], YT[:, P * t:P * t + P], ident[:, :])
                ins.then_inc(S["yb_ready"], 1)

            def output(l, b, c, k):
                a = attn(l, b, c)
                pe.wait_ge(S["u_ready"], a + 1)
                for t in range(T):
                    for k2 in range(2):
                        o = 256 * t + 128 * k2
                        ins = t_.transpose(PS[:, 4 + o // 512, o % 512:o % 512 + P], U[:, k2, P * t:P * t + P],
                                           ident[:, :])
                ins.then_inc(S["T_ready"], 1)
                pe.wait_ge(S["on_ready"], a + 1)
                for t in range(T):
                    ins = t_.transpose(PS[:, M0, P * t:P * t + P], ON[:, t, :], ident[:, :])
                ins.then_inc(S["onT_ready"], 1)
                pe.wait_ge(S["oT_ready"], a + 1)
                mm(PS[:, M1, :], w(f"{'c' if c else ''}o{l}"), OT[:, :]).then_inc(S["y_ps"], 1)
                back_to_tokens(k)

            def heads(pair, i):
                return slice(64 * i, 64 * i + ROWS), slice(64 * i, 64 * i + ROWS_FULL)

            def max_rows(l, b, c):
                n = maxes(l, b, c)
                held(pe, S["m_step"], 4 * n + 4)
                for t in range(T):
                    ins = t_.transpose(M0B[0:48, P * t:P * t + P],
                                       m3[:, t, :, :, :].rearrange("p i r j -> p (i r j)"), identb[:, :])
                ins.then_inc(S["mT_ps"], 1)
                held(pe, S["m_stacked"], 32 * (n + 1))

            def values_in(l, b, c, hd, lhs_rows, kt, moving, o, start, stop):
                g, bank = hd % 4, (hd // 4) % 2
                va = VX[0:NC, 32 * hd:32 * hd + 32] if c else VA[lhs_rows, kt, 32 * hd:32 * hd + 32]
                return mm(o[32 * g:32 * g + 32], va, moving, start=start, stop=stop, skip_group_check=True)

            for l in (0,):
                with pe.Fori(0, B) as b:
                    n = selfs(l, b)
                    a, k = attn(l, b, 0), branch(l, b, 0)
                    turned_norm(k)
                    mm(PS[:, 0, :], w(f"q{l}"), hT[:, :])
                    ins = mm(PS[:, 1, :], w(f"k{l}"), hT[:, :])
                    if l == 1:
                        mm(PS[:, 2, :], w("qrot1"), hT[:, :])
                        ins = mm(PS[:, 3, :], w("krot1"), hT[:, :])
                    ins.then_inc(S["qk_ready"], 1)
                    for t in range(T):
                        ins = mm(PS[:, M1, P * t:P * t + P], hT[:, P * t:P * t + P], w(f"v{l}"))
                    ins.then_inc(S["v_ready"], 1)
                    ua, ub = units_a(l, b, 0), units_b(l, b, 0)
                    pe.wait_ge(S["k_stacked"], 192 * (n + 1))
                    held(pe, S["q_stacked"], 192 * (a + 1))
                    if l == 0:
                        pe.wait_ge(S["const_rows_in"], 16 * 2 * (1 + NL))
                        for t in range(T):
                            if t >= 2:
                                held(pe, S["sA_used"], reduced(l, b, 0) + t - 1)
                            for i in range(2):
                                r = slice(64 * i, 64 * i + ROWS)
                                for j in range(J):
                                    for wd in range(2):
                                        q0 = P * t + WIN * wd
                                        ins = mm(PS[64 * wd:64 * wd + 64, 2 * (t % 2) + i, WIN * j:WIN * j + WIN],
                                                 QS[r, j, q0:q0 + WIN], KS[r, j, q0:q0 + WIN])
                            ins.then_inc(S["sA_ready"], 1)
                    else:
                        for u in range(32):
                            t, j = divmod(u, J)
                            if u >= 2:
                                pe.wait_ge(S["sA_used"], reduced(l, b, 0) + u - 1)
                            for i in range(2):
                                r = slice(64 * i, 64 * i + ROWS)
                                ins = mm(PS[:, 2 * (u % 2) + i, :], QS[r, j, P * t:P * t + P], KS[r, j, :],
                                         stop=l != 1)
                            if l == 1:
                                for i in range(2):
                                    ins = mm(PS[:, 2 * (u % 2) + i, :], identb[:, :], MB[:, t, :], start=False)
                            ins.then_inc(S["sA_ready"], 1)
                    max_rows(l, b, 0)
                    held(pe, S["va_ready"], 2 * n + 2)
                    if l == 0:
                        def win_scores(t):
                            if t >= 2:
                                held(pe, S["p_ready"], ub + t - 1)
                            for i in range(2):
                                r = slice(64 * i, 64 * i + ROWS_FULL)
                                for j in range(J):
                                    for wd in range(2):
                                        q0 = P * t + WIN * wd
                                        ins = mm(PS[64 * wd:64 * wd + 64, 2 * (t % 2) + i, WIN * j:WIN * j + WIN],
                                                 KS[r, j, q0:q0 + WIN], QS[r, j, q0:q0 + WIN])
                            ins.then_inc(S["sB_ready"], 1)

                        def win_values(t):
                            held(pe, S["p_ready"], ub + t + 1)
                            for wd in range(2):
                                r = slice(64 * wd, 64 * wd + 64)
                                for hd in range(H):
                                    i, j = hd % 2, hd // 2
                                    o = PS[:, 4 + 2 * wd + (hd // 4) % 2, WIN * t:WIN * t + WIN]
                                    ins = values_in(l, b, 0, hd, r, t,
                                                    PT[r, t, 512 * i + WIN * j:512 * i + WIN * j + WIN], o,
                                                    t == 0 and hd < 8, t == T - 1 and hd >= 8)
                            ins.then_inc(S["pv_used"], 1)

                        for t in range(T):
                            win_scores(t)
                            if t:
                                win_values(t - 1)
                        win_values(T - 1)
                    else:
                        def scores(u):
                            q, kt, half = u // 8, u % 8 // 2, u % 2
                            j = 2 * q + half
                            if u >= 2:
                                pe.wait_ge(S["p_ready"], ub + u - 1)
                            for i in range(2):
                                r = slice(64 * i, 64 * i + ROWS_FULL)
                                ins = mm(PS[:, 2 * (u % 2) + i, :], KS[r, j, P * kt:P * kt + P], QS[r, j, :],
                                         stop=l != 1)
                            if l == 1:
                                for i in range(2):
                                    ins = mm(PS[:, 2 * (u % 2) + i, :], identb[:, :], MBT[:, kt, :], start=False)
                            ins.then_inc(S["sB_ready"], 1)

                        def values(u):
                            q, kt = u // 8, u % 8 // 2
                            pe.wait_ge(S["p_ready"], ub + u + 2)
                            for g in range(4):
                                ins = values_in(l, b, 0, 4 * q + g, slice(0, P), kt,
                                                PT[:, (u + g // 2) % 4, 512 * (g % 2):512 * (g % 2) + 512],
                                                PS[:, 4 + q % 2, :], q < 2 and kt == 0, q >= 2 and kt == 3)
                            ins.then_inc(S["pv_used"], 2)

                        for u in range(0, 32, 2):
                            scores(u)
                            scores(u + 1)
                            if u:
                                values(u - 2)
                        values(30)
                    output(l, b, 0, k)
                    a, k = attn(l, b, 1), branch(l, b, 1)
                    turned_norm(k)
                    mm(PS[:, 0, :], w(f"cq{l}"), hT[:, :]).then_inc(S["qk_ready"], 1)
                    ua, ub = units_a(l, b, 1), units_b(l, b, 1)
                    pe.wait_ge(S["kvx_ready"], 4 * n + 4)
                    held(pe, S["q_stacked"], 192 * (a + 1))

                    def ctx_scores(u):
                        t, part = divmod(u, 2)
                        if u >= 2:
                            pe.wait_ge(S["sA_used" if l else "sx_ready"], (reduced(l, b, 1) if l else 8 * b) + u - 1)
                        rows = ROWS + 1 if l in (1, 2) else ROWS
                        for i in range(2):
                            r = slice(64 * i, 64 * i + rows)
                            for jj in range(4):
                                j = 4 * part + jj
                                ins = mm(PS[:, 2 * (u % 2) + i, NC * jj:NC * jj + NC], QS[r, j, P * t:P * t + P],
                                         KX[r, j, :])
                        ins.then_inc(S["sA_ready"], 1)

                    if l:
                        for u in range(8):
                            ctx_scores(u)
                        max_rows(l, b, 1)

                        def scores_x(j):
                            if j >= 2:
                                pe.wait_ge(S["p_ready"], ub + j - 1)
                            for i in range(2):
                                r = slice(64 * i, 64 * i + ROWS_FULL)
                                ins = mm(PS[0:NC, 2 * (j % 2) + i, :], KX[r, j, :], QS[r, j, :])
                            ins.then_inc(S["sB_ready"], 1)

                        def values_x(j):
                            pe.wait_ge(S["p_ready"], ub + j + 2)
                            for g in range(4):
                                hd = 2 * j + g
                                ins = values_in(l, b, 1, hd, None, 0,
                                                PT[0:NC, (j + g // 2) % 4, 512 * (g % 2):512 * (g % 2) + 512],
                                                PS[:, 4 + (hd // 4) % 2, :], hd < 8, hd >= 8)
                            ins.then_inc(S["pv_used"], 2)

                        for j in range(0, J, 2):
                            scores_x(j)
                            scores_x(j + 1)
                            if j:
                                values_x(j - 2)
                        values_x(J - 2)
                    else:
                        def turn_probs(u):
                            pe.wait_ge(S["pw_ready"], 8 * b + u + 1)
                            if u:
                                pe.wait_ge(S["p_ready"], ub + u)
                            for h in range(8):
                                ins = t_.transpose(PS[0:NC, M0 + h // 4, P * (h % 4):P * (h % 4) + P],
                                                   PW[:, h, :], ident[:, :])
                            ins.then_inc(S["pT_ready"], 1)

                        def values_t(u):
                            t, part = divmod(u, 2)
                            pe.wait_ge(S["p_ready"], ub + u + 1)
                            for hh in range(8):
                                hd = 8 * part + hh
                                i, jj = hh % 2, hh // 2
                                ins = values_in(l, b, 1, hd, None, 0,
                                                PT[0:NC, u % 2, 512 * i + P * jj:512 * i + P * jj + P],
                                                PS[:, 4 + (hd // 4) % 2, P * t:P * t + P],
                                                u == 0, u == 7)
                            ins.then_inc(S["pv_used"], 1)

                        ctx_scores(0)
                        for u in range(8):
                            if u < 7:
                                ctx_scores(u + 1)
                            turn_probs(u)
                            if u:
                                values_t(u - 1)
                        values_t(7)
                    output(l, b, 1, k)
                with pe.Fori(0, B) as b:
                    n, k = selfs(l, b), branch(l, b, 2)
                    turned_norm(k)
                    for m in range(4):
                        if l == 0:
                            if m >= 2:
                                pe.wait_ge(S["hid_ready"], 4 * n + m - 1)
                            mm(PS[:, 2 * (m % 2), :], w("f1_0", P * m, P), hT[:, :])
                            mm(PS[:, 2 * (m % 2) + 1, :], w("f1_0", P * (4 + m), P), hT[:, :]).then_inc(
                                S["ff_ready"], 1)
                        else:
                            mm(PS[:, m, :], w(f"f1_{l}", P * m, P), hT[:, :]).then_inc(S["ff_ready"], 1)
                    for m in range(4):
                        pe.wait_ge(S["hid_ready"], 4 * n + m + 1)
                        ins = mm(PS[:, M1, :], w(f"f2_{l}", C * m, C), HB[:, m, :], start=m == 0, stop=m == 3)
                    ins.then_inc(S["y_ps"], 1)
                    back_to_tokens(k)

            def turned(dst, src_of, done):
                for t in range(T):
                    ins = t_.transpose(PS[:, dst, P * t:P * t + P], src_of(t), ident[:, :])
                ins.then_inc(done, 1)

            def scores_of(n, p):
                l, q, kt, g = 1 + n // B, QUADS[p // 16], p // 4 % 4, p % 4
                hd, u = 4 * q + g, 64 * n + p
                i, j = hd % 2, hd // 2
                if p == 0:
                    pe.wait_ge(S["a_rows"], 32 * (n + 1))
                if u >= 2:
                    pe.wait_ge(S["b_exp"], u - 1)
                r = slice(64 * i, 64 * i + 64)
                ins = mm(PS[:, BANK_B[p % 2], :], KSs[n % 2][r, j, P * kt:P * kt + P], QSs[n % 2][r, j, :],
                         stop=l != 1)
                if l == 1:
                    ins = mm(PS[:, BANK_B[p % 2], :], identb[:, :], MBT[:, kt, :], start=False)
                ins.then_inc(S["b_ready"], 1)

            def maxima_of(n, a):
                l, u = 1 + n // B, 64 * n + a
                i, t, j = unit_a(a)
                if a % 32 == 0:
                    pe.wait_ge(S[("q_in0", "q_in")[i]], 96 * (n + 1))
                    pe.wait_ge(S[("k_in0", "k_in")[i]], 96 * (n + 1))
                if a == 0:
                    pe.wait_ge(S["late_rows"], 32)
                    pe.wait_ge(S["late_consts"], LATE)
                if u >= 2:
                    pe.wait_ge(S["a_used"], u - 1)
                r = slice(64 * i, 64 * i + ROWS)
                ins = mm(PS[:, BANK_A[a % 2], :], QSs[n % 2][r, j, P * t:P * t + P], KSs[n % 2][r, j, :],
                         stop=l != 1)
                if l == 1:
                    ins = mm(PS[:, BANK_A[a % 2], :], identb[:, :], MB[:, t, :], start=False)
                ins.then_inc(S["a_ready"], 1)

            def values_of(n, grp):
                q, kt, u = QUADS[grp // 4], grp % 4, 16 * n + grp
                pe.wait_ge(S["b_exp"], 4 * u + 4)
                if grp % 8 == 0 and u:
                    pe.wait_ge(S["b_u"], u // 8)
                if grp == 0:
                    pe.wait_ge(S["v_in"], 2 * n + 2)
                for g in range(4):
                    hd = 4 * q + g
                    ins = mm(PS[32 * g:32 * g + 32, BANK_V, :], VAs[n % 2][:, kt, 32 * hd:32 * hd + 32],
                             GP[:, 4 * (u % 2) + g, :], start=grp % 8 == 0, stop=grp % 8 == 7, skip_group_check=True)
                ins.then_inc(S["b_pv"], 1)

            def cross_scores(n, h):
                l, b = item(n)
                hd, u = 4 * QUADS[h // 4] + h % 4, 16 * n + h
                i, j = hd % 2, hd // 2
                if h == 0:
                    pe.wait_ge(S["xa_rows"], 32 * (n + 1))
                    pe.wait_ge(S["f_q"], min(n + 4, N))
                    pe.wait_ge(S["f_k"], min(n + 4, N))
                if u:
                    pe.wait_ge(S["xb_exp"], u)
                r = slice(64 * i, 64 * i + ROWS_FULL)
                mm(PS[0:NC, BANK_2[0], :], KC[r, l, j, NC * b:NC * b + NC], QX[r, j, :]).then_inc(S["xb_ready"], 1)

            def cross_values(n, quad):
                q = QUADS[quad]
                pe.wait_ge(S["xb_exp"], 16 * n + 4 * quad + 4)
                if quad == 0:
                    pe.wait_ge(S["xb_kv"], 2 * n + 2)
                if quad == 2:
                    pe.wait_ge(S["xb_u"], 2 * n + 1)
                for g in range(4):
                    hd = 4 * q + g
                    ins = mm(PS[32 * g:32 * g + 32, BANK_2[1], :], VX[0:NC, 32 * hd:32 * hd + 32], PX[0:NC, g, :],
                             start=quad % 2 == 0, stop=quad % 2 == 1, skip_group_check=True)
                ins.then_inc(S["xb_pv"], 1)

            def cross_maxima(n, u):
                l, b = item(n)
                i, t, half = u // 8, u // 2 % 4, u % 2
                if u % 8 == 0:
                    pe.wait_ge(S[("x_in0", "x_in")[i]], 96 * (n + 1))
                if u:
                    pe.wait_ge(S["xa_used"], 16 * n + u)
                else:
                    pe.wait_ge(S["v_in"], min(2 * (n + 3), 2 * N))
                r = slice(64 * i, 64 * i + (ROWS + 1 if l in (1, 2) else ROWS))
                for jj in range(4):
                    j = 4 * half + jj
                    ins = mm(PS[:, BANK_1, NC * jj:NC * jj + NC], QX[r, j, P * t:P * t + P],
                             KC[r, l, j, NC * b:NC * b + NC])
                ins.then_inc(S["xa_ready"], 1)

            def parts_turned(parts, bank, ready, n, done):
                pe.wait_ge(ready, 4 * n + 4)
                dst = PS[:, bank, :].bitcast(BF16)
                for t in range(T):
                    ins = t_.transpose(dst[0:48, P * t:P * t + P],
                                       parts[:, t, :, :, :].rearrange("p i r j -> p (i r j)"), identb[:, :])
                ins.then_inc(done, 1)

            for s in SLOTS:
                n1, n2, n3 = s - 1, s - 2, s + 2
                (l1, b1), (l2, b2), (l3, b3) = item(n1), item(n2), item(n3)
                for p in range(POINTS):
                    if item(s)[0]:
                        scores_of(s, p)
                    if item(s + 1)[0]:
                        for a in range(maxima_at(p), maxima_at(p + 1)):
                            maxima_of(s + 1, a)
                        if p == M_TURN:
                            parts_turned(m3, BANK_A[0], S["a_m"], s + 1, S["a_mTps"])
                    if item(s)[0] and p % 4 == 2 and p >= 6:
                        values_of(s, p // 4 - 1)
                    if l1:
                        if p == 2:
                            values_of(n1, 15)
                        if p in (4, 7):
                            half = p // 7
                            pe.wait_ge(S["b_u"], 2 * n1 + 1 + half)
                            if half:
                                pe.wait_ge(S["c1_on"], 2 * n1 + 1)
                            elif n1:
                                pe.wait_ge(S["xa_mT"], n1)
                            turned(BANK_1, lambda t: U[:, half, P * t:P * t + P], S["c1_T"])
                        if p == 10:
                            pe.wait_ge(S["c1_on"], 2 * n1 + 2)
                            turned(BANK_1, lambda t: XN1[:, t, :], S["c1_onT"])
                        if p == 12:
                            pe.wait_ge(S["c1_oT"], n1 + 1)
                            mm(PS[:, BANK_1, :], w(f"o{l1}"), H1[:, :]).then_inc(S["c1_yps"], 1)
                        if p == 14:
                            pe.wait_ge(S["c1_y"], n1 + 1)
                            turned(BANK_1, lambda t: XN1[:, :, :].rearrange("p t c -> p (t c)")[:, P * t:P * t + P],
                                   S["c1_yb"])
                        if p == 20:
                            pe.wait_ge(S["c1_xn"], 4 * n1 + 4)
                            turned(BANK_1, lambda t: XN1[:, t, :], S["c1_xnT"])
                        if p == 22:
                            pe.wait_ge(S["c1_h"], n1 + 1)
                            mm(PS[:, BANK_1, :], w(f"cq{l1}"), H1[:, :]).then_inc(S["x_qps"], 1)
                    if p == 26 and item(s + 1)[0]:
                        if l1:
                            pe.wait_ge(S["x_q"], n1 + 1)
                        if s + 1:
                            pe.wait_ge(S["v_in"], 2 * (s + 1))
                        for t in range(T):
                            ins = mm(PS[:, BANK_1, P * t:P * t + P], HF[:, P * t:P * t + P],
                                     w(f"v{item(s + 1)[0]}"))
                        ins.then_inc(S["v_ps"], 1)
                    if l1:
                        if XA_FROM <= p < XA_FROM + 16:
                            cross_maxima(n1, p - XA_FROM)
                        if p == XM_TURN:
                            parts_turned(m3x, BANK_1, S["xa_m"], n1, S["xa_mTps"])
                    if l2:
                        quad, k = divmod(p, 5)
                        if quad < 4 and k < 4:
                            cross_scores(n2, 4 * quad + k)
                        elif quad < 4:
                            cross_values(n2, quad)
                        if p == 21:
                            pe.wait_ge(S["xb_u"], 2 * n2 + 2)
                            turned(BANK_2[0], lambda t: U2[:, 0, P * t:P * t + P], S["c2_T"])
                            turned(BANK_2[1], lambda t: U2[:, 1, P * t:P * t + P], S["c2_T"])
                        if p == 24:
                            pe.wait_ge(S["c2_on"], 2 * n2 + 2)
                            turned(BANK_2[0], lambda t: XN2[:, t, :], S["c2_onT"])
                        if p == 26:
                            pe.wait_ge(S["c2_oT"], n2 + 1)
                            mm(PS[:, BANK_2[1], :], w(f"co{l2}"), H2[:, :]).then_inc(S["c2_yps"], 1)
                        if p in (28, 45):
                            pe.wait_ge(S["c2_y"], 2 * n2 + 1 + p // 45)
                            turned(BANK_2[0], lambda t: XN2[:, :, :].rearrange("p t c -> p (t c)")[:, P * t:P * t + P],
                                   S["c2_yb"])
                        if p == 34:
                            pe.wait_ge(S["c2_xn"], 4 * order2("ff", n2) + 4)
                            turned(BANK_2[0], lambda t: XN2[:, t, :], S["c2_xnT"])
                        if p in (36, 39):
                            half = (p - 36) // 3
                            if half:
                                pe.wait_ge(S["ff_hid"], 4 * n2 + 2)
                            else:
                                pe.wait_ge(S["c2_h"], order2("ff", n2) + 1)
                            for m in (2 * half, 2 * half + 1):
                                mm(PS[:, BANK_2[m % 2], :], w(f"f1_{l2}", P * m, P), H2[:, :]).then_inc(S["ff_ps"], 1)
                        if p == 42:
                            pe.wait_ge(S["ff_hid"], 4 * n2 + 4)
                            for m in range(4):
                                ins = mm(PS[:, BANK_2[1], :], w(f"f2_{l2}", C * m, C), HB[:, m, :], start=m == 0,
                                         stop=m == 3)
                            ins.then_inc(S["c2_yps"], 1)
                    if l3:
                        if p == 52:
                            pe.wait_ge(S["c2_xn"], 4 * order2("front", n3) + 4)
                            turned(BANK_2[0], lambda t: XN2[:, t, :], S["c2_xnT"])
                        if p == 54:
                            pe.wait_ge(S["c2_h"], order2("front", n3) + 1)
                            if l3 != 1:
                                mm(PS[:, BANK_2[0], :], w(f"q{l3}"), HF[:, :]).then_inc(S["f_qkps"], 1)
                                mm(PS[:, BANK_2[1], :], w(f"k{l3}"), HF[:, :]).then_inc(S["f_qkps"], 1)
                        if p in (54, 57) and l3 == 1:
                            a, c = ("q1", "qrot1") if p == 54 else ("k1", "krot1")
                            if p == 57:
                                pe.wait_ge(S["f_rope"], 4 * n3 + 2)
                            mm(PS[:, BANK_2[0], :], w(a), HF[:, :])
                            mm(PS[:, BANK_2[1], :], w(c), HF[:, :]).then_inc(S["f_qkps"], 1)

        @block.vector
        def _(dve):
            v = nc.vector
            done = [0]

            def step(ins):
                done[0] += 1
                ins.then_inc(S["prep_dve"], 1)
                return done[0]

            def after(n):
                dve.wait_ge(S["prep_dve"], n)

            dve.wait_ge(S["loaded"], 16 * 10)
            stats = S["stats_ctx"]
            for b in range(B):
                v.bn_stats(cst[:, b, :], ctxK[:, b, :]).then_inc(stats, 1)
            for b in range(B):
                dve.wait_ge(stats, b + 1)
                v.bn_aggr(cmv[:, b, :], cst[:, b, :]).then_inc(stats, 1)
            dve.wait_ge(stats, 2 * B)
            assert step(v.tensor_scalar(cve[:, 0:B], cmv[:, :, 1], EPS[3], None, ALU.add)) == 1
            o, _ = CT["bq0"]
            step(v.tensor_scalar(bqs[:, :], COL[:, o:o + 6], QSCALE, None, ALU.mult))
            step(v.tensor_copy(identb[:, :], ident[:, :]))
            dve.wait_ge(S["ctx_rstd_ready"], 1)
            for b in range(B):
                step(v.tensor_scalar(ctxK[:, b, :], ctxK[:, b, :], cmv[:, b, 0:1], cve[:, B + b:B + b + 1],
                                     ALU.subtract, ALU.mult))
            assert done[0] == DVE_CTX
            step(v.tensor_copy(mkf[:, :], mrow8))
            after(done[0])
            m_any = step(v.tensor_reduce(mkany[:, :], mkf[:, :].rearrange("p (b n) -> p b n", b=B), AX.X, ALU.max))
            after(m_any)
            n = step(v.tensor_scalar(mkf[:, :], mkf[:, :], -MASKED, MASKED, ALU.mult, ALU.add))
            after(n)
            n = step(v.tensor_tensor(mkb[:, 0, :].rearrange("p (b n) -> p b n", b=B),
                                     mkf[0:8, :].rearrange("p (b n) -> p b n", b=B),
                                     mkany[0:8, :].unsqueeze(2).broadcast_to([8, B, NC]), ALU.mult))
            after(n)
            n = step(v.tensor_copy(mkf[:, :], mrow32[:, :]))
            after(n)
            n = step(v.tensor_scalar(mkf[:, :], mkf[:, :], 0.0, None, ALU.is_equal))
            after(n)
            n = step(v.tensor_reduce(poison[:, :], mkf[:, :].rearrange("p (b n) -> p b n", b=B), AX.X, ALU.min))
            v.tensor_scalar(mkb[:, 1, :], mkf[0:8, :], MASKED, None, ALU.mult).then_inc(S["prep_mask_rows"], 2)
            after(n)
            n = step(v.tensor_scalar(poison[:, :], poison[:, :], -1.0, 1.0, ALU.mult, ALU.add))
            after(n)
            n = step(v.reciprocal(poison[:, :], poison[:, :]))
            after(n)
            step(v.tensor_scalar(poison[:, :], poison[:, :], 0.0, None, ALU.mult))
            dve.wait_ge(S["prep_pe"], 1)
            o, _ = CT["adab"]
            nch = len(CHUNKS)
            n = step(v.tensor_tensor(mod[:, :, :], PS[:, M0, 0:B * nch].rearrange("p (n b) -> p n b", b=B),
                                     COL[:, o:o + nch].unsqueeze(2).broadcast_to([P, nch, B]), ALU.add))
            for i, l in enumerate((0, 2, 3)):
                for c in range(2):
                    q = PS[:, M0, B * nch + 2 * i + c:B * nch + 2 * i + c + 1]
                    n = step(v.tensor_scalar(cb[:, 2 * i + c:2 * i + c + 1], q,
                                             col(f"{'bco' if c else 'bo'}{l}"), None, ALU.add))
            after(n)
            where = {ch: i for i, ch in enumerate(CHUNKS)}

            def m(l, kind, br):
                return mod[:, where[(l, kind, br)], :]

            VV = VEC[:, :].rearrange("p (l b r f) -> p l b r f", l=NL, b=B, r=3)
            for l in range(NL):
                for br in range(3):
                    scale, shift, gate, gbias = (VV[:, l, :, br, f] for f in range(4))
                    has = (l, "sc", br) in where
                    if has:
                        step(v.tensor_scalar(scale, m(l, "sc", br), 1.0, col("w1", br) if l == 1 else 1.0,
                                             ALU.add, ALU.mult))
                        step(v.tensor_copy(shift, m(l, "sh", br)))
                        step(v.tensor_copy(gate, m(l, "g", br)))
                    else:
                        step(v.memset(gate, 1.0))
                        if l == 2:
                            step(v.tensor_copy(scale, col("w2", br).broadcast_to([P, B])))
                            step(v.tensor_copy(shift, col("lb2", br).broadcast_to([P, B])))
                        else:
                            step(v.memset(scale, 1.0))
                            step(v.memset(shift, 0.0))
                    bias = (col(f"b2_{l}") if br == 2 else
                            None if l == 1 else cb[:, 2 * (0, None, 1, 2)[l] + br:2 * (0, None, 1, 2)[l] + br + 1])
                    if bias is None:
                        step(v.memset(gbias, 0.0))
                    elif l == 2:
                        n = step(v.tensor_scalar(gbias, m(2, "t", br), bias, None, ALU.add))
                        if br == 1:
                            after(n)
                            step(v.tensor_tensor(gbias, gbias, poison[:, :], ALU.add))
                    elif has:
                        step(v.tensor_scalar(gbias, m(l, "g", br), bias, None, ALU.mult))
                    else:
                        step(v.tensor_copy(gbias, bias.broadcast_to([P, B])))
            kstep = S["prep_kparts"]
            for l in range(NL):
                dve.wait_ge(S["prep_act"], 2 + l)
                if l:
                    dve.wait_ge(S["prep_stacked"], 16 * 12 * l)
                if l == 1:
                    k3 = kc32[:, :].rearrange("p (b n) -> p b n", b=B)
                    after(step(v.tensor_tensor(k3, k3, mkany[:, :].unsqueeze(2).broadcast_to([P, B, NC]), ALU.mult)))
                v.tensor_copy(kcp[:, 0, :], kc32[:, :]).then_inc(kstep, 1)
                dve.wait_ge(kstep, 4 * l + 1)
                v.tensor_tensor(kc32[:, :], kc32[:, :], kcp[:, 0, :], ALU.subtract).then_inc(kstep, 1)
                dve.wait_ge(kstep, 4 * l + 2)
                v.tensor_copy(kcp[:, 1, :], kc32[:, :]).then_inc(kstep, 1)
                dve.wait_ge(kstep, 4 * l + 3)
                v.tensor_tensor(kcp[:, 2, :], kc32[:, :], kcp[:, 1, :], ALU.subtract).then_inc(kstep, 1)
                dve.wait_ge(S["prep_pe"], PE_V[l])
                n = step(v.tensor_copy(VC[:, l, :, :], PS[0:NC, 4 + l % 2, :].rearrange("p (b n) -> p b n", b=B)))
                if l < 2:
                    assert n == DVE_VC[l], (l, n)
            assert n == PREP_VC, n
            n = step(v.tensor_copy(MB[:, :, :], ms8))
            after(n)
            n = step(v.tensor_reduce(rany[:, :], MB[:, :, :], AX.X, ALU.max))
            after(n)
            n = step(v.tensor_scalar(MB[:, :, :], MB[:, :, :], -MASKED, MASKED, ALU.mult, ALU.add))
            after(n)
            for t in range(T):
                step(v.tensor_scalar(MB[:, t, :], MB[:, t, :], rany[:, t:t + 1], None, ALU.mult))
                n = step(v.tensor_scalar(diag[:, t, :], ident[:, :], rany[:, t:t + 1], None, ALU.mult))
            assert n == DVE_MASK, n
            dve.wait_ge(S["prep_pe"], PE_V[3] + 2)
            for k2, src in enumerate((M0B, M1B)):
                step(v.tensor_copy(MBT[:, 2 * k2:2 * k2 + 2, :], src.rearrange("p (a n) -> p a n", a=2)))
            for f in range(2):
                n = step(v.scalar_tensor_tensor(ROPEQ[:, f, :], PS[:, 4, :], QSCALE, ROPE[:, f, :], ALU.mult, ALU.mult))
            after(n)
            dve.wait_ge(S["x_loaded"], 16 * B)
            dve.wait_ge(S["base_consts"], 10)

            def norm(l, b, br):
                k = branch(l, b, br)
                X = xr if l == 0 else xs
                v.tensor_copy(V4[:, :], VEC[:, bass.ds(12 * b + 48 * l + 4 * br, 4)]).then_inc(S["stats_done"], 1)
                for t in range(T):
                    v.bn_stats(st[:, t, :], X[:, bass.ds(T * b + t, 1), :].rearrange("p a c -> p (a c)")).then_inc(
                        S["stats_done"], 1)
                for t in range(T):
                    held(dve, S["stats_done"], 5 * k + t + 2)
                    v.bn_aggr(mv[:, t, :], st[:, t, :]).then_inc(S["aggr_done"], 1)
                dve.wait_ge(S["aggr_done"], 4 * k + 4)
                v.tensor_scalar(ve[:, :], mv[:, :, 1], EPS[l], None, ALU.add).then_inc(S["ve_ready"], 1)
                dve.wait_ge(S["rstd_ready"], k + 1)
                for t in range(T):
                    v.tensor_scalar(XN[:, t, :], X[:, bass.ds(T * b + t, 1), :].rearrange("p a c -> p (a c)"),
                                    mv[:, t, 0:1], rstd[:, t:t + 1], ALU.subtract, ALU.mult).then_inc(
                        S["xn_ready"], 1)

            def residual(l, b, br):
                k = branch(l, b, br)
                X = xr if l == 0 else xs
                xb = X[:, bass.ds(T * b, T), :]
                dve.wait_ge(S["yb_ready"], k + 1)
                v.tensor_tensor(xb, PS[:, M0, :].rearrange("p (t c) -> p t c", t=T), xb, ALU.add).then_inc(
                    S["x_done"], 1)
                dve.wait_ge(S["x_done"], k + 1)

            def query_parts(a):
                q32, qp, part = qk[:, 0, :], qkp[:, 0, :, :], S["q_part"]
                dve.wait_ge(S["q_ready"], a + 1)
                v.tensor_copy(qp[:, 0, :], q32).then_inc(part, 1)
                dve.wait_ge(part, 4 * a + 1)
                v.tensor_tensor(q32, q32, qp[:, 0, :], ALU.subtract).then_inc(part, 1)
                dve.wait_ge(part, 4 * a + 2)
                v.tensor_copy(qp[:, 1, :], q32).then_inc(part, 1)
                dve.wait_ge(part, 4 * a + 3)
                v.tensor_tensor(qp[:, 2, :], q32, qp[:, 1, :], ALU.subtract).then_inc(part, 1)

            def max_parts(l, b, c):
                n = maxes(l, b, c)
                step_ = S["m_step"]
                src = mneg[:, :, :].rearrange("p t (j i) -> p t i j", i=2)
                dve.wait_ge(S["sA_used"], reduced(l, b, c) + (4 if l == 0 else 8 if c else 32))
                v.tensor_copy(m3[:, :, :, 0, :], src).then_inc(step_, 1)
                dve.wait_ge(step_, 4 * n + 1)
                v.tensor_tensor(src, src, m3[:, :, :, 0, :], ALU.subtract).then_inc(step_, 1)
                dve.wait_ge(step_, 4 * n + 2)
                v.tensor_copy(m3[:, :, :, 1, :], src).then_inc(step_, 1)
                dve.wait_ge(step_, 4 * n + 3)
                v.tensor_tensor(m3[:, :, :, 2, :], src, m3[:, :, :, 1, :], ALU.subtract).then_inc(step_, 1)
                dve.wait_ge(S["mT_ps"], n + 1)
                v.tensor_copy(mT[:, :], M0B[0:48, 0:L]).then_inc(S["mT_ready"], 1)

            def normalise(a):
                dve.wait_ge(S["T_ready"], a + 1)
                rows = PS[:, 4:6, :].rearrange("p k (h e) -> p (k h) e", e=16)
                v.reciprocal(rec[:, :].unsqueeze(2), rows[:, :, 8:9]).then_inc(S["rec_ready"], 1)
                dve.wait_ge(S["rec_ready"], a + 1)
                v.tensor_tensor(ON[:, :, :].rearrange("p t (h d) -> p (t h) d", d=HD), rows[:, :, 0:8],
                                rec[:, :].unsqueeze(2).broadcast_to([P, T * H, HD]), ALU.mult).then_inc(
                    S["on_ready"], 1)

            for l in (0,):
                with dve.Fori(0, B) as b:
                    n = selfs(l, b)
                    norm(l, b, 0)
                    if l == 1:
                        dve.wait_ge(S["qk_ready"], 2 * n + 1)
                        for which, tab in ((0, ROPEQ), (1, ROPE)):
                            o = 4 * b + 2 * which
                            v.tensor_tensor(ra[:, :], PS[:, which, :], tab[:, 0, :], ALU.mult).then_inc(
                                S["rope_step"], 1)
                            v.tensor_tensor(rb[:, :], PS[:, 2 + which, :], tab[:, 1, :], ALU.mult).then_inc(
                                S["rope_step"], 1)
                            dve.wait_ge(S["rope_step"], o + 2)
                            v.tensor_tensor(qk[:, which, :], ra[:, :], rb[:, :], ALU.add).then_inc(
                                S["q_ready" if which == 0 else "k_ready"], 1)
                            dve.wait_ge(S["q_ready" if which == 0 else "k_ready"],
                                        attn(1, b, 0) + 1 if which == 0 else n + 1)
                    query_parts(attn(l, b, 0))
                    dve.wait_ge(S["v_ready"], n + 1)
                    for s in range(2):
                        src = PS[:, M1, :].rearrange("p (t n) -> p t n", t=T)[:, :, 64 * s:64 * s + 64]
                        dst = VA[:, :, 256 * s:256 * s + 256].rearrange("p t (h e) -> p t h e", e=32)
                        v.tensor_copy(dst[:, :, :, 16 * s:16 * s + 8],
                                      src.rearrange("p t (h d) -> p t h d", d=8)).then_inc(S["va_ready"], 1)
                    ua = units_a(l, b, 0)
                    if l == 0:
                        for t in range(T):
                            dve.wait_ge(S["sA_ready"], ua + t + 1)
                            bk = 2 * (t % 2)
                            v.tensor_reduce(mneg[:, t, :].rearrange("p (j i) -> p i j", i=2),
                                            PS[:, bk:bk + 2, :].rearrange("p i (j n) -> p i j n", n=WIN), AX.X,
                                            ALU.max, negate=True).then_inc(S["sA_used"], 1)
                    else:
                        for u in range(32):
                            t, j = divmod(u, J)
                            dve.wait_ge(S["sA_ready"], ua + u + 1)
                            bk = 2 * (u % 2)
                            v.tensor_reduce(mneg[:, t, 2 * j:2 * j + 2], PS[:, bk:bk + 2, :], AX.X, ALU.max,
                                            negate=True).then_inc(S["sA_used"], 1)
                    max_parts(l, b, 0)
                    normalise(attn(l, b, 0))
                    residual(l, b, 0)
                    norm(l, b, 1)
                    query_parts(attn(l, b, 1))
                    ua = units_a(l, b, 1)
                    if l:
                        for u in range(8):
                            t, part = divmod(u, 2)
                            dve.wait_ge(S["sA_ready"], ua + u + 1)
                            bk = 2 * (u % 2)
                            v.tensor_reduce(mneg[:, t, 8 * part:8 * part + 8].rearrange("p (j i) -> p i j", i=2),
                                            PS[:, bk:bk + 2, 0:4 * NC].rearrange("p i (j n) -> p i j n", n=NC),
                                            AX.X, ALU.max, negate=True).then_inc(S["sA_used"], 1)
                        max_parts(l, b, 1)
                    else:
                        top = S["top_step"]
                        for u in range(8):
                            o = 31 * (8 * b + u)
                            sl = u % 2
                            held(dve, S["sx_ready"], 8 * b + u + 1)
                            for h in range(8):
                                v.max(v8[:, 0, h, :], SX[:, sl, h, :]).then_inc(top, 1)
                            dve.wait_ge(top, o + 8)
                            if u >= 2:
                                dve.wait_ge(S["e_ready"], 8 * b + u - 1)
                            v.tensor_scalar(nm8[:, sl, :], v8[:, 0, :, 0], -1.0, None, ALU.mult).then_inc(
                                S["negm_ready"], 1)
                            for h in range(8):
                                v.match_replace(W1[:, h, :], v8[:, 0, h, :], SX[:, sl, h, :], TAKEN).then_inc(top, 1)
                            for h in range(8):
                                held(dve, top, o + 9 + h)
                                v.max(v8[:, 1, h, :], W1[:, h, :]).then_inc(top, 1)
                            if u >= 2:
                                dve.wait_ge(S["pick_ready"], 8 * b + u - 1)
                            for h in range(8):
                                held(dve, top, o + 17 + h)
                                v.match_replace(W2[:, sl, h, :], v8[:, 1, h, :], W1[:, h, :], TAKEN).then_inc(
                                    S["w2_ready"] if h == 7 else top, 1)
                            held(dve, S["w2_ready"], 8 * b + u + 1)
                    normalise(attn(l, b, 1))
                    residual(l, b, 1)
                with dve.Fori(0, B) as b:
                    n = selfs(l, b)
                    norm(l, b, 2)
                    if l == 0:
                        for q in range(4):
                            dve.wait_ge(S["gate_ready"], 4 * n + q + 1)
                            v.scalar_tensor_tensor(HB[:, q, :], PS[:, 2 * (q % 2) + 1, :], col("b1_0", 4 + q),
                                                   HB[:, q, :], ALU.add, ALU.mult).then_inc(S["hid_ready"], 1)
                    residual(l, b, 2)

            dve.wait_ge(S["unrolled"], 16 * (1 + 2 * B))

            def normed(l, b, chain, k, XN_, st_, mv_, ve_, rstd_):
                for t in range(T):
                    v.bn_stats(st_[:, t, :], xs[:, T * b + t, :]).then_inc(S[chain + "_st"], 1)
                dve.wait_ge(S[chain + "_st"], 4 * k + 4)
                for t in range(T):
                    v.bn_aggr(mv_[:, t, :], st_[:, t, :]).then_inc(S[chain + "_ag"], 1)
                dve.wait_ge(S[chain + "_ag"], 4 * k + 4)
                v.tensor_scalar(ve_[:, :], mv_[:, :, 1], EPS[l], None, ALU.add).then_inc(S[chain + "_ve"], 1)

            def normed_out(b, chain, k, XN_, mv_, rstd_):
                dve.wait_ge(S[chain + "_rs"], k + 1)
                for t in range(T):
                    v.tensor_scalar(XN_[:, t, :], xs[:, T * b + t, :], mv_[:, t, 0:1], rstd_[:, t:t + 1],
                                    ALU.subtract, ALU.mult).then_inc(S[chain + "_xn"], 1)

            def added(b, chain, bank, k):
                xb = xs[:, T * b:T * b + T, :]
                dve.wait_ge(S[chain + "_yb"], k + 1)
                v.tensor_tensor(xb, PS[:, bank, :].rearrange("p (t c) -> p t c", t=T), xb, ALU.add).then_inc(
                    S[chain + "_x"], 1)
                dve.wait_ge(S[chain + "_x"], k + 1)

            def over_sums(chain, bank, half, k, ON_, rec_):
                rows = PS[:, bank, :].rearrange("p (t h e) -> p t h e", t=T, e=16)
                rr = rec_[:, 32 * half:32 * half + 32].rearrange("p (t h) -> p t h", t=T).unsqueeze(3)
                dve.wait_ge(S[chain + "_T"], k + 1)
                v.reciprocal(rr, rows[:, :, :, 8:9]).then_inc(S[chain + "_rec"], 1)
                dve.wait_ge(S[chain + "_rec"], k + 1)
                v.tensor_tensor(ON_[:, :, 64 * half:64 * half + 64].rearrange("p t (h d) -> p t h d", d=HD),
                                rows[:, :, :, 0:8], rr.broadcast_to([P, T, 8, HD]), ALU.mult).then_inc(
                    S[chain + "_on"], 1)

            def three_parts(src, dst, part, n):
                v.tensor_copy(dst[:, 0, :], src).then_inc(part, 1)
                dve.wait_ge(part, 4 * n + 1)
                v.tensor_tensor(src, src, dst[:, 0, :], ALU.subtract).then_inc(part, 1)
                dve.wait_ge(part, 4 * n + 2)
                v.tensor_copy(dst[:, 1, :], src).then_inc(part, 1)
                dve.wait_ge(part, 4 * n + 3)
                v.tensor_tensor(dst[:, 2, :], src, dst[:, 1, :], ALU.subtract).then_inc(part, 1)

            def maxima_parts(mneg_, m3_, step_, n):
                src = mneg_[:, :, :].rearrange("p t (j i) -> p t i j", i=2)
                v.tensor_copy(m3_[:, :, :, 0, :], src).then_inc(step_, 1)
                dve.wait_ge(step_, 4 * n + 1)
                v.tensor_tensor(src, src, m3_[:, :, :, 0, :], ALU.subtract).then_inc(step_, 1)
                dve.wait_ge(step_, 4 * n + 2)
                v.tensor_copy(m3_[:, :, :, 1, :], src).then_inc(step_, 1)
                dve.wait_ge(step_, 4 * n + 3)
                v.tensor_tensor(m3_[:, :, :, 2, :], src, m3_[:, :, :, 1, :], ALU.subtract).then_inc(step_, 1)

            for s in SLOTS:
                n1, n2, n3 = s - 1, s - 2, s + 2
                (l1, b1), (l2, b2), (l3, b3) = item(n1), item(n2), item(n3)
                for p in range(POINTS):
                    if item(s + 1)[0]:
                        n = s + 1
                        for a in range(maxima_at(p), maxima_at(p + 1)):
                            dve.wait_ge(S["a_ready"], 64 * n + a + 1)
                            i, t, j = unit_a(a)
                            v.tensor_reduce(mneg[:, t, 2 * j + i:2 * j + i + 1], PS[:, BANK_A[a % 2], :], AX.X,
                                            ALU.max, negate=True).then_inc(S["a_used"], 1)
                        if p == A_TO:
                            dve.wait_ge(S["a_used"], 64 * n + 64)
                            maxima_parts(mneg, m3, S["a_m"], n)
                    if l1:
                        if p in (5, 8):
                            over_sums("c1", BANK_1, p // 8, 2 * n1 + p // 8, XN1, rec)
                        if p == 15:
                            added(b1, "c1", BANK_1, n1)
                            normed(l1, b1, "c1", n1, XN1, st, mv, ve, rstd)
                        if p == 18:
                            normed_out(b1, "c1", n1, XN1, mv, rstd)
                        if p == 24:
                            dve.wait_ge(S["x_q"], n1 + 1)
                            if n1:
                                dve.wait_ge(S["x_in"], 96 * n1)
                            three_parts(QX32, qxp, S["x_part"], n1)
                    if l1:
                        if XA_FROM <= p < XA_FROM + 16:
                            u = p - XA_FROM
                            i, t, half = u // 8, u // 2 % 4, u % 2
                            dve.wait_ge(S["xa_ready"], 16 * n1 + u + 1)
                            v.tensor_reduce(mnegx[:, t, 8 * half:8 * half + 8].rearrange("p (j i) -> p i j", i=2)[:, i],
                                            PS[:, BANK_1, 0:4 * NC].rearrange("p (j n) -> p j n", n=NC), AX.X,
                                            ALU.max, negate=True).then_inc(S["xa_used"], 1)
                        if p == XA_FROM + 16:
                            dve.wait_ge(S["xa_used"], 16 * n1 + 16)
                            maxima_parts(mnegx, m3x, S["xa_m"], n1)
                    if l2:
                        if p == 22:
                            for half in range(2):
                                over_sums("c2", BANK_2[half], half, 2 * n2 + half, XN2, rec2)
                        if p in (29, 46):
                            added(b2, "c2", BANK_2[0], 2 * n2 + p // 46)
                        if p == 29:
                            normed(l2, b2, "c2", order2("ff", n2), XN2, st2, mv2, ve2, rstd2)
                        if p == 32:
                            normed_out(b2, "c2", order2("ff", n2), XN2, mv2, rstd2)
                    if l3:
                        k = order2("front", n3)
                        if p == 47:
                            normed(l3, b3, "c2", k, XN2, st2, mv2, ve2, rstd2)
                        if p == 50:
                            normed_out(b3, "c2", k, XN2, mv2, rstd2)
                        if l3 == 1 and p in (55, 58):
                            which = (p - 55) // 3
                            tab = (ROPEQ, ROPE)[which]
                            dve.wait_ge(S["f_qkps"], 2 * n3 + which + 1)
                            if which:
                                dve.wait_ge(S["f_q"], n3 + 1)
                            elif n3:
                                dve.wait_ge(S["k_in"], 96 * n3)
                            v.tensor_tensor(RA, PS[:, BANK_2[0], :], tab[:, 0, :], ALU.mult).then_inc(S["f_rope"], 1)
                            v.tensor_tensor(RB, PS[:, BANK_2[1], :], tab[:, 1, :], ALU.mult).then_inc(S["f_rope"], 1)
                            dve.wait_ge(S["f_rope"], 4 * n3 + 2 * which + 2)
                            v.tensor_tensor(qk[:, which, :], RA, RB, ALU.add).then_inc(S[("f_q", "f_k")[which]], 1)
                        if p == 60:
                            dve.wait_ge(S["f_q"], n3 + 1)
                            if n3:
                                dve.wait_ge(S["q_in"], 96 * n3)
                            three_parts(qk[:, 0, :], qkp[:, 0, :, :], S["f_qpart"], n3)


PE_CTXT = 2
PE_K = [3, 5, 7, 9]
PE_V = [4, 6, 8, 10]
DVE_CTX = 7
DVE_VC = [74, 76]
PREP_VC = 78
DVE_MASK = 89
BQ = {0: 0, 2: 2, 3: 4}
A_FROM, A_TO = 8, 59
M_TURN = 60
XA_FROM, XM_TURN = 37, 55
U_HALF = 35


def qk_order():
    return np.array([8 * (2 * j + i) + d for i in range(2) for d in range(HD) for j in range(J)])


def out_order():
    return np.array([8 * (8 * s + hh) + d for hh in range(8) for s in range(2) for d in range(HD)])


def pack(inputs):
    g = {k: np.asarray(v) for k, v in inputs.items()}
    qo, oo = qk_order(), out_order()
    rot = np.array([c // HD * HD + (c % HD + HD // 2) % HD for c in range(C)])
    W, V = {}, {}
    L0, L1, L2, L3 = ("L%d_xcond_" % l for l in range(4))
    for l, (pre, wqkv) in enumerate(((L0, "w_qkv"), (L1, "qkv_W"), (None, None), (L3, "W_qkv"))):
        if pre:
            q = g[pre + wqkv]
            W[f"q{l}"], W[f"k{l}"], W[f"v{l}"] = q[:, :C][:, qo], q[:, C:2 * C][:, qo], q[:, 2 * C:]
            if l == 1:
                W["qrot1"], W["krot1"] = q[:, :C][:, rot][:, qo], q[:, C:2 * C][:, rot][:, qo]
    W["q2"], W["k2"], W["v2"] = g[L2 + "sa_wq"][:, qo], g[L2 + "sa_wk"][:, qo], g[L2 + "sa_wv"]
    for l, n in enumerate((L0 + "w_so", L1 + "attn_out_W", L2 + "sa_wo", L3 + "W_proj")):
        W[f"o{l}"] = g[n][oo]
    for l, n in enumerate((L0 + "w_co", L1 + "co_W", L2 + "ca_wo", L3 + "W_cproj")):
        W[f"co{l}"] = g[n][oo]
    for l, n in enumerate((L0 + "w_q", L1 + "cq_W", L2 + "ca_wq", L3 + "W_qc")):
        W[f"cq{l}"] = g[n][:, qo]
    W["ck0"], W["cv0"] = g[L0 + "w_kv"][:, :C][:, qo], g[L0 + "w_kv"][:, C:]
    W["ck1"], W["cv1"] = g[L1 + "ck_W"][:, qo], g[L1 + "cv_W"]
    W["ck2"], W["cv2"] = g[L2 + "ca_wk"][:, qo], g[L2 + "ca_wv"]
    W["ck3"], W["cv3"] = g[L3 + "W_kvc"][:, :C][:, qo], g[L3 + "W_kvc"][:, C:]
    ff = ((L0 + "w_m1", L0 + "w_m2"), (L1 + "mlp_W1", L1 + "mlp_W2"), (L2 + "w1", L2 + "w2"),
          (L3 + "W_mlp1", L3 + "W_mlp2"))
    for l, (a, b) in enumerate(ff):
        W[f"f1_{l}"] = g[a]
        W[f"f2_{l}"] = g[b].reshape(4, P, C).transpose(1, 0, 2).reshape(P, 4 * C)
    ada = {0: (L0 + "w_ada", L0 + "b_ada"), 1: (L1 + "adaLN_W", L1 + "adaLN_b"), 2: (L2 + "tp_w", L2 + "tp_b"),
           3: (L3 + "W_mod", L3 + "b_mod")}
    place = {"sh": 0, "sc": 1, "g": 2}
    aw, ab = [], []
    for l, kind, br in CHUNKS:
        n = br if l == 2 else 3 * (br // 2 if l == 3 else br) + place[kind]
        aw.append(g[ada[l][0]][:, n * C:(n + 1) * C])
        ab.append(g[ada[l][1]][n * C:(n + 1) * C])
    V["cond"] = g["cond_1024"].T
    V["adab"] = np.stack(ab, 1)
    for l, n in ((0, L0 + "b_qkv"), (3, L3 + "b_qkv")):
        V[f"bq{l}"], V[f"bk{l}"], V[f"bv{l}"] = g[n][:C][qo], g[n][C:2 * C][qo], g[n][2 * C:][oo]
    V["bq2"], V["bk2"], V["bv2"] = g[L2 + "sa_bq"][qo], g[L2 + "sa_bk"][qo], g[L2 + "sa_bv"][oo]
    V["bo0"], V["bo2"], V["bo3"] = g[L0 + "b_so"], g[L2 + "sa_bo"], g[L3 + "b_proj"]
    V["bcq0"], V["bcq2"], V["bcq3"] = g[L0 + "b_q"][qo], g[L2 + "ca_bq"][qo], g[L3 + "b_qc"][qo]
    V["bck0"], V["bcv0"] = g[L0 + "b_kv"][:C][qo], g[L0 + "b_kv"][C:][oo]
    V["bck2"], V["bcv2"] = g[L2 + "ca_bk"][qo], g[L2 + "ca_bv"][oo]
    V["bck3"], V["bcv3"] = g[L3 + "b_kvc"][:C][qo], g[L3 + "b_kvc"][C:][oo]
    V["bco0"], V["bco2"], V["bco3"] = g[L0 + "b_co"], g[L2 + "ca_bo"], g[L3 + "b_cproj"]
    for l, (a, b) in enumerate(((L0 + "b_m1", L0 + "b_m2"), (L1 + "mlp_b1", L1 + "mlp_b2"), (L2 + "b1", L2 + "b2"),
                                (L3 + "b_mlp1", L3 + "b_mlp2"))):
        V[f"b1_{l}"], V[f"b2_{l}"] = g[a].reshape(-1, P).T, g[b]
    V["w1"] = np.stack([g[L1 + "norm1_w"], g[L1 + "normc_w"], g[L1 + "norm2_w"]], 1)
    V["w2"] = np.stack([g[L2 + "ln1_g"], g[L2 + "ln3_g"], g[L2 + "ln2_g"]], 1)
    V["lb2"] = np.stack([g[L2 + "ln1_b"], g[L2 + "ln3_b"], g[L2 + "ln2_b"]], 1)
    out = {}
    for name, table, parts in (("wpack", weight_table(), W), ("cols", column_table(), V)):
        at, width = table
        out[name] = np.zeros((P, width), np.float32)
        for n, (o, k) in at.items():
            out[name][:, o:o + k] = parts[n].reshape(P, k)
    out["ada_w"] = np.concatenate(aw, 1)
    out["x"] = np.roll(g["x"], -SHIFT, axis=1)
    out["ctx_t"] = g["ctx_1024"].transpose(2, 0, 1).reshape(C, B * NC)
    out["ctx_tok"] = g["ctx_1024"].transpose(1, 0, 2)
    out["mask_self"] = g["mask_SxS_bk0"].view(np.int32)
    out["mask1"] = g["mask_BxS2_bf1"].reshape(B * NC).view(np.int32)
    out["mask2"] = g["mask_BxS2_ik0"].reshape(B * NC)
    out["ident_in"] = np.eye(P, dtype=np.float32)
    half = L // 2
    inv = 1.0 / 10000.0 ** (np.arange(0, HD, 2, dtype=np.float32) / HD)
    freqs = np.outer(np.arange(half, dtype=np.float32), inv)
    emb = np.concatenate([freqs, freqs], axis=-1)
    cos, sin = np.cos(emb).astype(np.float32), np.sin(emb).astype(np.float32)
    d = qo % HD
    sign = np.where(d < HD // 2, -1.0, 1.0).astype(np.float32)[:, None]
    out["rope"] = np.stack([np.tile(cos.T[d], (1, 2)), sign * np.tile(sin.T[d], (1, 2))], 1)
    rows = np.full((4, J * L), 0x3F80, np.uint16)
    rows[0] = 0
    out["const_rows"] = rows
    return {k: np.ascontiguousarray(v) for k, v in out.items()}


_INS = ["x", "wpack", "ada_w", "cols", "ctx_t", "ctx_tok", "mask_self", "mask1", "mask2", "ident_in", "rope", "const_rows"]


def kernel(**inputs):
    import concourse.bacc as bacc
    from concourse.bass_utils import run_bass_kernel_spmd

    nc = bacc.Bacc("TRN2", target_bir_lowering=False, num_devices=1)
    laid = pack(inputs)
    arrays, args = {}, []
    for name in _INS:
        a = laid[name]
        arrays[f"in_{name}"] = a
        args.append(nc.dram_tensor(f"in_{name}", a.shape, mybir.dt.from_np(a.dtype), kind="ExternalInput").ap())
    args.append(nc.dram_tensor("out_x", (B, L, C), F32, kind="ExternalOutput").ap())
    build(nc, *args)
    r = run_bass_kernel_spmd(nc, [arrays], core_ids=[0])
    return r.results[0]["out_x"]
```

```python
from contextlib import ExitStack

import numpy as np
import concourse.bass as bass
import concourse.mybir as mybir

F32 = mybir.dt.float32
BF16 = mybir.dt.bfloat16
U8 = mybir.dt.uint8
I32 = mybir.dt.int32
ALU = mybir.AluOpType
ACT = mybir.ActivationFunctionType
AX = mybir.AxisListType

P = 128
B, L, C, H, HD = 4, 512, 128, 16, 8
T = L // P
NC = 77
WIN, SHIFT = 64, 32
HID = 512
NL = 4
J = H // 2
QUERY_PART = (0, 0, 0, 1, 1, 2)
KEY_PART = (0, 1, 2, 0, 1, 0)
ROWS = 8 * len(QUERY_PART)
ROW_MASK, ROW_MAX = ROWS, ROWS + 1
ROWS_FULL = ROWS + 4
QSCALE = float(1.0 / np.sqrt(np.float32(HD)))
MASKED = -1.0e30
TAKEN = -3.0e38
EPS = (1e-6, 1e-5, 1e-5, 1e-6)
FF_TILES = (8, 4, 4, 4)

CHUNKS = ([(l, kind, br) for l in (0, 1) for br in range(3) for kind in ("sh", "sc", "g")]
          + [(2, "t", br) for br in range(3)]
          + [(3, kind, br) for br in (0, 2) for kind in ("sh", "sc", "g")])


def weight_table():
    names = []
    for l in range(NL):
        names += [(f"q{l}", C), (f"k{l}", C), (f"v{l}", C), (f"o{l}", C)]
        if l == 1:
            names += [("qrot1", C), ("krot1", C)]
        names += [(f"cq{l}", C), (f"ck{l}", C), (f"cv{l}", C), (f"co{l}", C)]
        names += [(f"f1_{l}", FF_TILES[l] * P), (f"f2_{l}", HID)]
    at, off = {}, 0
    for n, w in names:
        at[n] = (off, w)
        off += w
    return at, off


def column_table():
    names = [("cond", B), ("adab", len(CHUNKS))]
    for l in (0, 2, 3):
        names += [(f"{n}{l}", 1) for n in ("bq", "bcq")]
    for l in (0, 2, 3):
        names += [(f"{n}{l}", 1) for n in ("bk", "bv", "bo", "bck", "bcv", "bco")]
    for l in range(NL):
        names += [(f"b1_{l}", FF_TILES[l]), (f"b2_{l}", 1)]
    names += [("w1", 3), ("w2", 3), ("lb2", 3)]
    at, off = {}, 0
    for n, w in names:
        at[n] = (off, w)
        off += w
    return at, off


def build(nc, x, wpack, ada_w, cols, ctx_t, ctx_tok, mask_self, mask1, mask2, ident_in, rope, const_rows, out):
    const_rows = const_rows.bitcast(BF16)
    WT, NW = weight_table()
    CT, NCOL = column_table()
    ctx = ExitStack()
    with ctx:
        def sb(name, shape, dt=F32):
            return ctx.enter_context(nc.sbuf_tensor(name, shape, dt))

        def sem(name):
            return ctx.enter_context(nc.semaphore(name))

        W = sb("weights", [P, NW])
        COL = sb("columns", [P, NCOL])
        ident = sb("ident", [P, P])
        identb = sb("identb", [P, P], BF16)
        xs = sb("x_state", [P, B * T, C])
        room = sb("room", [P, 9216])
        taken = [0]

        def early(n, dt=F32):
            width = n if dt != BF16 else (n + 1) // 2
            a = room[:, taken[0]:taken[0] + width]
            taken[0] += width
            assert taken[0] <= 9216
            return a if dt == F32 else a.bitcast(dt)

        ctxT = early(B * NC)
        ctxLT = early(B * NC)
        ctxK = early(B * C)[0:NC].rearrange("p (b c) -> p b c", c=C)
        kc32 = early(B * NC)
        kcp = early(3 * B * NC, BF16).rearrange("p (r n) -> p r n", r=3)
        mword = early(B * NC // 4, I32)
        mrow8 = mword.bitcast(U8)
        mrow32 = early(B * NC, I32)
        mkf = early(B * NC)
        ms32 = early(T * L // 4, I32).rearrange("p (t n) -> p t n", t=T)
        ms8 = ms32.bitcast(U8)
        diag = early(T * P).rearrange("p (t n) -> p t n", t=T)
        ones = early(P)
        assert taken[0] >= J * L // 2 + 2 * L
        xr = early(B * T * C).rearrange("p (t c) -> p t c", c=C)
        SX = early(16 * NC).rearrange("p (a h n) -> p a h n", a=2, h=8)
        W1 = early(8 * NC).rearrange("p (h n) -> p h n", h=8)
        W2 = early(16 * NC).rearrange("p (a h n) -> p a h n", a=2, h=8)
        taken[0] = 0
        QX0 = early(J * L, BF16).rearrange("p (j n) -> p j n", j=J)
        PC = early(2 * L)
        taken[0] = 0
        QS2 = early(J * L, BF16).rearrange("p (j n) -> p j n", j=J)
        KS2 = early(J * L, BF16).rearrange("p (j n) -> p j n", j=J)
        QX = early(J * L, BF16).rearrange("p (j n) -> p j n", j=J)
        QZ1 = early(J * L, BF16).rearrange("p (j n) -> p j n", j=J)
        qxp = early(3 * L, BF16).rearrange("p (r n) -> p r n", r=3)
        mTx = early(L, BF16)[0:48]
        scond = sb("silu_cond", [P, B])
        mod = sb("mod", [P, len(CHUNKS), B])
        cb = sb("out_bias", [P, 6])
        VEC = sb("vectors", [P, NL * B * 12])
        bqs = sb("q_bias_scaled", [P, 6])
        KC = sb("ctx_keys_stacked", [P, NL, J, B * NC], BF16)
        VC = sb("ctx_values", [NC, NL, B, C])
        mkany = sb("ctx_any", [P, B])
        poison = sb("ctx_none", [P, B])
        mkb = sb("ctx_mask_bias", [8, 2, B * NC], BF16)
        MB = sb("self_bias", [P, T, L], BF16)
        MBT = sb("self_bias_t", [P, T, L], BF16)
        rany = sb("row_any", [P, T])
        ROPE = sb("rope", [P, 2, L])
        ROPEQ = sb("rope_q", [P, 2, L])
        cst = sb("ctx_stats", [NC, B, 6])
        cmv = sb("ctx_mv", [NC, B, 2])
        cve = sb("ctx_ve", [NC, 2 * B])
        st = sb("stats", [P, T, 6])
        mv = sb("mv", [P, T, 2])
        ve = sb("ve", [P, T])
        rstd = sb("rstd", [P, T])
        mhalf = sb("minus_half", [P, T])
        XN = sb("x_normed", [P, T, C])
        hT = sb("h_channels", [P, L])
        qk = sb("qk", [P, 2, L])
        qkp = sb("qk_parts", [P, 2, 3, L], BF16)
        QS = sb("q_stacked", [P, J, L], BF16)
        KS = sb("k_stacked", [P, J, L], BF16)
        VA = sb("values", [P, T, H * 32])
        VX = sb("ctx_values_now", [NC, H * 32])
        mneg = sb("minus_max", [P, T, H])
        m3 = sb("max_parts", [P, T, 2, 3, J], BF16)
        mT = sb("max_rows", [48, L], BF16)
        PT = sb("probs", [P, 4, 2 * L])
        ADA = PT[:, :, :].rearrange("p a n -> p (a n)")
        U = sb("out_rows", [P, 2, L])
        rec = sb("recip", [P, T * H])
        ON = sb("out_normed", [P, T, C])
        OT = sb("out_channels", [P, L])
        YT = sb("y_channels", [P, L])
        HB = sb("hidden", [P, 4, L])
        HBF = HB[:, :, :].rearrange("p a n -> p (a n)")
        E = HBF[:, 0:16 * NC].rearrange("p (a h n) -> p a h n", a=2, h=8)
        v8 = sb("top8", [P, 2, 8, 8])
        nm8 = sb("topk_minus_max", [P, 2, 8])

        QZ0 = W[:, 0:J * L // 2].bitcast(BF16).rearrange("p (j n) -> p j n", j=J)
        QZs, KSs = ((QS, QZ0), (QS2, QZ1)), (KS, KS2)
        RA, RB = HB[:, 0, :], HB[:, 1, :]
        PX = HB
        GP = PT[:, :, :].rearrange("p a (g n) -> p (a g) n", g=2)
        XN1, XN2 = XN, ON
        QX32 = XN1[:, :, :].rearrange("p t c -> p (t c)")
        H1, H2, HF = hT, OT, YT
        HFs = (YT[:, :], W[:, J * L // 2:J * L // 2 + L])
        assert WT["f2_0"][0] + WT["f2_0"][1] >= J * L // 2 + L
        U2 = sb("cross_out_rows", [P, 2, L])
        mnegx = sb("cross_minus_max", [P, T, H])
        m3x = sb("cross_max_parts", [P, T, 2, 3, J], BF16)
        st2, mv2, ve2, rstd2 = (sb("stats2", [P, T, 6]), sb("mv2", [P, T, 2]), sb("ve2", [P, T]), sb("rstd2", [P, T]))
        rec2 = sb("recip2", [P, T * H])

        PS = ctx.enter_context(nc.psum_tensor("PS", [P, 8, 512], F32))
        M0, M1 = 6, 7
        M0B = PS[:, M0, :].bitcast(BF16)
        M1B = PS[:, M1, :].bitcast(BF16)

        names = """loaded x_loaded const_rows_in base_consts prep_act prep_pe prep_dve prep_kparts prep_stacked
            prep_mask_rows unrolled zf_st zf_ag zf_ve zf_rs zf_xn zf_xnT zf_h zf_yps zf_y
            zf_yb zf_x zf_gate_ps zf_gate zf_up_ps zf_hid silu_ready ctx_rstd_ready stats_ctx stored late_consts
            late_rows b_ready b_exp b_pv b_u a_ready a_used a_m a_mTps a_mT a_rows f_qkps f_rope f_q f_k f_qpart
            f_kpart k_in k_in0 q_in q_in0 v_ps v_in x_in0 c1_T c1_rec c1_on c1_onT c1_oT c1_yps c1_y c1_yb c1_x
            c1_st c1_ag c1_ve c1_rs c1_xn c1_xnT c1_h x_qps x_q x_part x_in xa_ready xa_used xa_m xa_mTps xa_mT
            xa_rows xb_kv xb_ready xb_exp xb_pv xb_u c2_T c2_rec c2_on c2_onT c2_oT c2_yps c2_y c2_yb c2_x c2_st
            c2_ag c2_ve c2_rs c2_xn c2_xnT c2_h ff_ps ff_hid z_q_in z_q_in0 z_k_in z_k_in0 z_x_in z_x_in0
            z_qk_ps z_q z_k z_qpart z_kpart z_v_ps z_v_in z_a_ready z_a_used z_m z_mTps z_mT z_rows z_b_ready
            z_p z_pv z_u z_xq_ps z_xq z_xpart z_kv z_u2 z2_T z2_rec z2_on z2_onT z2_oT z2_yps z2_y z2_yb z2_x
            t_scores t_sx t_step t_w2 t_negm t_e t_pick t_pw t_pT t_p t_pv""".split()
        S = {n: sem(n) for n in names}

        def w(name, a=0, n=None):
            o, width = WT[name]
            return W[:, o + a:o + (width if n is None else a + n)]

        def col(name, a=0):
            o, _ = CT[name]
            return COL[:, o + a:o + a + 1]

        SLOTS0 = range(-1, B + 2)
        POINTS0 = max(28 + Z_TURN + 3, Z_NORM[-1] + 1)
        BANK_S, BANK_T, BANK_U, BANK_Z = (0, 1), (2, 3), (4, 5), (6, 7)
        U0, QXP0 = U2, U[:, :, :].rearrange("p k n -> p (k n)").bitcast(BF16)[:, 0:3 * L].rearrange(
            "p (r n) -> p r n", r=3)

        def seq(b):
            return 0 <= b < B

        def order1(which, b):
            return b + max(0, b - 1) if which == "front" else b + min(b + 2, B)

        def forward_at(s):
            return FF_AT.get(s, ())

        def score_point(u):
            return (0, 1)[u] if u < 2 else 4 * u - 4

        N = (NL - 1) * B
        SLOTS = range(-2, N + 2)
        POINTS = 64
        QUADS = (0, 2, 1, 3)
        BANK_B, BANK_A, BANK_V, BANK_1, BANK_2 = (0, 1), (2, 3), 4, 5, (6, 7)

        LATE_QUERIES, LATE_KEYS, LATE_CROSS = 8, 9, 10

        def item(n):
            return (1 + n // B, n % B) if 0 <= n < N else (None, None)

        def maxima_at(p):
            return max(0, min(64, (p - A_FROM) * 64 // (A_TO - A_FROM)))

        def unit_a(a):
            return a // 32, a // 8 % 4, a % 8

        def vec(l, b, br, f):
            o = 12 * (B * l + b) + 4 * br + f
            return VEC[:, o:o + 1]

        def order2(which, n):
            if which == "ff":
                return n + min(n + 4, N)
            return n + max(0, n - 3)

        block = ctx.enter_context(nc.Block())

        @block.sync
        def _(sp):
            for dst, src in ((COL[:, :], cols), (ident[:, :], ident_in), (ctxT[:, :], ctx_t),
                             (W[:, :], wpack), (ADA[:, 0:len(CHUNKS) * C], ada_w),
                             (ctxK[:, :, :], ctx_tok), (ms32[:, :, :], mask_self.rearrange("(t p) k -> p t k", p=P)),
                             (mword[:, :], mask1.rearrange("(a n) -> a n", a=1).broadcast_to([P, B * NC // 4])),
                             (mrow32[:, :], mask2.rearrange("(a n) -> a n", a=1).broadcast_to([P, B * NC])),
                             (ROPE[:, :, :], rope)):
                sp.dma_start(dst, src).then_inc(S["loaded"], 16)
            for b in range(B):
                sp.dma_start(xr[:, T * b:T * b + T, :],
                             x[b].rearrange("(t p) c -> p t c", p=P)).then_inc(S["x_loaded"], 16)
            sp.wait_ge(S["base_consts"], 1)
            for i in range(2):
                r = 64 * i + ROW_MASK
                sp.dma_start(KS[r:r + 4, :, :], const_rows.rearrange("r (j n) -> r j n", j=J)).then_inc(
                    S["const_rows_in"], 16)
                for l in range(NL):
                    sp.dma_start(KC[r:r + 4, l, :, :],
                                 const_rows[:, 0:J * B * NC].rearrange("r (j n) -> r j n", j=J)).then_inc(
                        S["const_rows_in"], 16)
            for l in range(NL):
                for r, part in enumerate(KEY_PART):
                    sp.wait_ge(S["prep_kparts"], 4 * l + (1, 3, 4)[part])
                    for i in range(2):
                        sp.dma_start(KC[64 * i + 8 * r:64 * i + 8 * r + 8, l, :, :],
                                     kcp[64 * i:64 * i + 64, part, :]).then_inc(S["prep_stacked"], 16)
            sp.wait_ge(S["const_rows_in"], 16 * 2 * (1 + NL))
            sp.wait_ge(S["prep_mask_rows"], 2)
            for i in range(2):
                r = 64 * i + ROW_MASK
                for n in range(2):
                    sp.dma_start(KC[r:r + 1, 1 + n, :, :], mkb[:, n, :]).then_inc(S["prep_stacked"], 16)

            def stack_parts(dst, src, map_, ready, n, done, i):
                for part in range(3):
                    if i == 0:
                        sp.wait_ge(ready, 4 * n + (1, 3, 4)[part])
                    for r in range(len(map_)):
                        if map_[r] == part:
                            sp.dma_start(dst[64 * i + 8 * r:64 * i + 8 * r + 8, :, :],
                                         src[64 * i:64 * i + 64, part, :]).then_inc(done[i], 16)

            def max_rows_in(dst, rows, ready, n, done):
                sp.wait_ge(ready, n + 1)
                for i in range(2):
                    sp.dma_start(dst[i][64 * i + ROW_MAX:64 * i + ROW_MAX + 3, :, :],
                                 rows[24 * i:24 * i + 24, :]).then_inc(done, 16)

            for s in SLOTS0:
                if seq(s):
                    sp.wait_ge(S["z_mT"], s + 1)
                    for i in range(2):
                        sp.dma_start(QS[64 * i + ROW_MAX:64 * i + ROW_MAX + 3, :, :],
                                     mT[24 * i:24 * i + 24, :]).then_inc(S["z_rows"], 16)
                n = s + 1
                if seq(n):
                    if n:
                        sp.wait_ge(S["z_b_ready"], 4 * n)
                    for i in range(2):
                        stack_parts(QS, qkp[:, 0, :, :], QUERY_PART, S["z_qpart"], n, (S["z_q_in0"], S["z_q_in"]), i)
                        stack_parts(KS, qkp[:, 1, :, :], KEY_PART, S["z_kpart"], n, (S["z_k_in0"], S["z_k_in"]), i)
                if seq(s):
                    if s:
                        sp.wait_ge(S["t_scores"], 8 * s)
                    for i in range(2):
                        stack_parts(QX0, QXP0, QUERY_PART, S["z_xpart"], s, (S["z_x_in0"], S["z_x_in"]), i)
            sp.wait_ge(S["zf_x"], B)
            q = P - SHIFT
            sp.dma_start(xs[SHIFT:P, :, :], xr[0:q, :, :]).then_inc(S["unrolled"], 16)
            for b in range(B):
                sp.dma_start(xs[0:SHIFT, T * b + 1:T * b + T, :],
                             xr[q:P, T * b:T * b + T - 1, :]).then_inc(S["unrolled"], 16)
                sp.dma_start(xs[0:SHIFT, T * b:T * b + 1, :],
                             xr[q:P, T * b + T - 1:T * b + T, :]).then_inc(S["unrolled"], 16)
            for s in SLOTS:
                if 0 <= s + 1 < N:
                    n = s + 1
                    if n == 0:
                        sp.wait_ge(S["late_consts"], LATE_QUERIES)
                    if n == 1:
                        sp.wait_ge(S["late_consts"], LATE_KEYS)
                        for i in range(2):
                            r = 64 * i + ROW_MASK
                            sp.dma_start(KS2[r:r + 4, :, :], const_rows.rearrange("r (j n) -> r j n", j=J)).then_inc(
                                S["late_rows"], 16)
                    if n >= 2:
                        sp.wait_ge(S["b_ready"], 64 * (n - 1))
                    for i in range(2):
                        QZ = QZs[n % 2][i]
                        sp.dma_start(QZ[64 * i + ROW_MAX:64 * i + ROW_MAX + 3, :, :],
                                     QZ[64 * (1 - i):64 * (1 - i) + 3, :, :]).then_inc(S[("q_in0", "q_in")[i]], 16)
                        stack_parts(QZ, qkp[:, 0, :, :], QUERY_PART, S["f_qpart"], n, (S["q_in0"], S["q_in"]), i)
                        if i == 0:
                            for i2 in range(2):
                                stack_parts(KSs[n % 2], qkp[:, 1, :, :], KEY_PART, S["f_kpart"], n,
                                            (S["k_in0"], S["k_in"]), i2)
                if 0 <= s - 1 < N:
                    n = s - 1
                    if n:
                        sp.wait_ge(S["xb_ready"], 16 * n)
                    else:
                        sp.wait_ge(S["late_consts"], LATE_CROSS)
                    for i in range(2):
                        stack_parts(QX, qxp, QUERY_PART, S["x_part"], n, (S["x_in0"], S["x_in"]), i)
                    max_rows_in((QX, QX), mTx, S["xa_mT"], n, S["xa_rows"])
                if 0 <= s + 1 < N:
                    max_rows_in(QZs[(s + 1) % 2], mT, S["a_mT"], s + 1, S["a_rows"])
                if B * (NL - 2) <= s - 2 < N:
                    b = s - 2 - B * (NL - 2)
                    sp.wait_ge(S["c2_x"], 2 * (s - 1))
                    sp.dma_start(out[b].rearrange("(t p) c -> p t c", p=P), xs[:, T * b:T * b + T, :]).then_inc(
                        S["stored"], 16)
            sp.wait_ge(S["stored"], 16 * B)

        @block.gpsimd
        def _(pool):
            g = nc.gpsimd
            g.memset(KS[:, :, :], 0.0).then_inc(S["base_consts"], 1)
            g.memset(mhalf[:, :], -0.5).then_inc(S["base_consts"], 1)
            g.memset(QS[:, :, :], 1.0).then_inc(S["base_consts"], 1)
            g.memset(VX[:, :], 0.0).then_inc(S["base_consts"], 1)
            g.memset(VA[:, :, :], 0.0).then_inc(S["base_consts"], 1)
            g.memset(ones[:, :], 1.0).then_inc(S["base_consts"], 1)
            pool.wait_ge(S["base_consts"], 5)
            for s in range(2):
                VAv = VA[:, :, 256 * s:256 * s + 256].rearrange("p t (h e) -> p t h e", e=32)
                g.memset(VAv[:, :, :, 16 * s + 8:16 * s + 16], 1.0).then_inc(S["base_consts"], 1)
                VXv = VX[:, 256 * s:256 * s + 256].rearrange("p (h e) -> p h e", e=32)
                g.memset(VXv[:, :, 16 * s + 8:16 * s + 16], 1.0).then_inc(S["base_consts"], 1)
            pool.wait_ge(S["prep_dve"], 1)
            pool.wait_ge(S["base_consts"], 2)
            g.tensor_tensor(cve[:, B:2 * B], cve[:, 0:B], mhalf[0:NC, :], ALU.pow).then_inc(S["ctx_rstd_ready"], 1)

            def deviation(ready, done, ve_, rstd_, k):
                pool.wait_ge(ready, k + 1)
                g.tensor_tensor(rstd_[:, :], ve_[:, :], mhalf[:, :], ALU.pow).then_inc(done, 1)

            def key_parts(n, base, made):
                k32, kp = qk[:, 1, :], qkp[:, 1, :, :]
                if base == 0:
                    g.tensor_copy(kp[:, 0, :], k32).then_inc(made, 1)
                else:
                    pool.wait_ge(made, 4 * n + base)
                    if base == 1:
                        g.tensor_tensor(k32, k32, kp[:, 0, :], ALU.subtract).then_inc(made, 1)
                    if base == 2:
                        g.tensor_copy(kp[:, 1, :], k32).then_inc(made, 1)
                    if base == 3:
                        g.tensor_tensor(kp[:, 2, :], k32, kp[:, 1, :], ALU.subtract).then_inc(made, 1)

            def zeros_and_ones(buffer, i, n):
                for rows, value in ((slice(64 * (1 - i), 64 * (2 - i)), 0.0), (slice(64 * i, 64 * i + 64), 1.0)):
                    if n:
                        pool.wait_ge(S["late_consts"], n)
                    g.memset(buffer[rows, :, :], value).then_inc(S["late_consts"], 1)
                    n += 1

            for s in SLOTS0:
                c = s - 1
                for p in range(POINTS0):
                    if s == B + 1 and p == 0:
                        pool.wait_ge(S["z_b_ready"], 4 * B)
                        pool.wait_ge(S["t_pw"], 8 * B)
                        zeros_and_ones(QS, 0, 0)
                        pool.wait_ge(S["late_consts"], 2)
                    for e, p0 in forward_at(s):
                        if p == p0 + 1:
                            deviation(S["zf_ve"], S["zf_rs"], ve2, rstd2, e)
                            if e == B - 1:
                                pool.wait_ge(S["t_pT"], 8 * B)
                                pool.wait_ge(S["t_e"], 8 * B)
                                pool.wait_ge(S["zf_rs"], B)
                                zeros_and_ones(QS2, 0, 2)
                                zeros_and_ones(QZ1, 1, 4)
                    if seq(c) and p == 0:
                        if c == 0:
                            pool.wait_ge(S["prep_dve"], PREP_VC)
                            pool.wait_ge(S["base_consts"], 10)
                        else:
                            pool.wait_ge(S["t_pv"], 8 * c)
                        for s2 in range(2):
                            src = VC[:, 0, c, 64 * s2:64 * s2 + 64].rearrange("p (h d) -> p h d", d=HD)
                            dst = VX[:, 256 * s2:256 * s2 + 256].rearrange("p (h e) -> p h e", e=32)
                            if s2:
                                pool.wait_ge(S["z_kv"], 2 * c + 1)
                            g.tensor_copy(dst[:, :, 16 * s2:16 * s2 + 8], src).then_inc(S["z_kv"], 1)
                        pool.wait_ge(S["z_kv"], 2 * c + 2)
                    if seq(s + 1):
                        if p == Z_FRONT[1]:
                            deviation(S["c1_ve"], S["c1_rs"], ve2, rstd2, order1("front", s + 1))
                        if Z_KPART <= p < Z_KPART + 4:
                            if p == Z_KPART:
                                pool.wait_ge(S["z_k"], s + 2)
                                if s + 1:
                                    pool.wait_ge(S["z_k_in"], 96 * (s + 1))
                            key_parts(s + 1, p - Z_KPART, S["z_kpart"])
                    if seq(s) and p == Z_NORM[0]:
                        deviation(S["c1_ve"], S["c1_rs"], ve, rstd, order1("cross", s))
                    if seq(c) and p % 4 == 3 and p < 32:
                        u = 8 * c + p // 4
                        pool.wait_ge(S["t_w2"], u + 1)
                        pw = W2[:, u % 2, :, :]
                        g.tensor_scalar(pw, pw, TAKEN / 2, None, ALU.is_le).then_inc(S["t_pick"], 1)
                        pool.wait_ge(S["t_pick"], u + 1)
                        pool.wait_ge(S["t_e"], u + 1)
                        g.tensor_tensor(pw, pw, E[:, u % 2, :, :], ALU.mult).then_inc(S["t_pw"], 1)

            pool.wait_ge(S["zf_yps"], B)
            zeros_and_ones(QZ0, 1, 6)
            pool.wait_ge(S["late_consts"], LATE_QUERIES)

            for s in SLOTS:
                n = s - 2
                l, b = item(n)
                if l:
                    if n:
                        pool.wait_ge(S["xb_pv"], 4 * n)
                    for s2 in range(2):
                        src = VC[:, l, b, 64 * s2:64 * s2 + 64].rearrange("p (h d) -> p h d", d=HD)
                        dst = VX[:, 256 * s2:256 * s2 + 256].rearrange("p (h e) -> p h e", e=32)
                        if s2:
                            pool.wait_ge(S["xb_kv"], 2 * n + 1)
                        g.tensor_copy(dst[:, :, 16 * s2:16 * s2 + 8], src).then_inc(S["xb_kv"], 1)
                    pool.wait_ge(S["xb_kv"], 2 * n + 2)
                if s == -1:
                    pool.wait_ge(S["unrolled"], 16 * (1 + 2 * B))
                    g.memset(KS2, 0.0).then_inc(S["late_consts"], 1)
                    pool.wait_ge(S["late_consts"], LATE_KEYS)
                    g.memset(QX, 1.0).then_inc(S["late_consts"], 1)
                    pool.wait_ge(S["late_consts"], LATE_CROSS)
                if item(s - 1)[0]:
                    deviation(S["c1_ve"], S["c1_rs"], ve, rstd, s - 1 + 2 * B)
                if l:
                    deviation(S["c2_ve"], S["c2_rs"], ve2, rstd2, order2("ff", n))
                n = s + 2
                if item(n)[0]:
                    deviation(S["c2_ve"], S["c2_rs"], ve2, rstd2, order2("front", n))
                    pool.wait_ge(S["f_k"], n + 1)
                    if n:
                        pool.wait_ge(S["k_in"], 96 * n)
                    k32, kp = qk[:, 1, :], qkp[:, 1, :, :]
                    g.tensor_copy(kp[:, 0, :], k32).then_inc(S["f_kpart"], 1)
                    pool.wait_ge(S["f_kpart"], 4 * n + 1)
                    g.tensor_tensor(k32, k32, kp[:, 0, :], ALU.subtract).then_inc(S["f_kpart"], 1)
                    pool.wait_ge(S["f_kpart"], 4 * n + 2)
                    g.tensor_copy(kp[:, 1, :], k32).then_inc(S["f_kpart"], 1)
                    pool.wait_ge(S["f_kpart"], 4 * n + 3)
                    g.tensor_tensor(kp[:, 2, :], k32, kp[:, 1, :], ALU.subtract).then_inc(S["f_kpart"], 1)

        @block.scalar
        def _(act):
            a_ = nc.scalar
            act.wait_ge(S["loaded"], 16 * 10)
            a_.activation(scond[:, :], COL[:, CT["cond"][0]:CT["cond"][0] + B], ACT.Silu).then_inc(S["silu_ready"], 1)
            act.wait_ge(S["prep_pe"], PE_CTXT)
            a_.activation(ctxLT[:, :], PS[:, M1, 0:B * NC], ACT.Identity).then_inc(S["prep_act"], 1)
            for l in range(NL):
                act.wait_ge(S["prep_pe"], PE_K[l])
                if l:
                    act.wait_ge(S["prep_kparts"], 4 * l)
                a_.activation(kc32[:, :], PS[:, l, 0:B * NC], ACT.Identity,
                              bias=(0.0 if l == 1 else col(f"bck{l}"))).then_inc(S["prep_act"], 1)

            def out_of(dst, src, done, bias=0.0, scale=1.0):
                a_.activation(dst, src, ACT.Identity, bias=bias, scale=scale).then_inc(done, 1)

            def rows_out(dst, bank, ready, n, done):
                act.wait_ge(ready, n + 1)
                out_of(dst[:, :], PS[:, bank, :].bitcast(BF16)[0:48, 0:L], done)

            def self_exp(n, p):
                u, grp = 64 * n + p, 16 * n + p // 4
                act.wait_ge(S["b_ready"], u + 1)
                if p % 4 == 0 and grp >= 2:
                    act.wait_ge(S["b_pv"], grp - 1)
                a_.activation(GP[:, 4 * (grp % 2) + p % 4, :], PS[:, BANK_B[p % 2], :], ACT.Exp).then_inc(
                    S["b_exp"], 1)

            def cross_exp(n, h):
                act.wait_ge(S["xb_ready"], 16 * n + h + 1)
                if h % 4 == 0 and 4 * n + h // 4 >= 1:
                    act.wait_ge(S["xb_pv"], 4 * n + h // 4)
                a_.activation(PX[0:NC, h % 4, :], PS[0:NC, BANK_2[0], :], ACT.Exp).then_inc(S["xb_exp"], 1)

            def gelus(l, n, half):
                act.wait_ge(S["ff_ps"], 4 * n + 2 * half + 2)
                for m in (2 * half, 2 * half + 1):
                    a_.activation(HB[:, m, :], PS[:, BANK_2[m % 2], :], ACT.Gelu if l == 2 else ACT.Gelu_apprx_tanh,
                                  bias=col(f"b1_{l}", m)).then_inc(S["ff_hid"], 1)

            for s in SLOTS0:
                c, e = s - 1, s - 2
                for p in range(POINTS0):
                    if seq(e):
                        if p == 0:
                            act.wait_ge(S["t_pv"], 8 * e + 8)
                            out_of(U0[:, :, :], PS[:, BANK_U[0]:BANK_U[1] + 1, :], S["z_u2"])
                        if p == 3:
                            act.wait_ge(S["z2_onT"], e + 1)
                            out_of(H1[:, :], PS[:, BANK_T[0], :], S["z2_oT"])
                        if p == 4:
                            act.wait_ge(S["z2_yps"], e + 1)
                            out_of(XN1[:, :, :].rearrange("p t c -> p (t c)"), PS[:, BANK_T[1], :], S["z2_y"],
                                   vec(0, e, 1, 3), vec(0, e, 1, 2))
                    if seq(s + 1):
                        n = s + 1
                        if p == Z_FRONT[3]:
                            act.wait_ge(S["c1_xnT"], order1("front", n) + 1)
                            out_of(HF[:, :], PS[:, BANK_Z[0], :], S["c1_h"], vec(0, n, 0, 1), vec(0, n, 0, 0))
                        if p == Z_FRONT[4]:
                            act.wait_ge(S["z_qk_ps"], n + 1)
                            if n:
                                act.wait_ge(S["z_k_in"], 96 * n)
                                act.wait_ge(S["z_kpart"], 4 * n)
                            out_of(qk[:, 0, :], PS[:, BANK_Z[0], :], S["z_q"], bqs[:, BQ[0]:BQ[0] + 1], QSCALE)
                            out_of(qk[:, 1, :], PS[:, BANK_Z[1], :], S["z_k"], col("bk0"))
                        if p == Z_V:
                            act.wait_ge(S["z_v_ps"], n + 1)
                            for s2 in range(2):
                                src = PS[:, BANK_Z[0], :].rearrange("p (t n) -> p t n", t=T)[:, :, 64 * s2:64 * s2 + 64]
                                dst = VA[:, :, 256 * s2:256 * s2 + 256].rearrange("p t (h e) -> p t h e", e=32)
                                out_of(dst[:, :, :, 16 * s2:16 * s2 + 8], src.rearrange("p t (h d) -> p t h d", d=8),
                                       S["z_v_in"])
                    if seq(s):
                        if p == Z_MAX[1]:
                            rows_out(mT, BANK_Z[0], S["z_mTps"], s, S["z_mT"])
                        if p - Z_LAG in Z_B:
                            t = Z_B.index(p - Z_LAG)
                            act.wait_ge(S["z_b_ready"], 4 * s + t + 1)
                            if s:
                                act.wait_ge(S["z_pv"], 4 * s)
                            a_.activation(PT[:, t, :].rearrange("p (a n) -> p a n", a=2),
                                          PS[:, BANK_Z[0]:BANK_Z[1] + 1, :], ACT.Exp).then_inc(S["z_p"], 1)
                        if p - Z_LAG in Z_PV:
                            k2, wd = divmod(Z_PV.index(p - Z_LAG), 2)
                            act.wait_ge(S["z_pv"], 4 * s + Z_PV.index(p - Z_LAG) + 1)
                            if s:
                                act.wait_ge(S["z_x_in"], 96 * s)
                            out_of(U[:, k2, :].rearrange("p (t w n) -> p t w n", t=T, w=2)[:, :, wd, :],
                                   PS[:, BANK_Z[wd], 0:4 * WIN].rearrange("p (t n) -> p t n", t=T), S["z_u"])
                        if p == Z_OUT[2]:
                            act.wait_ge(S["c1_onT"], s + 1)
                            out_of(H1[:, :], PS[:, BANK_Z[1], :], S["c1_oT"])
                        if p == Z_OUT[3]:
                            act.wait_ge(S["c1_yps"], s + 1)
                            out_of(XN1[:, :, :].rearrange("p t c -> p (t c)"), PS[:, BANK_Z[0], :], S["c1_y"],
                                   vec(0, s, 0, 3), vec(0, s, 0, 2))
                        if p == Z_NORM[2]:
                            act.wait_ge(S["c1_xnT"], order1("cross", s) + 1)
                            out_of(H1[:, :], PS[:, BANK_Z[0], :], S["c1_h"], vec(0, s, 1, 1), vec(0, s, 1, 0))
                        if p == Z_NORM[3]:
                            act.wait_ge(S["z_xq_ps"], s + 1)
                            out_of(QX32, PS[:, BANK_Z[1], :], S["z_xq"], bqs[:, BQ[0] + 1:BQ[0] + 2], QSCALE)
                    if seq(c):
                        for u in range(8):
                            n = 8 * c + u
                            if p == 4 * u + 2:
                                act.wait_ge(S["t_negm"], n + 1)
                                if n >= 2:
                                    act.wait_ge(S["t_pw"], n - 1)
                                for h in range(8):
                                    ins = a_.activation(E[:, u % 2, h, :], SX[:, u % 2, h, :], ACT.Exp,
                                                        bias=nm8[:, u % 2, h:h + 1])
                                ins.then_inc(S["t_e"], 1)
                            if p == score_point(u):
                                act.wait_ge(S["t_scores"], n + 1)
                                if n >= 2:
                                    act.wait_ge(S["t_w2"], n - 1)
                                    act.wait_ge(S["t_e"], n - 1)
                                a_.activation(SX[:, u % 2, :, :].rearrange("p (i j) n -> p i (j n)", i=2),
                                              PS[:, BANK_S[0]:BANK_S[1] + 1, 0:4 * NC], ACT.Identity).then_inc(
                                    S["t_sx"], 1)
                            if p == 4 * u + Z_TURN + 1:
                                act.wait_ge(S["t_pT"], n + 1)
                                if n:
                                    act.wait_ge(S["t_pv"], n)
                                a_.activation(PC[0:NC, :].rearrange("p (a n) -> p a n", a=2),
                                              PS[0:NC, BANK_T[0]:BANK_T[1] + 1, :], ACT.Identity).then_inc(S["t_p"], 1)
                    for e, p0 in forward_at(s):
                        if p == p0 + 2:
                            act.wait_ge(S["zf_xnT"], e + 1)
                            out_of(H2[:, :], PS[:, BANK_Z[0], :], S["zf_h"], vec(0, e, 2, 1), vec(0, e, 2, 0))
                        if p in (p0 + 3, p0 + 5):
                            m0 = p - p0 - 3
                            act.wait_ge(S["zf_gate_ps"], 4 * e + m0 + 2)
                            if e:
                                act.wait_ge(S["zf_yps"], e)
                            for m in (m0, m0 + 1):
                                a_.activation(PT[:, m, 0:L], PS[:, BANK_Z[m % 2], :], ACT.Silu,
                                              bias=col("b1_0", m)).then_inc(S["zf_gate"], 1)
                        if p == p0 + 7:
                            act.wait_ge(S["zf_yps"], e + 1)
                            out_of(XN2[:, :, :].rearrange("p t c -> p (t c)"), PS[:, BANK_Z[0], :], S["zf_y"],
                                   vec(0, e, 2, 3), vec(0, e, 2, 2))

            for s in SLOTS:
                n1, n2, n3 = s - 1, s - 2, s + 2
                (l1, b1), (l2, b2), (l3, b3) = item(n1), item(n2), item(n3)
                for p in range(POINTS):
                    if item(s + 1)[0]:
                        if p == M_TURN + 1:
                            rows_out(mT, BANK_A[0], S["a_mTps"], s + 1, S["a_mT"])
                    if l1 and p == XM_TURN + 1:
                        rows_out(mTx, BANK_1, S["xa_mTps"], n1, S["xa_mT"])
                    if item(s)[0] and p == 3:
                        act.wait_ge(S["v_ps"], s + 1)
                        if s:
                            act.wait_ge(S["b_pv"], 16 * s)
                        for s2 in range(2):
                            src = PS[:, BANK_2[1], :].rearrange("p (t n) -> p t n", t=T)[:, :, 64 * s2:64 * s2 + 64]
                            dst = VA[:, :, 256 * s2:256 * s2 + 256].rearrange("p t (h e) -> p t h e", e=32)
                            out_of(dst[:, :, :, 16 * s2:16 * s2 + 8], src.rearrange("p t (h d) -> p t h d", d=8),
                                   S["v_in"])
                    if item(s)[0]:
                        self_exp(s, p)
                        if p == U_HALF:
                            act.wait_ge(S["b_pv"], 16 * s + 8)
                            if s:
                                act.wait_ge(S["c1_T"], 2 * s + 2 * B)
                            out_of(U[:, 0, :], PS[:, BANK_V, :], S["b_u"])
                    if l1:
                        if p == 3:
                            act.wait_ge(S["b_pv"], 16 * n1 + 16)
                            out_of(U[:, 1, :], PS[:, BANK_V, :], S["b_u"])
                        if p == 11:
                            act.wait_ge(S["c1_onT"], n1 + 1 + B)
                            out_of(H1[:, :], PS[:, BANK_1, :], S["c1_oT"])
                        if p == 13:
                            act.wait_ge(S["c1_yps"], n1 + 1 + B)
                            out_of(XN1[:, :, :].rearrange("p t c -> p (t c)"), PS[:, BANK_1, :], S["c1_y"],
                                   vec(l1, b1, 0, 3), vec(l1, b1, 0, 2))
                        if p == 21:
                            act.wait_ge(S["c1_xnT"], n1 + 1 + 2 * B)
                            out_of(H1[:, :], PS[:, BANK_1, :], S["c1_h"], vec(l1, b1, 1, 1), vec(l1, b1, 1, 0))
                        if p == 23:
                            act.wait_ge(S["x_qps"], n1 + 1)
                            i = BQ.get(l1, 0) + 1
                            out_of(QX32, PS[:, BANK_1, :], S["x_q"], 0.0 if l1 == 1 else bqs[:, i:i + 1], QSCALE)
                    if l2:
                        quad, k = divmod(p, 5)
                        if quad < 4 and k < 4:
                            cross_exp(n2, 4 * quad + k)
                        if p in (10, 20):
                            act.wait_ge(S["xb_pv"], 4 * n2 + (2 if p == 10 else 4))
                            out_of(U2[:, p // 20, :], PS[:, BANK_2[1], :], S["xb_u"])
                        if p == 25:
                            act.wait_ge(S["c2_onT"], n2 + 1)
                            out_of(H2[:, :], PS[:, BANK_2[0], :], S["c2_oT"])
                        if p == 27:
                            act.wait_ge(S["c2_yps"], 2 * n2 + 1)
                            out_of(XN2[:, :, :].rearrange("p t c -> p (t c)"), PS[:, BANK_2[1], :], S["c2_y"],
                                   vec(l2, b2, 1, 3), vec(l2, b2, 1, 2))
                        if p == 35:
                            act.wait_ge(S["c2_xnT"], order2("ff", n2) + 1)
                            out_of(H2[:, :], PS[:, BANK_2[0], :], S["c2_h"], vec(l2, b2, 2, 1), vec(l2, b2, 2, 0))
                        if p in (38, 41):
                            gelus(l2, n2, (p - 38) // 3)
                        if p == 44:
                            act.wait_ge(S["c2_yps"], 2 * n2 + 2)
                            out_of(XN2[:, :, :].rearrange("p t c -> p (t c)"), PS[:, BANK_2[1], :], S["c2_y"],
                                   vec(l2, b2, 2, 3), vec(l2, b2, 2, 2))
                    if l3:
                        if p == 53:
                            act.wait_ge(S["c2_xnT"], order2("front", n3) + 1)
                            out_of(HFs[n3 % 2], PS[:, BANK_2[0], :], S["c2_h"], vec(l3, b3, 0, 1), vec(l3, b3, 0, 0))
                        if p == 55 and l3 != 1:
                            act.wait_ge(S["f_qkps"], 2 * n3 + 2)
                            i = BQ[l3]
                            if n3:
                                act.wait_ge(S["k_in"], 96 * n3)
                            out_of(qk[:, 0, :], PS[:, BANK_2[0], :], S["f_q"], bqs[:, i:i + 1], QSCALE)
                            out_of(qk[:, 1, :], PS[:, BANK_2[1], :], S["f_k"], col(f"bk{l3}"))

        @block.tensor
        def _(pe):
            t_ = nc.tensor

            def mm(o, a, m, start=True, stop=True, **kw):
                return t_.matmul(o, a, m, start=start, stop=stop, **kw)

            pe.wait_ge(S["loaded"], 16 * 10)
            pe.wait_ge(S["silu_ready"], 1)
            for n, (l, kind, br) in enumerate(CHUNKS):
                cond = COL[:, CT["cond"][0]:CT["cond"][0] + B] if l == 1 else scond[:, :]
                mm(PS[:, M0, B * n:B * n + B], ADA[:, C * n:C * n + C], cond)
            n0 = B * len(CHUNKS)
            for n, l in enumerate((0, 2, 3)):
                mm(PS[:, M0, n0 + 2 * n:n0 + 2 * n + 1], w(f"o{l}"), col(f"bv{l}"))
                ins = mm(PS[:, M0, n0 + 2 * n + 1:n0 + 2 * n + 2], w(f"co{l}"), col(f"bcv{l}"))
            ins.then_inc(S["prep_pe"], 1)
            pe.wait_ge(S["prep_dve"], DVE_CTX)
            for b in range(B):
                ins = t_.transpose(PS[:, M1, NC * b:NC * b + NC], ctxK[:, b, :], ident[0:NC, 0:NC])
            ins.then_inc(S["prep_pe"], 1)
            for l in range(NL):
                if l == 3:
                    pe.wait_ge(S["prep_act"], 1)
                src = ctxLT if l == 3 else ctxT
                mm(PS[:, l, 0:B * NC], w(f"ck{l}"), src[:, :]).then_inc(S["prep_pe"], 1)
                if l >= 2:
                    pe.wait_ge(S["prep_dve"], DVE_VC[l - 2])
                for b in range(B):
                    ins = mm(PS[0:NC, 4 + l % 2, C * b:C * b + C], src[:, NC * b:NC * b + NC], w(f"cv{l}"))
                ins.then_inc(S["prep_pe"], 1)
            pe.wait_ge(S["prep_dve"], DVE_MASK)
            for kt in range(T):
                for t in range(T):
                    dst = (M0B, M1B)[kt // 2]
                    o = 512 * (kt % 2) + P * t
                    ins = t_.transpose(dst[:, o:o + P], MB[:, t, P * kt:P * kt + P], identb[:, :])
            ins.then_inc(S["prep_pe"], 1)
            for t in range(T):
                ins = mm(PS[:, 4, P * t:P * t + P], ones[:, :], diag[:, t, :])
            ins.then_inc(S["prep_pe"], 1)

            def turned(dst, src_of, done):
                for t in range(T):
                    ins = t_.transpose(PS[:, dst, P * t:P * t + P], src_of(t), ident[:, :])
                ins.then_inc(done, 1)

            def scores_of(n, p):
                l, q, kt, g = 1 + n // B, QUADS[p // 16], p // 4 % 4, p % 4
                hd, u = 4 * q + g, 64 * n + p
                i, j = hd % 2, hd // 2
                if p == 0:
                    pe.wait_ge(S["a_rows"], 32 * (n + 1))
                if u >= 2:
                    pe.wait_ge(S["b_exp"], u - 1)
                ins = mm(PS[:, BANK_B[p % 2], :], KSs[n % 2][:, j, P * kt:P * kt + P], QZs[n % 2][i][:, j, :],
                         stop=l != 1)
                if l == 1:
                    ins = mm(PS[:, BANK_B[p % 2], :], identb[:, :], MBT[:, kt, :], start=False)
                ins.then_inc(S["b_ready"], 1)

            def maxima_of(n, a):
                l, u = 1 + n // B, 64 * n + a
                i, t, j = unit_a(a)
                if a % 32 == 0:
                    pe.wait_ge(S[("q_in0", "q_in")[i]], 112 * (n + 1))
                if a == 0:
                    pe.wait_ge(S["k_in0"], 96 * (n + 1))
                    pe.wait_ge(S["k_in"], 96 * (n + 1))
                    pe.wait_ge(S["late_consts"], LATE_QUERIES)
                    if n:
                        pe.wait_ge(S["late_rows"], 32)
                if u >= 2:
                    pe.wait_ge(S["a_used"], u - 1)
                ins = mm(PS[:, BANK_A[a % 2], :], QZs[n % 2][i][:, j, P * t:P * t + P], KSs[n % 2][:, j, :],
                         stop=l != 1)
                if l == 1:
                    ins = mm(PS[:, BANK_A[a % 2], :], identb[:, :], MB[:, t, :], start=False)
                ins.then_inc(S["a_ready"], 1)

            def values_of(n, grp, part):
                q, kt, u = QUADS[grp // 4], grp % 4, 16 * n + grp
                pe.wait_ge(S["b_exp"], 4 * u + 4)
                cols = slice(L // 2 * part, L // 2 * part + L // 2)
                if grp % 8 == 0 and u:
                    pe.wait_ge(S["b_u"], u // 8)
                if grp == 0:
                    pe.wait_ge(S["v_in"], 2 * n + 2)
                for g in range(4):
                    hd = 4 * q + g
                    ins = mm(PS[32 * g:32 * g + 32, BANK_V, cols], VA[:, kt, 32 * hd:32 * hd + 32],
                             GP[:, 4 * (u % 2) + g, cols], start=grp % 8 == 0 and part == 0,
                             stop=grp % 8 == 7 and part == 1, skip_group_check=True)
                if part:
                    ins.then_inc(S["b_pv"], 1)

            def cross_scores(n, h):
                l, b = item(n)
                hd, u = 4 * QUADS[h // 4] + h % 4, 16 * n + h
                i, j = hd % 2, hd // 2
                if h == 0:
                    pe.wait_ge(S["xa_rows"], 32 * (n + 1))
                    pe.wait_ge(S["f_q"], min(n + 4, N))
                    pe.wait_ge(S["f_k"], min(n + 4, N))
                if u:
                    pe.wait_ge(S["xb_exp"], u)
                r = slice(64 * i, 64 * i + ROWS_FULL)
                mm(PS[0:NC, BANK_2[0], :], KC[r, l, j, NC * b:NC * b + NC], QX[r, j, :]).then_inc(S["xb_ready"], 1)

            def cross_values(n, quad):
                q = QUADS[quad]
                pe.wait_ge(S["xb_exp"], 16 * n + 4 * quad + 4)
                if quad == 0:
                    pe.wait_ge(S["xb_kv"], 2 * n + 2)
                    pe.wait_ge(S["v_in"], 2 * min(n + 3, N))
                if quad == 2:
                    pe.wait_ge(S["xb_u"], 2 * n + 1)
                for g in range(4):
                    hd = 4 * q + g
                    ins = mm(PS[32 * g:32 * g + 32, BANK_2[1], :], VX[0:NC, 32 * hd:32 * hd + 32], PX[0:NC, g, :],
                             start=quad % 2 == 0, stop=quad % 2 == 1, skip_group_check=True)
                ins.then_inc(S["xb_pv"], 1)

            def cross_maxima(n, u):
                l, b = item(n)
                i, t, half = u // 8, u // 2 % 4, u % 2
                if u % 8 == 0:
                    pe.wait_ge(S[("x_in0", "x_in")[i]], 96 * (n + 1))
                if u:
                    pe.wait_ge(S["xa_used"], 16 * n + u)
                r = slice(64 * i, 64 * i + (ROWS + 1 if l in (1, 2) else ROWS))
                for jj in range(4):
                    j = 4 * half + jj
                    ins = mm(PS[:, BANK_1, NC * jj:NC * jj + NC], QX[r, j, P * t:P * t + P],
                             KC[r, l, j, NC * b:NC * b + NC])
                ins.then_inc(S["xa_ready"], 1)

            def parts_turned(parts, bank, ready, n, done):
                pe.wait_ge(ready, 4 * n + 4)
                dst = PS[:, bank, :].bitcast(BF16)
                for t in range(T):
                    ins = t_.transpose(dst[0:48, P * t:P * t + P],
                                       parts[:, t, :, :, :].rearrange("p i r j -> p (i r j)"), identb[:, :])
                ins.then_inc(done, 1)

            def window_values(n, half, wd):
                r = slice(64 * wd, 64 * wd + 64)
                for t in range(T):
                    for q in (half, half + 2):
                        for g in range(4):
                            hd = 4 * q + g
                            i, j = hd % 2, hd // 2
                            ins = mm(PS[32 * g:32 * g + 32, BANK_Z[wd], WIN * t:WIN * t + WIN],
                                     VA[r, t, 32 * hd:32 * hd + 32],
                                     PT[r, t, 512 * i + WIN * j:512 * i + WIN * j + WIN],
                                     start=t == 0 and q < 2, stop=t == T - 1 and q >= 2, skip_group_check=True)
                ins.then_inc(S["z_pv"], 1)

            def window_scores(a, m, rows, t, done):
                for i in range(2):
                    r = slice(64 * i, 64 * i + rows)
                    for j in range(J):
                        for wd in range(2):
                            q0 = P * t + WIN * wd
                            ins = mm(PS[64 * wd:64 * wd + 64, BANK_Z[i], WIN * j:WIN * j + WIN],
                                     a[r, j, q0:q0 + WIN], m[r, j, q0:q0 + WIN])
                ins.then_inc(done, 1)

            for s in SLOTS0:
                c, e = s - 1, s - 2
                for p in range(POINTS0):
                    if seq(e):
                        if p == 1:
                            pe.wait_ge(S["z_u2"], e + 1)
                            for half in range(2):
                                turned(BANK_T[half], lambda t: U0[:, half, P * t:P * t + P], S["z2_T"])
                        if p == 3:
                            pe.wait_ge(S["z2_on"], 2 * e + 2)
                            turned(BANK_T[0], lambda t: XN1[:, t, :], S["z2_onT"])
                        if p == 4:
                            pe.wait_ge(S["z2_oT"], e + 1)
                            mm(PS[:, BANK_T[1], :], w("co0"), H1[:, :]).then_inc(S["z2_yps"], 1)
                        if p == 5:
                            pe.wait_ge(S["z2_y"], e + 1)
                            turned(BANK_T[0], lambda t: XN1[:, :, :].rearrange("p t c -> p (t c)")[:, P * t:P * t + P],
                                   S["z2_yb"])
                    if seq(c):
                        for u in range(8):
                            n = 8 * c + u
                            if p == score_point(u):
                                t, part = divmod(u, 2)
                                if u == 0:
                                    pe.wait_ge(S["z_x_in0"], 96 * (c + 1))
                                    pe.wait_ge(S["z_x_in"], 96 * (c + 1))
                                    pe.wait_ge(S["prep_stacked"], 16 * (12 * NL + 4))
                                if n:
                                    pe.wait_ge(S["t_sx"], n)
                                for i in range(2):
                                    r = slice(64 * i, 64 * i + ROWS)
                                    for jj in range(4):
                                        j = 4 * part + jj
                                        ins = mm(PS[:, BANK_S[i], NC * jj:NC * jj + NC], QX0[r, j, P * t:P * t + P],
                                                 KC[r, 0, j, NC * c:NC * c + NC])
                                ins.then_inc(S["t_scores"], 1)
                            if p == 4 * u + Z_TURN:
                                pe.wait_ge(S["t_pw"], n + 1)
                                if n:
                                    pe.wait_ge(S["t_p"], n)
                                if u == 0 and c:
                                    pe.wait_ge(S["z2_x"], c)
                                for h in range(8):
                                    ins = t_.transpose(PS[0:NC, BANK_T[h // 4], P * (h % 4):P * (h % 4) + P],
                                                       W2[:, u % 2, h, :], ident[:, :])
                                ins.then_inc(S["t_pT"], 1)
                            if p == 4 * u + Z_TURN + 2:
                                t, part = divmod(u, 2)
                                pe.wait_ge(S["t_p"], n + 1)
                                if u == 0:
                                    pe.wait_ge(S["z_kv"], 2 * c + 2)
                                    if c:
                                        pe.wait_ge(S["z_u2"], c)
                                for h in range(8):
                                    hd = 8 * part + h
                                    i, jj = h % 2, h // 2
                                    g = hd % 4
                                    ins = mm(PS[32 * g:32 * g + 32, BANK_U[hd // 4 % 2], P * t:P * t + P],
                                             VX[0:NC, 32 * hd:32 * hd + 32],
                                             PC[0:NC, 512 * i + P * jj:512 * i + P * jj + P],
                                             start=u == 0, stop=u == 7, skip_group_check=True)
                                ins.then_inc(S["t_pv"], 1)
                    if seq(s):
                        if p in Z_A:
                            t = Z_A.index(p)
                            if t:
                                pe.wait_ge(S["z_a_used"], 4 * s + t)
                            else:
                                for name in ("z_q_in0", "z_q_in", "z_k_in0", "z_k_in"):
                                    pe.wait_ge(S[name], 96 * (s + 1))
                                pe.wait_ge(S["const_rows_in"], 16 * 2 * (1 + NL))
                                pe.wait_ge(S["z_v_in"], 2 * (s + 1))
                                if s:
                                    pe.wait_ge(S["z_xq"], s)
                            window_scores(QS, KS, ROWS, t, S["z_a_ready"])
                    if seq(s + 1):
                        n = s + 1
                        if p == Z_FRONT[3]:
                            if s >= 0:
                                pe.wait_ge(S["z_mT"], s + 1)
                            pe.wait_ge(S["c1_xn"], 4 * order1("front", n) + 4)
                            turned(BANK_Z[0], lambda t: XN2[:, t, :], S["c1_xnT"])
                        if p == Z_FRONT[4]:
                            pe.wait_ge(S["c1_h"], order1("front", n) + 1)
                            mm(PS[:, BANK_Z[0], :], w("q0"), HF[:, :])
                            mm(PS[:, BANK_Z[1], :], w("k0"), HF[:, :]).then_inc(S["z_qk_ps"], 1)
                    if seq(s):
                        if p == Z_MAX[1]:
                            parts_turned(m3, BANK_Z[0], S["z_m"], s, S["z_mTps"])
                        if p in Z_B:
                            t = Z_B.index(p)
                            if t:
                                pe.wait_ge(S["z_p"], 4 * s + t)
                            else:
                                pe.wait_ge(S["z_rows"], 32 * (s + 1))
                                pe.wait_ge(S["z_k"], min(s + 2, B))
                            window_scores(KS, QS, ROWS_FULL, t, S["z_b_ready"])
                        if p in Z_PV:
                            half, wd = divmod(Z_PV.index(p), 2)
                            pe.wait_ge(S["z_p"], 4 * s + 4)
                            if half:
                                pe.wait_ge(S["z_u"], 4 * s + wd + 1)
                            window_values(s, half, wd)
                    if seq(s + 1) and p == Z_V:
                        if s >= 0:
                            pe.wait_ge(S["z_u"], 4 * s + 3)
                        pe.wait_ge(S["z_q"], s + 2)
                        for t in range(T):
                            ins = mm(PS[:, BANK_Z[0], P * t:P * t + P], HF[:, P * t:P * t + P], w("v0"))
                        ins.then_inc(S["z_v_ps"], 1)
                    if seq(s):
                        if p == Z_OUT[0]:
                            pe.wait_ge(S["z_u"], 4 * s + 4)
                            turned(BANK_Z[1], lambda t: U[:, 0, P * t:P * t + P], S["c1_T"])
                        if p == Z_OUT[1]:
                            pe.wait_ge(S["z_v_in"], 2 * min(s + 2, B))
                            turned(BANK_Z[0], lambda t: U[:, 1, P * t:P * t + P], S["c1_T"])
                        if p == Z_OUT[2]:
                            pe.wait_ge(S["c1_on"], 2 * s + 2)
                            turned(BANK_Z[1], lambda t: XN1[:, t, :], S["c1_onT"])
                        if p == Z_OUT[3]:
                            pe.wait_ge(S["c1_oT"], s + 1)
                            mm(PS[:, BANK_Z[0], :], w("o0"), H1[:, :]).then_inc(S["c1_yps"], 1)
                        if p == Z_OUT[4]:
                            pe.wait_ge(S["c1_y"], s + 1)
                            turned(BANK_Z[1], lambda t: XN1[:, :, :].rearrange("p t c -> p (t c)")[:, P * t:P * t + P],
                                   S["c1_yb"])
                        if p == Z_NORM[2]:
                            pe.wait_ge(S["c1_xn"], 4 * order1("cross", s) + 4)
                            turned(BANK_Z[0], lambda t: XN1[:, t, :], S["c1_xnT"])
                        if p == Z_NORM[3]:
                            pe.wait_ge(S["c1_h"], order1("cross", s) + 1)
                            mm(PS[:, BANK_Z[1], :], w("cq0"), H1[:, :]).then_inc(S["z_xq_ps"], 1)

                    for e, p0 in forward_at(s):
                        if p == p0 + 2:
                            if e == 0:
                                pe.wait_ge(S["z_xq"], B)
                            pe.wait_ge(S["zf_xn"], 4 * e + 4)
                            turned(BANK_Z[0], lambda t: XN2[:, t, :], S["zf_xnT"])
                        if p in (p0 + 3, p0 + 5):
                            m0 = p - p0 - 3
                            pe.wait_ge(S["zf_h"], e + 1)
                            if m0:
                                pe.wait_ge(S["zf_hid"], 4 * e + 2)
                            for m in (m0, m0 + 1):
                                mm(PS[:, BANK_Z[m % 2], :], w("f1_0", P * m, P), H2[:, :]).then_inc(S["zf_gate_ps"], 1)
                        if p in (p0 + 4, p0 + 6):
                            m0 = p - p0 - 4
                            pe.wait_ge(S["zf_gate"], 4 * e + m0 + 2)
                            for m in (m0, m0 + 1):
                                mm(PS[:, BANK_Z[m % 2], :], w("f1_0", P * (4 + m), P), H2[:, :]).then_inc(
                                    S["zf_up_ps"], 1)
                        if p == p0 + 7:
                            pe.wait_ge(S["zf_hid"], 4 * e + 4)
                            for m in range(4):
                                ins = mm(PS[:, BANK_Z[0], :], w("f2_0", C * m, C), PT[:, m, 0:L], start=m == 0,
                                         stop=m == 3)
                            ins.then_inc(S["zf_yps"], 1)
                        if p == p0 + 8:
                            pe.wait_ge(S["zf_y"], e + 1)
                            turned(BANK_Z[0], lambda t: XN2[:, :, :].rearrange("p t c -> p (t c)")[:, P * t:P * t + P],
                                   S["zf_yb"])

            for s in SLOTS:
                n1, n2, n3 = s - 1, s - 2, s + 2
                (l1, b1), (l2, b2), (l3, b3) = item(n1), item(n2), item(n3)
                for p in range(POINTS):
                    if item(s)[0]:
                        scores_of(s, p)
                        if p == 0:
                            pe.wait_ge(S["f_k"], min(s + 2, N))
                            for t in range(T):
                                ins = mm(PS[:, BANK_2[1], P * t:P * t + P], HFs[s % 2][:, P * t:P * t + P],
                                         w(f"v{item(s)[0]}"))
                            ins.then_inc(S["v_ps"], 1)
                    if item(s + 1)[0]:
                        for a in range(maxima_at(p), maxima_at(p + 1))[:1]:
                            maxima_of(s + 1, a)
                        if p == M_TURN:
                            parts_turned(m3, BANK_A[0], S["a_m"], s + 1, S["a_mTps"])
                    if item(s)[0] and p % 4 in (1, 3) and p >= 5:
                        values_of(s, p // 4 - 1, p % 4 // 2)
                    if l1:
                        if p in (1, 2):
                            values_of(n1, 15, p - 1)
                        if p in (4, 7):
                            half = p // 7
                            pe.wait_ge(S["b_u"], 2 * n1 + 1 + half)
                            if half:
                                pe.wait_ge(S["c1_on"], 2 * n1 + 1 + 2 * B)
                            elif n1:
                                pe.wait_ge(S["xa_mT"], n1)
                            turned(BANK_1, lambda t: U[:, half, P * t:P * t + P], S["c1_T"])
                        if p == 10:
                            pe.wait_ge(S["c1_on"], 2 * n1 + 2 + 2 * B)
                            turned(BANK_1, lambda t: XN1[:, t, :], S["c1_onT"])
                        if p == 12:
                            pe.wait_ge(S["c1_oT"], n1 + 1 + B)
                            mm(PS[:, BANK_1, :], w(f"o{l1}"), H1[:, :]).then_inc(S["c1_yps"], 1)
                        if p == 14:
                            pe.wait_ge(S["c1_y"], n1 + 1 + B)
                            turned(BANK_1, lambda t: XN1[:, :, :].rearrange("p t c -> p (t c)")[:, P * t:P * t + P],
                                   S["c1_yb"])
                        if p == 20:
                            pe.wait_ge(S["c1_xn"], 4 * n1 + 4 + 8 * B)
                            turned(BANK_1, lambda t: XN1[:, t, :], S["c1_xnT"])
                        if p == 22:
                            pe.wait_ge(S["c1_h"], n1 + 1 + 2 * B)
                            mm(PS[:, BANK_1, :], w(f"cq{l1}"), H1[:, :]).then_inc(S["x_qps"], 1)
                    if l1:
                        if XA_FROM <= p < XA_FROM + 16:
                            cross_maxima(n1, p - XA_FROM)
                        if p == XM_TURN:
                            parts_turned(m3x, BANK_1, S["xa_m"], n1, S["xa_mTps"])
                    if l2:
                        quad, k = divmod(p, 5)
                        if quad < 4 and k < 4:
                            cross_scores(n2, 4 * quad + k)
                        elif quad < 4:
                            cross_values(n2, quad)
                        if p == 21:
                            pe.wait_ge(S["xb_u"], 2 * n2 + 2)
                            turned(BANK_2[0], lambda t: U2[:, 0, P * t:P * t + P], S["c2_T"])
                            turned(BANK_2[1], lambda t: U2[:, 1, P * t:P * t + P], S["c2_T"])
                        if p == 24:
                            pe.wait_ge(S["c2_on"], 2 * n2 + 2)
                            turned(BANK_2[0], lambda t: XN2[:, t, :], S["c2_onT"])
                        if p == 26:
                            pe.wait_ge(S["c2_oT"], n2 + 1)
                            mm(PS[:, BANK_2[1], :], w(f"co{l2}"), H2[:, :]).then_inc(S["c2_yps"], 1)
                        if p in (28, 45):
                            pe.wait_ge(S["c2_y"], 2 * n2 + 1 + p // 45)
                            turned(BANK_2[0], lambda t: XN2[:, :, :].rearrange("p t c -> p (t c)")[:, P * t:P * t + P],
                                   S["c2_yb"])
                        if p == 34:
                            pe.wait_ge(S["c2_xn"], 4 * order2("ff", n2) + 4)
                            turned(BANK_2[0], lambda t: XN2[:, t, :], S["c2_xnT"])
                        if p in (36, 39):
                            half = (p - 36) // 3
                            if half:
                                pe.wait_ge(S["ff_hid"], 4 * n2 + 2)
                            else:
                                pe.wait_ge(S["c2_h"], order2("ff", n2) + 1)
                            for m in (2 * half, 2 * half + 1):
                                mm(PS[:, BANK_2[m % 2], :], w(f"f1_{l2}", P * m, P), H2[:, :]).then_inc(S["ff_ps"], 1)
                        if p == 42:
                            pe.wait_ge(S["ff_hid"], 4 * n2 + 4)
                            for m in range(4):
                                ins = mm(PS[:, BANK_2[1], :], w(f"f2_{l2}", C * m, C), HB[:, m, :], start=m == 0,
                                         stop=m == 3)
                            ins.then_inc(S["c2_yps"], 1)
                    if l3:
                        if p == 52:
                            pe.wait_ge(S["c2_xn"], 4 * order2("front", n3) + 4)
                            turned(BANK_2[0], lambda t: XN2[:, t, :], S["c2_xnT"])
                        if p == 54:
                            pe.wait_ge(S["c2_h"], order2("front", n3) + 1)
                            if l3 != 1:
                                mm(PS[:, BANK_2[0], :], w(f"q{l3}"), HFs[n3 % 2]).then_inc(S["f_qkps"], 1)
                                mm(PS[:, BANK_2[1], :], w(f"k{l3}"), HFs[n3 % 2]).then_inc(S["f_qkps"], 1)
                        if p in (54, 57) and l3 == 1:
                            a, c = ("q1", "qrot1") if p == 54 else ("k1", "krot1")
                            if p == 57:
                                pe.wait_ge(S["f_rope"], 4 * n3 + 2)
                            mm(PS[:, BANK_2[0], :], w(a), HFs[n3 % 2])
                            mm(PS[:, BANK_2[1], :], w(c), HFs[n3 % 2]).then_inc(S["f_qkps"], 1)
                    if item(s + 1)[0]:
                        for a in range(maxima_at(p), maxima_at(p + 1))[1:]:
                            maxima_of(s + 1, a)

        @block.vector
        def _(dve):
            v = nc.vector
            done = [0]

            def step(ins):
                done[0] += 1
                ins.then_inc(S["prep_dve"], 1)
                return done[0]

            def after(n):
                dve.wait_ge(S["prep_dve"], n)

            dve.wait_ge(S["loaded"], 16 * 10)
            stats = S["stats_ctx"]
            for b in range(B):
                v.bn_stats(cst[:, b, :], ctxK[:, b, :]).then_inc(stats, 1)
            for b in range(B):
                dve.wait_ge(stats, b + 1)
                v.bn_aggr(cmv[:, b, :], cst[:, b, :]).then_inc(stats, 1)
            dve.wait_ge(stats, 2 * B)
            assert step(v.tensor_scalar(cve[:, 0:B], cmv[:, :, 1], EPS[3], None, ALU.add)) == 1
            o, _ = CT["bq0"]
            step(v.tensor_scalar(bqs[:, :], COL[:, o:o + 6], QSCALE, None, ALU.mult))
            step(v.tensor_copy(identb[:, :], ident[:, :]))
            dve.wait_ge(S["ctx_rstd_ready"], 1)
            for b in range(B):
                step(v.tensor_scalar(ctxK[:, b, :], ctxK[:, b, :], cmv[:, b, 0:1], cve[:, B + b:B + b + 1],
                                     ALU.subtract, ALU.mult))
            assert done[0] == DVE_CTX
            step(v.tensor_copy(mkf[:, :], mrow8))
            after(done[0])
            m_any = step(v.tensor_reduce(mkany[:, :], mkf[:, :].rearrange("p (b n) -> p b n", b=B), AX.X, ALU.max))
            after(m_any)
            n = step(v.tensor_scalar(mkf[:, :], mkf[:, :], -MASKED, MASKED, ALU.mult, ALU.add))
            after(n)
            n = step(v.tensor_tensor(mkb[:, 0, :].rearrange("p (b n) -> p b n", b=B),
                                     mkf[0:8, :].rearrange("p (b n) -> p b n", b=B),
                                     mkany[0:8, :].unsqueeze(2).broadcast_to([8, B, NC]), ALU.mult))
            after(n)
            n = step(v.tensor_copy(mkf[:, :], mrow32[:, :]))
            after(n)
            n = step(v.tensor_scalar(mkf[:, :], mkf[:, :], 0.0, None, ALU.is_equal))
            after(n)
            n = step(v.tensor_reduce(poison[:, :], mkf[:, :].rearrange("p (b n) -> p b n", b=B), AX.X, ALU.min))
            v.tensor_scalar(mkb[:, 1, :], mkf[0:8, :], MASKED, None, ALU.mult).then_inc(S["prep_mask_rows"], 2)
            after(n)
            n = step(v.tensor_scalar(poison[:, :], poison[:, :], -1.0, 1.0, ALU.mult, ALU.add))
            after(n)
            n = step(v.reciprocal(poison[:, :], poison[:, :]))
            after(n)
            step(v.tensor_scalar(poison[:, :], poison[:, :], 0.0, None, ALU.mult))
            dve.wait_ge(S["prep_pe"], 1)
            o, _ = CT["adab"]
            nch = len(CHUNKS)
            n = step(v.tensor_tensor(mod[:, :, :], PS[:, M0, 0:B * nch].rearrange("p (n b) -> p n b", b=B),
                                     COL[:, o:o + nch].unsqueeze(2).broadcast_to([P, nch, B]), ALU.add))
            for i, l in enumerate((0, 2, 3)):
                for c in range(2):
                    q = PS[:, M0, B * nch + 2 * i + c:B * nch + 2 * i + c + 1]
                    n = step(v.tensor_scalar(cb[:, 2 * i + c:2 * i + c + 1], q,
                                             col(f"{'bco' if c else 'bo'}{l}"), None, ALU.add))
            after(n)
            where = {ch: i for i, ch in enumerate(CHUNKS)}

            def m(l, kind, br):
                return mod[:, where[(l, kind, br)], :]

            VV = VEC[:, :].rearrange("p (l b r f) -> p l b r f", l=NL, b=B, r=3)
            for l in range(NL):
                for br in range(3):
                    scale, shift, gate, gbias = (VV[:, l, :, br, f] for f in range(4))
                    has = (l, "sc", br) in where
                    if has:
                        step(v.tensor_scalar(scale, m(l, "sc", br), 1.0, col("w1", br) if l == 1 else 1.0,
                                             ALU.add, ALU.mult))
                        step(v.tensor_copy(shift, m(l, "sh", br)))
                        step(v.tensor_copy(gate, m(l, "g", br)))
                    else:
                        step(v.memset(gate, 1.0))
                        if l == 2:
                            step(v.tensor_copy(scale, col("w2", br).broadcast_to([P, B])))
                            step(v.tensor_copy(shift, col("lb2", br).broadcast_to([P, B])))
                        else:
                            step(v.memset(scale, 1.0))
                            step(v.memset(shift, 0.0))
                    bias = (col(f"b2_{l}") if br == 2 else
                            None if l == 1 else cb[:, 2 * (0, None, 1, 2)[l] + br:2 * (0, None, 1, 2)[l] + br + 1])
                    if bias is None:
                        step(v.memset(gbias, 0.0))
                    elif l == 2:
                        n = step(v.tensor_scalar(gbias, m(2, "t", br), bias, None, ALU.add))
                        if br == 1:
                            after(n)
                            step(v.tensor_tensor(gbias, gbias, poison[:, :], ALU.add))
                    elif has:
                        step(v.tensor_scalar(gbias, m(l, "g", br), bias, None, ALU.mult))
                    else:
                        step(v.tensor_copy(gbias, bias.broadcast_to([P, B])))
            kstep = S["prep_kparts"]
            for l in range(NL):
                dve.wait_ge(S["prep_act"], 2 + l)
                if l:
                    dve.wait_ge(S["prep_stacked"], 16 * 12 * l)
                if l == 1:
                    k3 = kc32[:, :].rearrange("p (b n) -> p b n", b=B)
                    after(step(v.tensor_tensor(k3, k3, mkany[:, :].unsqueeze(2).broadcast_to([P, B, NC]), ALU.mult)))
                v.tensor_copy(kcp[:, 0, :], kc32[:, :]).then_inc(kstep, 1)
                dve.wait_ge(kstep, 4 * l + 1)
                v.tensor_tensor(kc32[:, :], kc32[:, :], kcp[:, 0, :], ALU.subtract).then_inc(kstep, 1)
                dve.wait_ge(kstep, 4 * l + 2)
                v.tensor_copy(kcp[:, 1, :], kc32[:, :]).then_inc(kstep, 1)
                dve.wait_ge(kstep, 4 * l + 3)
                v.tensor_tensor(kcp[:, 2, :], kc32[:, :], kcp[:, 1, :], ALU.subtract).then_inc(kstep, 1)
                dve.wait_ge(S["prep_pe"], PE_V[l])
                n = step(v.tensor_copy(VC[:, l, :, :], PS[0:NC, 4 + l % 2, :].rearrange("p (b n) -> p b n", b=B)))
                if l < 2:
                    assert n == DVE_VC[l], (l, n)
            assert n == PREP_VC, n
            n = step(v.tensor_copy(MB[:, :, :], ms8))
            after(n)
            n = step(v.tensor_reduce(rany[:, :], MB[:, :, :], AX.X, ALU.max))
            after(n)
            n = step(v.tensor_scalar(MB[:, :, :], MB[:, :, :], -MASKED, MASKED, ALU.mult, ALU.add))
            after(n)
            for t in range(T):
                step(v.tensor_scalar(MB[:, t, :], MB[:, t, :], rany[:, t:t + 1], None, ALU.mult))
                n = step(v.tensor_scalar(diag[:, t, :], ident[:, :], rany[:, t:t + 1], None, ALU.mult))
            assert n == DVE_MASK, n
            dve.wait_ge(S["prep_pe"], PE_V[3] + 2)
            for k2, src in enumerate((M0B, M1B)):
                step(v.tensor_copy(MBT[:, 2 * k2:2 * k2 + 2, :], src.rearrange("p (a n) -> p a n", a=2)))
            for f in range(2):
                n = step(v.scalar_tensor_tensor(ROPEQ[:, f, :], PS[:, 4, :], QSCALE, ROPE[:, f, :], ALU.mult, ALU.mult))
            after(n)
            dve.wait_ge(S["x_loaded"], 16 * B)
            dve.wait_ge(S["base_consts"], 10)

            def normed(l, b, chain, k, st_, mv_, ve_):
                X = xs if l else xr
                for t in range(T):
                    v.bn_stats(st_[:, t, :], X[:, T * b + t, :]).then_inc(S[chain + "_st"], 1)
                dve.wait_ge(S[chain + "_st"], 4 * k + 4)
                for t in range(T):
                    v.bn_aggr(mv_[:, t, :], st_[:, t, :]).then_inc(S[chain + "_ag"], 1)
                dve.wait_ge(S[chain + "_ag"], 4 * k + 4)
                v.tensor_scalar(ve_[:, :], mv_[:, :, 1], EPS[l], None, ALU.add).then_inc(S[chain + "_ve"], 1)

            def normed_out(b, chain, k, XN_, mv_, rstd_, X=xs):
                dve.wait_ge(S[chain + "_rs"], k + 1)
                for t in range(T):
                    v.tensor_scalar(XN_[:, t, :], X[:, T * b + t, :], mv_[:, t, 0:1], rstd_[:, t:t + 1],
                                    ALU.subtract, ALU.mult).then_inc(S[chain + "_xn"], 1)

            def added(b, chain, bank, k, X=xs):
                xb = X[:, T * b:T * b + T, :]
                dve.wait_ge(S[chain + "_yb"], k + 1)
                v.tensor_tensor(xb, PS[:, bank, :].rearrange("p (t c) -> p t c", t=T), xb, ALU.add).then_inc(
                    S[chain + "_x"], 1)
                dve.wait_ge(S[chain + "_x"], k + 1)

            def maximum_of(n, a):
                i, t, j = unit_a(a)
                dve.wait_ge(S["a_ready"], 64 * n + a + 1)
                v.tensor_reduce(mneg[:, t, 2 * j + i:2 * j + i + 1], PS[:, BANK_A[a % 2], :], AX.X, ALU.max,
                                negate=True).then_inc(S["a_used"], 1)

            def over_sums(chain, bank, half, k, ON_, rec_):
                rows = PS[:, bank, :].rearrange("p (t h e) -> p t h e", t=T, e=16)
                rr = rec_[:, 32 * half:32 * half + 32].rearrange("p (t h) -> p t h", t=T).unsqueeze(3)
                dve.wait_ge(S[chain + "_T"], k + 1)
                v.reciprocal(rr, rows[:, :, :, 8:9]).then_inc(S[chain + "_rec"], 1)
                dve.wait_ge(S[chain + "_rec"], k + 1)
                v.tensor_tensor(ON_[:, :, 64 * half:64 * half + 64].rearrange("p t (h d) -> p t h d", d=HD),
                                rows[:, :, :, 0:8], rr.broadcast_to([P, T, 8, HD]), ALU.mult).then_inc(
                    S[chain + "_on"], 1)

            def three_parts(src, dst, part, n):
                v.tensor_copy(dst[:, 0, :], src).then_inc(part, 1)
                dve.wait_ge(part, 4 * n + 1)
                v.tensor_tensor(src, src, dst[:, 0, :], ALU.subtract).then_inc(part, 1)
                dve.wait_ge(part, 4 * n + 2)
                v.tensor_copy(dst[:, 1, :], src).then_inc(part, 1)
                dve.wait_ge(part, 4 * n + 3)
                v.tensor_tensor(dst[:, 2, :], src, dst[:, 1, :], ALU.subtract).then_inc(part, 1)

            def maxima_parts(mneg_, m3_, step_, n):
                src = mneg_[:, :, :].rearrange("p t (j i) -> p t i j", i=2)
                v.tensor_copy(m3_[:, :, :, 0, :], src).then_inc(step_, 1)
                dve.wait_ge(step_, 4 * n + 1)
                v.tensor_tensor(src, src, m3_[:, :, :, 0, :], ALU.subtract).then_inc(step_, 1)
                dve.wait_ge(step_, 4 * n + 2)
                v.tensor_copy(m3_[:, :, :, 1, :], src).then_inc(step_, 1)
                dve.wait_ge(step_, 4 * n + 3)
                v.tensor_tensor(m3_[:, :, :, 2, :], src, m3_[:, :, :, 1, :], ALU.subtract).then_inc(step_, 1)

            for s in SLOTS0:
                c, e, n = s - 1, s - 2, s + 1
                for p in range(POINTS0):
                    if seq(e):
                        if p == 2:
                            for half in range(2):
                                over_sums("z2", BANK_T[half], half, 2 * e + half, XN1, rec2)
                        if p == 6:
                            added(e, "z2", BANK_T[0], e, xr)
                    if seq(n):
                        if p == Z_FRONT[0]:
                            normed(0, n, "c1", order1("front", n), st2, mv2, ve2)
                        if p == Z_FRONT[2]:
                            normed_out(n, "c1", order1("front", n), XN2, mv2, rstd2, xr)
                        if p == Z_QPART:
                            dve.wait_ge(S["z_q"], n + 1)
                            if n:
                                dve.wait_ge(S["z_q_in"], 96 * n)
                            three_parts(qk[:, 0, :], qkp[:, 0, :, :], S["z_qpart"], n)
                    if seq(s):
                        if p - Z_LAG in Z_A:
                            t = Z_A.index(p - Z_LAG)
                            dve.wait_ge(S["z_a_ready"], 4 * s + t + 1)
                            v.tensor_reduce(mneg[:, t, :].rearrange("p (j i) -> p i j", i=2),
                                            PS[:, BANK_Z[0]:BANK_Z[1] + 1, :].rearrange("p i (j n) -> p i j n", n=WIN),
                                            AX.X, ALU.max, negate=True).then_inc(S["z_a_used"], 1)
                        if p == Z_MAX[0]:
                            dve.wait_ge(S["z_a_used"], 4 * s + 4)
                            maxima_parts(mneg, m3, S["z_m"], s)
                        if p - Z_LAG in Z_OUT[:2]:
                            half = Z_OUT.index(p - Z_LAG)
                            over_sums("c1", BANK_Z[1 - half], half, 2 * s + half, XN1, rec)
                        if p == Z_OUT[4]:
                            added(s, "c1", BANK_Z[1], s, xr)
                            normed(0, s, "c1", order1("cross", s), st, mv, ve)
                        if p == Z_NORM[1]:
                            normed_out(s, "c1", order1("cross", s), XN1, mv, rstd, xr)
                        if p == Z_NORM[4]:
                            dve.wait_ge(S["z_xq"], s + 1)
                            three_parts(QX32, QXP0, S["z_xpart"], s)
                    if seq(c) and p < 32:
                        u, phase = divmod(p, 4)
                        k, sl = 8 * c + u, u % 2
                        step_, o = S["t_step"], 31 * k
                        if phase == 0:
                            dve.wait_ge(S["t_sx"], k + 1)
                            for h in range(8):
                                v.max(v8[:, 0, h, :], SX[:, sl, h, :]).then_inc(step_, 1)
                        if phase == 1:
                            dve.wait_ge(step_, o + 8)
                            if k:
                                dve.wait_ge(S["t_w2"], k)
                            if k >= 2:
                                dve.wait_ge(S["t_e"], k - 1)
                            v.tensor_scalar(nm8[:, sl, :], v8[:, 0, :, 0], -1.0, None, ALU.mult).then_inc(
                                S["t_negm"], 1)
                            for h in range(8):
                                v.match_replace(W1[:, h, :], v8[:, 0, h, :], SX[:, sl, h, :], TAKEN).then_inc(step_, 1)
                        if phase == 2:
                            for h in range(8):
                                dve.wait_ge(step_, o + 9 + h)
                                v.max(v8[:, 1, h, :], W1[:, h, :]).then_inc(step_, 1)
                        if phase == 3:
                            if k >= 2:
                                dve.wait_ge(S["t_pT"], k - 1)
                            for h in range(8):
                                dve.wait_ge(step_, o + 17 + h)
                                v.match_replace(W2[:, sl, h, :], v8[:, 1, h, :], W1[:, h, :], TAKEN).then_inc(
                                    S["t_w2"] if h == 7 else step_, 1)
                    for e, p0 in forward_at(s):
                        if p == p0:
                            normed(0, e, "zf", e, st2, mv2, ve2)
                        if p == p0 + 1:
                            normed_out(e, "zf", e, XN2, mv2, rstd2, xr)
                        if p in (p0 + 4, p0 + 6):
                            for m in (p - p0 - 4, p - p0 - 3):
                                dve.wait_ge(S["zf_up_ps"], 4 * e + m + 1)
                                v.scalar_tensor_tensor(PT[:, m, 0:L], PS[:, BANK_Z[m % 2], :], col("b1_0", 4 + m),
                                                       PT[:, m, 0:L], ALU.add, ALU.mult).then_inc(S["zf_hid"], 1)
                        if p == p0 + 8:
                            added(e, "zf", BANK_Z[0], e, xr)

            dve.wait_ge(S["unrolled"], 16 * (1 + 2 * B))
            for s in SLOTS:
                n1, n2, n3 = s - 1, s - 2, s + 2
                (l1, b1), (l2, b2), (l3, b3) = item(n1), item(n2), item(n3)
                for p in range(POINTS):
                    if item(s + 1)[0]:
                        n = s + 1
                        for a in range(maxima_at(p), maxima_at(p + 1))[:1]:
                            maximum_of(n, a)
                        if p == A_TO:
                            dve.wait_ge(S["a_used"], 64 * n + 64)
                            maxima_parts(mneg, m3, S["a_m"], n)
                    if l1:
                        if p in (5, 8):
                            over_sums("c1", BANK_1, p // 8, 2 * (n1 + B) + p // 8, XN1, rec)
                        if p == 15:
                            added(b1, "c1", BANK_1, n1 + B)
                            normed(l1, b1, "c1", n1 + 2 * B, st, mv, ve)
                        if p == 18:
                            normed_out(b1, "c1", n1 + 2 * B, XN1, mv, rstd)
                        if p == 24:
                            dve.wait_ge(S["x_q"], n1 + 1)
                            if n1:
                                dve.wait_ge(S["x_in"], 96 * n1)
                            three_parts(QX32, qxp, S["x_part"], n1)
                    if l1:
                        if XA_FROM <= p < XA_FROM + 16:
                            u = p - XA_FROM
                            i, t, half = u // 8, u // 2 % 4, u % 2
                            dve.wait_ge(S["xa_ready"], 16 * n1 + u + 1)
                            v.tensor_reduce(mnegx[:, t, 8 * half:8 * half + 8].rearrange("p (j i) -> p i j", i=2)[:, i],
                                            PS[:, BANK_1, 0:4 * NC].rearrange("p (j n) -> p j n", n=NC), AX.X,
                                            ALU.max, negate=True).then_inc(S["xa_used"], 1)
                        if p == XA_FROM + 16:
                            dve.wait_ge(S["xa_used"], 16 * n1 + 16)
                            maxima_parts(mnegx, m3x, S["xa_m"], n1)
                    if l2:
                        if p == 22:
                            for half in range(2):
                                over_sums("c2", BANK_2[half], half, 2 * n2 + half, XN2, rec2)
                        if p in (29, 46):
                            added(b2, "c2", BANK_2[0], 2 * n2 + p // 46)
                        if p == 29:
                            normed(l2, b2, "c2", order2("ff", n2), st2, mv2, ve2)
                        if p == 32:
                            normed_out(b2, "c2", order2("ff", n2), XN2, mv2, rstd2)
                    if l3:
                        k = order2("front", n3)
                        if p == 47:
                            normed(l3, b3, "c2", k, st2, mv2, ve2)
                        if p == 50:
                            normed_out(b3, "c2", k, XN2, mv2, rstd2)
                        if l3 == 1 and p in (55, 58):
                            which = (p - 55) // 3
                            tab = (ROPEQ, ROPE)[which]
                            dve.wait_ge(S["f_qkps"], 2 * n3 + which + 1)
                            if which:
                                dve.wait_ge(S["f_q"], n3 + 1)
                            elif n3:
                                dve.wait_ge(S["k_in"], 96 * n3)
                            v.tensor_tensor(RA, PS[:, BANK_2[0], :], tab[:, 0, :], ALU.mult).then_inc(S["f_rope"], 1)
                            v.tensor_tensor(RB, PS[:, BANK_2[1], :], tab[:, 1, :], ALU.mult).then_inc(S["f_rope"], 1)
                            dve.wait_ge(S["f_rope"], 4 * n3 + 2 * which + 2)
                            v.tensor_tensor(qk[:, which, :], RA, RB, ALU.add).then_inc(S[("f_q", "f_k")[which]], 1)
                        if p == 60:
                            dve.wait_ge(S["f_q"], n3 + 1)
                            if n3:
                                dve.wait_ge(S["q_in"], 112 * n3)
                            three_parts(qk[:, 0, :], qkp[:, 0, :, :], S["f_qpart"], n3)
                    if item(s + 1)[0]:
                        for a in range(maxima_at(p), maxima_at(p + 1))[1:]:
                            maximum_of(s + 1, a)


PE_CTXT = 2
PE_K = [3, 5, 7, 9]
PE_V = [4, 6, 8, 10]
DVE_CTX = 7
DVE_VC = [74, 76]
PREP_VC = 78
DVE_MASK = 89
BQ = {0: 0, 2: 2, 3: 4}
Z_TURN = 7
Z_LAG = 1
Z_A = (0, 2, 4, 6)
Z_FRONT = (1, 2, 3, 10, 11)
Z_MAX = (8, 9)
Z_KPART = 12
Z_QPART = 12
Z_B = (12, 14, 16, 18)
Z_PV = (19, 21, 23, 25)
Z_V = 27
Z_OUT = (27, 28, 30, 31, 32)
Z_NORM = (33, 34, 35, 36, 37)
FF_AT = {4: ((0, 0), (1, 8), (2, 16)), 5: ((3, 7),)}
A_FROM = 9
A_TO = 57
M_TURN = 58
XA_FROM = 37
XM_TURN = 55
U_HALF = 35


def qk_order():
    return np.array([8 * (2 * j + i) + d for i in range(2) for d in range(HD) for j in range(J)])


def out_order():
    return np.array([8 * (8 * s + hh) + d for hh in range(8) for s in range(2) for d in range(HD)])


def pack(inputs):
    g = {k: np.asarray(v) for k, v in inputs.items()}
    qo, oo = qk_order(), out_order()
    rot = np.array([c // HD * HD + (c % HD + HD // 2) % HD for c in range(C)])
    W, V = {}, {}
    L0, L1, L2, L3 = ("L%d_xcond_" % l for l in range(4))
    for l, (pre, wqkv) in enumerate(((L0, "w_qkv"), (L1, "qkv_W"), (None, None), (L3, "W_qkv"))):
        if pre:
            q = g[pre + wqkv]
            W[f"q{l}"], W[f"k{l}"], W[f"v{l}"] = q[:, :C][:, qo], q[:, C:2 * C][:, qo], q[:, 2 * C:]
            if l == 1:
                W["qrot1"], W["krot1"] = q[:, :C][:, rot][:, qo], q[:, C:2 * C][:, rot][:, qo]
    W["q2"], W["k2"], W["v2"] = g[L2 + "sa_wq"][:, qo], g[L2 + "sa_wk"][:, qo], g[L2 + "sa_wv"]
    for l, n in enumerate((L0 + "w_so", L1 + "attn_out_W", L2 + "sa_wo", L3 + "W_proj")):
        W[f"o{l}"] = g[n][oo]
    for l, n in enumerate((L0 + "w_co", L1 + "co_W", L2 + "ca_wo", L3 + "W_cproj")):
        W[f"co{l}"] = g[n][oo]
    for l, n in enumerate((L0 + "w_q", L1 + "cq_W", L2 + "ca_wq", L3 + "W_qc")):
        W[f"cq{l}"] = g[n][:, qo]
    W["ck0"], W["cv0"] = g[L0 + "w_kv"][:, :C][:, qo], g[L0 + "w_kv"][:, C:]
    W["ck1"], W["cv1"] = g[L1 + "ck_W"][:, qo], g[L1 + "cv_W"]
    W["ck2"], W["cv2"] = g[L2 + "ca_wk"][:, qo], g[L2 + "ca_wv"]
    W["ck3"], W["cv3"] = g[L3 + "W_kvc"][:, :C][:, qo], g[L3 + "W_kvc"][:, C:]
    ff = ((L0 + "w_m1", L0 + "w_m2"), (L1 + "mlp_W1", L1 + "mlp_W2"), (L2 + "w1", L2 + "w2"),
          (L3 + "W_mlp1", L3 + "W_mlp2"))
    for l, (a, b) in enumerate(ff):
        W[f"f1_{l}"] = g[a]
        W[f"f2_{l}"] = g[b].reshape(4, P, C).transpose(1, 0, 2).reshape(P, 4 * C)
    ada = {0: (L0 + "w_ada", L0 + "b_ada"), 1: (L1 + "adaLN_W", L1 + "adaLN_b"), 2: (L2 + "tp_w", L2 + "tp_b"),
           3: (L3 + "W_mod", L3 + "b_mod")}
    place = {"sh": 0, "sc": 1, "g": 2}
    aw, ab = [], []
    for l, kind, br in CHUNKS:
        n = br if l == 2 else 3 * (br // 2 if l == 3 else br) + place[kind]
        aw.append(g[ada[l][0]][:, n * C:(n + 1) * C])
        ab.append(g[ada[l][1]][n * C:(n + 1) * C])
    V["cond"] = g["cond_1024"].T
    V["adab"] = np.stack(ab, 1)
    for l, n in ((0, L0 + "b_qkv"), (3, L3 + "b_qkv")):
        V[f"bq{l}"], V[f"bk{l}"], V[f"bv{l}"] = g[n][:C][qo], g[n][C:2 * C][qo], g[n][2 * C:][oo]
    V["bq2"], V["bk2"], V["bv2"] = g[L2 + "sa_bq"][qo], g[L2 + "sa_bk"][qo], g[L2 + "sa_bv"][oo]
    V["bo0"], V["bo2"], V["bo3"] = g[L0 + "b_so"], g[L2 + "sa_bo"], g[L3 + "b_proj"]
    V["bcq0"], V["bcq2"], V["bcq3"] = g[L0 + "b_q"][qo], g[L2 + "ca_bq"][qo], g[L3 + "b_qc"][qo]
    V["bck0"], V["bcv0"] = g[L0 + "b_kv"][:C][qo], g[L0 + "b_kv"][C:][oo]
    V["bck2"], V["bcv2"] = g[L2 + "ca_bk"][qo], g[L2 + "ca_bv"][oo]
    V["bck3"], V["bcv3"] = g[L3 + "b_kvc"][:C][qo], g[L3 + "b_kvc"][C:][oo]
    V["bco0"], V["bco2"], V["bco3"] = g[L0 + "b_co"], g[L2 + "ca_bo"], g[L3 + "b_cproj"]
    for l, (a, b) in enumerate(((L0 + "b_m1", L0 + "b_m2"), (L1 + "mlp_b1", L1 + "mlp_b2"), (L2 + "b1", L2 + "b2"),
                                (L3 + "b_mlp1", L3 + "b_mlp2"))):
        V[f"b1_{l}"], V[f"b2_{l}"] = g[a].reshape(-1, P).T, g[b]
    V["w1"] = np.stack([g[L1 + "norm1_w"], g[L1 + "normc_w"], g[L1 + "norm2_w"]], 1)
    V["w2"] = np.stack([g[L2 + "ln1_g"], g[L2 + "ln3_g"], g[L2 + "ln2_g"]], 1)
    V["lb2"] = np.stack([g[L2 + "ln1_b"], g[L2 + "ln3_b"], g[L2 + "ln2_b"]], 1)
    out = {}
    for name, table, parts in (("wpack", weight_table(), W), ("cols", column_table(), V)):
        at, width = table
        out[name] = np.zeros((P, width), np.float32)
        for n, (o, k) in at.items():
            out[name][:, o:o + k] = parts[n].reshape(P, k)
    out["ada_w"] = np.concatenate(aw, 1)
    out["x"] = np.roll(g["x"], -SHIFT, axis=1)
    out["ctx_t"] = g["ctx_1024"].transpose(2, 0, 1).reshape(C, B * NC)
    out["ctx_tok"] = g["ctx_1024"].transpose(1, 0, 2)
    out["mask_self"] = g["mask_SxS_bk0"].view(np.int32)
    out["mask1"] = g["mask_BxS2_bf1"].reshape(B * NC).view(np.int32)
    out["mask2"] = g["mask_BxS2_ik0"].reshape(B * NC)
    out["ident_in"] = np.eye(P, dtype=np.float32)
    half = L // 2
    inv = 1.0 / 10000.0 ** (np.arange(0, HD, 2, dtype=np.float32) / HD)
    freqs = np.outer(np.arange(half, dtype=np.float32), inv)
    emb = np.concatenate([freqs, freqs], axis=-1)
    cos, sin = np.cos(emb).astype(np.float32), np.sin(emb).astype(np.float32)
    d = qo % HD
    sign = np.where(d < HD // 2, -1.0, 1.0).astype(np.float32)[:, None]
    out["rope"] = np.stack([np.tile(cos.T[d], (1, 2)), sign * np.tile(sin.T[d], (1, 2))], 1)
    rows = np.full((4, J * L), 0x3F80, np.uint16)
    rows[0] = 0
    out["const_rows"] = rows
    return {k: np.ascontiguousarray(v) for k, v in out.items()}


_INS = ["x", "wpack", "ada_w", "cols", "ctx_t", "ctx_tok", "mask_self", "mask1", "mask2", "ident_in", "rope", "const_rows"]


def kernel(**inputs):
    import concourse.bacc as bacc
    from concourse.bass_utils import run_bass_kernel_spmd

    nc = bacc.Bacc("TRN2", target_bir_lowering=False, num_devices=1)
    laid = pack(inputs)
    arrays, args = {}, []
    for name in _INS:
        a = laid[name]
        arrays[f"in_{name}"] = a
        args.append(nc.dram_tensor(f"in_{name}", a.shape, mybir.dt.from_np(a.dtype), kind="ExternalInput").ap())
    args.append(nc.dram_tensor("out_x", (B, L, C), F32, kind="ExternalOutput").ap())
    build(nc, *args)
    r = run_bass_kernel_spmd(nc, [arrays], core_ids=[0])
    return r.results[0]["out_x"]
```
